# Optimizing a Trainium2 kernel written in Bass

```python
import numpy as np
import jax
import jax.numpy as jnp

def _softmax(x, axis=-1):
    return jax.nn.softmax(x, axis=axis)

def _gelu(x):
    return jax.nn.gelu(x, approximate=True)

def _silu(x):
    return jax.nn.silu(x)

def _sigmoid(x):
    return jax.nn.sigmoid(x)

def _layernorm(x, axis=-1, eps=1e-05):
    m = jnp.mean(x, axis=axis, keepdims=True)
    v = jnp.var(x, axis=axis, keepdims=True)
    return (x - m) / jnp.sqrt(v + eps)

def _scatter_add(tgt, idx, src, axis=0):
    return tgt.at[idx].add(src)

def _segment_sum(src, seg, n):
    return jax.ops.segment_sum(src, seg, n)
kernel_name = 'mk_gps_d1_gnn_r16_6e3821'

def setup_inputs(seed: int=0):
    np.random.seed(seed)
    _w = jnp.asarray

    def _rec_inputs():
        import jax
        import jax.numpy as jnp
        _gk = jax.random.key(seed)
        x = -0.000202 + 1 * jax.random.normal(jax.random.fold_in(_gk, 1), (6250, 256), jnp.float32)
        _s = jax.random.randint(jax.random.fold_in(_gk, 2), (50000,), 0, 6250, jnp.int32)
        _d = jax.random.randint(jax.random.fold_in(_gk, 3), (50000,), 0, 6250, jnp.int32)
        _loop = jnp.arange(6250, dtype=jnp.int32)
        src = jnp.concatenate([_s, _d, _loop])
        dst = jnp.concatenate([_d, _s, _loop])
        _o = jnp.argsort(dst, stable=True)
        src = src[_o]
        dst = dst[_o]
        edge_attr_64 = 0.000283511 + 1.00007 * jax.random.normal(jax.random.fold_in(_gk, 11), (106250, 64), jnp.float32)
        return (x, src, dst, edge_attr_64)
    x, src, dst, edge_attr_64 = _rec_inputs()

    def _L0_gnn_setup():
        import jax, jax.numpy as jnp
        import numpy as np
        N_NODES = 25000
        N_EDGES = 18750
        D_NODE = 256
        D_EDGE = 64
        LN_EPS = 0.001
        key = jax.random.key(seed)
        k1, k2, k3, k4 = jax.random.split(key, 4)
        node_features = jax.random.normal(k1, (N_NODES, D_NODE), dtype=jnp.float32)
        edge_index = jax.random.randint(k2, (2, N_EDGES), 0, N_NODES, dtype=jnp.int32)
        edge_features = jax.random.normal(k3, (N_EDGES, D_EDGE), dtype=jnp.float32)
        W = jax.random.normal(k4, (D_NODE + D_EDGE, D_NODE), dtype=jnp.float32) * (1.0 / np.sqrt(D_NODE + D_EDGE))
        b = jnp.zeros((D_NODE,), dtype=jnp.float32)
        gamma = jnp.ones((D_NODE,), dtype=jnp.float32)
        beta = jnp.zeros((D_NODE,), dtype=jnp.float32)
        return {'node_features': node_features, 'edge_index': edge_index, 'edge_features': edge_features, 'W': W, 'b': b, 'gamma': gamma, 'beta': beta}
    _L0_gnn_all = _L0_gnn_setup()
    _L0_gnn_in = {k: v for k, v in _L0_gnn_all.items() if k in ('W', 'b', 'gamma', 'beta')}
    del _L0_gnn_all

    def _L0_mix_setup():
        import jax, jax.numpy as jnp
        import numpy as np
        HEADS = 8
        DIM_HEAD = 64
        EPS = 1e-05

        def _inst_norm_lastdim(t):
            mu = jnp.mean(t, axis=-1, keepdims=True)
            var = jnp.mean(jnp.square(t - mu), axis=-1, keepdims=True)
            return (t - mu) * jax.lax.rsqrt(var + EPS)
        key = jax.random.key(seed)
        k1, k2, k3, k4 = jax.random.split(key, 4)
        b, n, dim = (4, 512, 256)
        inner = HEADS * DIM_HEAD
        x = jax.random.normal(k1, (b, n, dim), dtype=jnp.float32)
        Wqkv = jax.random.normal(k2, (3 * inner, dim), dtype=jnp.float32) * (1.0 / np.sqrt(dim))
        Wout = jax.random.normal(k3, (dim, inner), dtype=jnp.float32) * (1.0 / np.sqrt(inner))
        bout = jax.random.normal(k4, (dim,), dtype=jnp.float32) * 0.01
        return {'x': x, 'Wqkv': Wqkv, 'Wout': Wout, 'bout': bout}
    _L0_mix_all = _L0_mix_setup()
    _L0_mix_in = {k: v for k, v in _L0_mix_all.items() if k in ('Wqkv', 'Wout', 'bout')}
    del _L0_mix_all

    def _L0_ffn_setup():
        import jax, jax.numpy as jnp
        import numpy as np
        B, K, D = (512, 16, 256)
        E = 32
        H = int(D * 0.25)
        key = jax.random.key(seed)
        ks = jax.random.split(key, 7)
        d_rs = D ** (-0.5)
        h_rs = H ** (-0.5)
        x = jax.random.normal(ks[0], (B, K, D), dtype=jnp.float32)
        router_w = jax.random.uniform(ks[1], (E, D), jnp.float32, -d_rs, d_rs)
        router_b = jax.random.uniform(ks[2], (E,), jnp.float32, -d_rs, d_rs)
        W1 = jax.random.uniform(ks[3], (E, D, H), jnp.float32, -h_rs, h_rs)
        b1 = jax.random.uniform(ks[4], (E, H), jnp.float32, -h_rs, h_rs)
        W2 = jax.random.uniform(ks[5], (E, H, D), jnp.float32, -d_rs, d_rs)
        b2 = jax.random.uniform(ks[6], (E, D), jnp.float32, -d_rs, d_rs)
        return {'x': x, 'router_w': router_w, 'router_b': router_b, 'W1': W1, 'b1': b1, 'W2': W2, 'b2': b2}
    _L0_ffn_all = _L0_ffn_setup()
    _L0_ffn_in = {k: v for k, v in _L0_ffn_all.items() if k in ('router_w', 'router_b', 'W1', 'b1', 'W2', 'b2')}
    del _L0_ffn_all
    return {'x': x, 'src': src, 'dst': dst, 'edge_attr_64': edge_attr_64, 'L0_gnn_W': _L0_gnn_in['W'], 'L0_gnn_b': _L0_gnn_in['b'], 'L0_gnn_gamma': _L0_gnn_in['gamma'], 'L0_gnn_beta': _L0_gnn_in['beta'], 'L0_mix_Wqkv': _L0_mix_in['Wqkv'], 'L0_mix_Wout': _L0_mix_in['Wout'], 'L0_mix_bout': _L0_mix_in['bout'], 'L0_ffn_router_w': _L0_ffn_in['router_w'], 'L0_ffn_router_b': _L0_ffn_in['router_b'], 'L0_ffn_W1': _L0_ffn_in['W1'], 'L0_ffn_b1': _L0_ffn_in['b1'], 'L0_ffn_W2': _L0_ffn_in['W2'], 'L0_ffn_b2': _L0_ffn_in['b2']}

def reference(x, src, dst, edge_attr_64, L0_gnn_W, L0_gnn_b, L0_gnn_gamma, L0_gnn_beta, L0_mix_Wqkv, L0_mix_Wout, L0_mix_bout, L0_ffn_router_w, L0_ffn_router_b, L0_ffn_W1, L0_ffn_b1, L0_ffn_W2, L0_ffn_b2):
    import jax
    import jax.numpy as jnp

    def _L0_gnn_ref(node_features, edge_index, edge_features, W, b, gamma, beta):
        import jax, jax.numpy as jnp
        import numpy as np
        N_NODES = 25000
        N_EDGES = 18750
        D_NODE = 256
        D_EDGE = 64
        LN_EPS = 0.001
        source = edge_index[0]
        target = edge_index[1]
        msgs = jnp.concatenate([node_features[source], edge_features], axis=-1)
        msgs = jax.nn.silu(msgs @ W + b)
        out = jax.ops.segment_sum(msgs, target, num_segments=node_features.shape[0])
        mean = jnp.mean(out, axis=-1, keepdims=True)
        var = jnp.mean(jnp.square(out - mean), axis=-1, keepdims=True)
        out = (out - mean) * jax.lax.rsqrt(var + LN_EPS) * gamma + beta
        return out

    def _L0_mix_ref(x, Wqkv, Wout, bout):
        import jax, jax.numpy as jnp
        import numpy as np
        HEADS = 8
        DIM_HEAD = 64
        EPS = 1e-05

        def _inst_norm_lastdim(t):
            mu = jnp.mean(t, axis=-1, keepdims=True)
            var = jnp.mean(jnp.square(t - mu), axis=-1, keepdims=True)
            return (t - mu) * jax.lax.rsqrt(var + EPS)
        b, n, dim = x.shape
        qkv = jnp.einsum('bnc,fc->bnf', x, Wqkv)
        q, k, v = jnp.split(qkv, 3, axis=-1)

        def to_heads(t):
            return t.reshape(b, n, HEADS, DIM_HEAD).transpose(0, 2, 1, 3)
        q, k, v = (to_heads(q), to_heads(k), to_heads(v))
        k = _inst_norm_lastdim(k)
        v = _inst_norm_lastdim(v)
        dots = jnp.einsum('bhnd,bhne->bhde', k, v)
        out = jnp.einsum('bhnd,bhde->bhne', q, dots) / n
        out = out.transpose(0, 2, 1, 3).reshape(b, n, HEADS * DIM_HEAD)
        return jnp.einsum('bnf,cf->bnc', out, Wout) + bout

    def _L0_ffn_ref(x, router_w, router_b, W1, b1, W2, b2):
        import jax, jax.numpy as jnp
        import numpy as np
        B, K, D = (512, 16, 256)
        E = 32
        H = int(D * 0.25)
        xf = x.reshape(-1, D)
        logits = xf @ router_w.T + router_b
        idx = jnp.argmax(logits, axis=-1)
        w1t = jnp.take(W1, idx, axis=0)
        h = jnp.einsum('nd,ndh->nh', xf, w1t) + jnp.take(b1, idx, axis=0)
        h = jax.nn.relu(h)
        w2t = jnp.take(W2, idx, axis=0)
        out = jnp.einsum('nh,nhd->nd', h, w2t) + jnp.take(b2, idx, axis=0)
        out = jax.nn.relu(out)
        return out.reshape(x.shape)
    edge_index = jnp.stack([src, dst])
    xn = _layernorm(x, axis=-1)
    x = x + _L0_gnn_ref(xn, edge_index, edge_attr_64, L0_gnn_W, L0_gnn_b, L0_gnn_gamma, L0_gnn_beta) + _L0_mix_ref(xn[None], L0_mix_Wqkv, L0_mix_Wout, L0_mix_bout)[0]
    x = x + _L0_ffn_ref(_layernorm(x, axis=-1)[None], L0_ffn_router_w, L0_ffn_router_b, L0_ffn_W1, L0_ffn_b1, L0_ffn_W2, L0_ffn_b2)[0]
    return x

_drawn_inputs = setup_inputs


def setup_inputs(seed=0):
    import zlib

    import numpy as np

    out = dict(_drawn_inputs(seed))
    spreads = {'L0_gnn_b': (0.0, 0.1), 'L0_gnn_gamma': (1.0, 0.2), 'L0_gnn_beta': (0.0, 0.1)}
    factors = {'L0_mix_bout': 5.808, 'L0_ffn_b1': 8.0, 'L0_ffn_b2': 3.477}
    for name, (base, spread) in spreads.items():
        noise = np.random.default_rng([zlib.crc32(name.encode()), seed]).standard_normal(out[name].shape)
        drawn = base * np.exp(spread * noise) if base else spread * noise
        out[name] = jnp.asarray(drawn.astype(out[name].dtype))
    for name, factor in factors.items():
        out[name] = (out[name] * factor).astype(out[name].dtype)
    return out
```

```python
from contextlib import ExitStack

import concourse.bass as bass
from concourse import mybir

ALU = mybir.AluOpType
ACT = mybir.ActivationFunctionType
AX = mybir.AxisListType
F32 = mybir.dt.float32
I32 = mybir.dt.int32

P = 128
N_NODES = 6250
D = 256
KC = D // P
N_EDGES = 106250
D_EDGE = 64
BATCH = 7
NT = -(-N_NODES // P)
NB = NT // BATCH
assert NT == NB * BATCH
WINDOW = 32
GROUPS = P // WINDOW
QUADS = 3
TILES = GROUPS * QUADS
GROUP_EDGES = QUADS * P
SUPER_EDGES = GROUPS * GROUP_EDGES
NS = 2 * -(-N_EDGES // (2 * SUPER_EDGES))
NI = NS // 2
NKV = 2 * -(-NT // 2)
KV_ITERS = NKV // 2
HEADS = 8
DH = 64
INNER = HEADS * DH
PAIRS = INNER // P
EXPERTS = 32
HID = 64
MEAN, RSTD, NODE = D, D + 1, D + 2
ROW = D + 4
PACK = KC * HID + D + 1
SLOT_TILES = (NT * P + EXPERTS * (P - 1)) // P
PAD_DST = 1 << 20
NO_NODE = 1 << 20
LN_EPS = 1e-5
GNN_EPS = 1e-3
HEAD_EPS = LN_EPS


def program(nc, x, attr, src, dst, base_group, base_row, w_gnn, b_gnn, gamma, beta, wq, wk_t, wv_t,
            wout_t, bout, router_t, router_b, experts, out):
    with ExitStack() as ctx:
        def sb(name, shape, dt=F32):
            return ctx.enter_context(nc.sbuf_tensor(name, shape, dt))

        def sem(name):
            return ctx.enter_context(nc.semaphore(name))

        y_dram = nc.dram_tensor("y_dram", [NT * P, D], F32).ap()
        xt_dram = nc.dram_tensor("xt_dram", [NKV, P, D], F32).ap()
        sorted_in = nc.dram_tensor("sorted_in", [SLOT_TILES * P, ROW], F32).ap()
        x_tiles = x.rearrange("(t p) c -> p t c", p=P)
        xt_tiles = xt_dram.rearrange("t p c -> p t c")
        slot_tiles = sorted_in.rearrange("(t p) c -> p t c", p=P)
        y_tiles = y_dram.rearrange("(t p) c -> p t c", p=P)

        banks = ctx.enter_context(nc.psum_tensor("banks", [P, 8, 512], F32))

        acc = sb("acc", [P, NT + 1, D])
        ident = sb("ident", [P, P])
        iota_i = sb("iota_i", [P, D], I32)
        iota = sb("iota", [P, D])
        eps = sb("eps", [P, 2])
        row_i = sb("row_i", [P, 1], I32)
        row = sb("row", [P, 1])
        tri = sb("tri", [P, P])
        ones = sb("ones", [P, P])
        w_node = sb("w_node", [P, KC, D])
        w_edge = sb("w_edge", [P, D])
        b_rows = sb("b_rows", [P, D])
        gamma_rows = sb("gamma_rows", [P, D])
        beta_rows = sb("beta_rows", [P, D])
        bout_rows = sb("bout_rows", [P, D])
        rb_rows = sb("rb_rows", [P, EXPERTS])
        wkv = sb("wkv", [P, KC, 2 * INNER])
        wkv_mean = sb("wkv_mean", [P, KC * 2 * HEADS])
        wq_sb = sb("wq_sb", [P, PAIRS, D])
        wo_sb = sb("wo_sb", [P, PAIRS, D])
        router = sb("router", [P, KC, EXPERTS])
        dst_f = sb("dst_f", [P, NS, QUADS, GROUPS])
        base_f = sb("base_f", [P, NS, GROUPS])
        block_i = sb("block_i", [P, NS], I32)
        block_f = sb("block_f", [P, NS])
        row_node = sb("row_node", [P, NS])
        rel = sb("rel", [P, NS, TILES])
        place = sb("place", [P, NS])
        missed = sb("missed", [P, NS, TILES])
        work = sb("work", [P, NS, TILES])
        miss_sum = sb("miss_sum", [P, 2])
        miss_i = sb("miss_i", [P, 1], I32)

        dve_tick = sem("dve_tick")
        pe_tick = sem("pe_tick")
        pool_tick = sem("pool_tick")
        dots_copied = sem("dots_copied")
        consts_landed = sem("consts_landed")
        first_landed = sem("first_landed")
        edges_landed = sem("edges_landed")
        consts_made = sem("consts_made")

        with ExitStack() as ctx_a:
            def sb_a(name, shape, dt=F32):
                return ctx_a.enter_context(nc.sbuf_tensor(name, shape, dt))

            x_all = sb_a("x_all", [P, NT, D])
            dst_i = sb_a("dst_i", [P, NS * TILES], I32)
            base_i = sb_a("base_i", [P, NS * GROUPS], I32)
            base_row_i = sb_a("base_row_i", [P, NS], I32)
            stats = sb_a("stats", [P, BATCH, 6])
            moments = sb_a("moments", [P, BATCH, 2])
            rstd = sb_a("rstd", [P, BATCH])
            xn = sb_a("xn", [P, BATCH, D])
            xt = sb_a("xt", [P, BATCH, D])
            y = sb_a("y", [P, BATCH, D])
            zeros = sb_a("zeros", [P, D])
            empty_rows = sb_a("empty_rows", [P, 2, ROW])
            x_landed = sem("x_landed")
            a_steps = sem("a_steps")
            xn_made = sem("xn_made")
            rstd_made = sem("rstd_made")
            rooted = sem("rooted")
            turned = sem("turned")
            xt_made = sem("xt_made")
            y_summed = sem("y_summed")
            y_made = sem("y_made")
            zeroed = sem("zeroed")
            acc_cleared = sem("acc_cleared")
            zeros_stored = sem("zeros_stored")
            pool_consts = sem("pool_consts")
            xt_stored = [sem(f"xt_stored{j}") for j in range(BATCH)]
            y_stored = [sem(f"y_stored{j}") for j in range(BATCH)]
            n_consts = 11

            with nc.Block() as block:
                @block.sync
                def _(sp):
                    def load_x(i):
                        sp.dma_start(x_all[:, bass.ds(i * BATCH, BATCH), :],
                                     x_tiles[:, bass.ds(i * BATCH, BATCH), :]).then_inc(x_landed, 16)

                    def store_turned(i):
                        for j in range(BATCH):
                            sp.wait_ge(xt_made, i * BATCH + j + 1)
                            sp.dma_start(xt_tiles[:, bass.ds(i * BATCH + j, 1), :], xt[:, j:j + 1, :]).then_inc(xt_stored[j], 16)

                    def store_y(i):
                        for j in range(BATCH):
                            sp.wait_ge(y_made, i * BATCH + j + 1)
                            sp.dma_start(y_tiles[:, bass.ds(i * BATCH + j, 1), :], y[:, j:j + 1, :]).then_inc(y_stored[j], 16)

                    sp.dma_start(w_node[:, :, :], w_gnn[0:D, :].rearrange("(k p) n -> p k n", p=P)).then_inc(first_landed, 16)
                    sp.dma_start(b_rows[:, :], b_gnn.to_broadcast([P, D])).then_inc(first_landed, 16)
                    load_x(0)
                    sp.wait_ge(x_landed, 16)
                    load_x(1)
                    store_turned(0)
                    with sp.Fori(1, NB - 1) as i:
                        sp.wait_ge(x_landed, i * 16 + 16)
                        load_x(i + 1)
                        store_y(i - 1)
                        store_turned(i)
                    store_y(NB - 2)
                    store_turned(NB - 1)
                    for h in range(2):
                        sp.dma_start(w_edge[h * D_EDGE:(h + 1) * D_EDGE, :], w_gnn[D:D + D_EDGE, :]).then_inc(consts_landed, 16)
                    sp.dma_start(gamma_rows[:, :], gamma.to_broadcast([P, D])).then_inc(consts_landed, 16)
                    sp.dma_start(beta_rows[:, :], beta.to_broadcast([P, D])).then_inc(consts_landed, 16)
                    sp.dma_start(bout_rows[:, :], bout.to_broadcast([P, D])).then_inc(consts_landed, 16)
                    sp.dma_start(rb_rows[:, :], router_b.to_broadcast([P, EXPERTS])).then_inc(consts_landed, 16)
                    sp.dma_start(wkv[:, :, 0:INNER], wk_t.rearrange("(k p) n -> p k n", p=P)).then_inc(consts_landed, 16)
                    sp.dma_start(wkv[:, :, INNER:2 * INNER], wv_t.rearrange("(k p) n -> p k n", p=P)).then_inc(consts_landed, 16)
                    sp.dma_start(wq_sb[:, :, :], wq.rearrange("(k p) n -> p k n", p=P)).then_inc(consts_landed, 16)
                    sp.dma_start(wo_sb[:, :, :], wout_t.rearrange("(k p) n -> p k n", p=P)).then_inc(consts_landed, 16)
                    sp.dma_start(router[:, :, :], router_t.rearrange("(k p) n -> p k n", p=P)).then_inc(consts_landed, 16)
                    sp.wait_ge(zeroed, 3)
                    for t in range(NT, NKV):
                        sp.dma_start(xt_dram[t], zeros[:, :]).then_inc(zeros_stored, 16)
                    with sp.Fori(0, SLOT_TILES // 2) as i:
                        sp.dma_start(slot_tiles[:, bass.ds(i * 2, 2), :], empty_rows[:, :, :]).then_inc(zeros_stored, 16)
                    store_y(NB - 1)
                    sp.wait_ge(zeros_stored, 16 * (NKV - NT + SLOT_TILES // 2))
                    sp.wait_ge(consts_landed, 16 * n_consts)
                    for j in range(BATCH):
                        sp.wait_ge(xt_stored[j], 16 * NB)
                        sp.wait_ge(y_stored[j], 16 * NB)

                @block.gpsimd
                def _(pool):
                    pool.dma_start(dst_i[:, :], dst).then_inc(edges_landed, 16)
                    pool.dma_start(base_i[:, :], base_group.to_broadcast([P, NS * GROUPS])).then_inc(edges_landed, 16)
                    for g in range(GROUPS):
                        pool.dma_start(base_row_i[g * WINDOW:(g + 1) * WINDOW, :],
                                       base_row[g:g + 1, :].to_broadcast([WINDOW, NS])).then_inc(edges_landed, 16)
                    pool.memset(ident[:, :], 0.0).then_inc(pool_consts, 1)
                    pool.memset(tri[:, :], 1.0).then_inc(pool_consts, 1)
                    pool.memset(ones[:, :], 1.0).then_inc(consts_made, 1)
                    pool.memset(zeros[:, :], 0.0).then_inc(zeroed, 1)
                    pool.memset(empty_rows[:, :, :], 0.0).then_inc(zeroed, 1)
                    pool.wait_ge(zeroed, 2)
                    pool.memset(empty_rows[:, :, NODE:NODE + 1], float(NO_NODE)).then_inc(zeroed, 1)
                    pool.iota(iota_i[:, :], [[1, D]], base=0, channel_multiplier=0).then_inc(consts_made, 1)
                    pool.iota(row_i[:, :], [[0, 1]], base=0, channel_multiplier=1).then_inc(consts_made, 1)
                    pool.memset(eps[:, 0:1], LN_EPS).then_inc(consts_made, 1)
                    pool.memset(eps[:, 1:2], GNN_EPS).then_inc(consts_made, 1)
                    pool.wait_ge(pool_consts, 2)
                    pool.affine_select(out=ident[:, :], in_=ident[:, :], compare_op=ALU.not_equal, fill=1.0, base=0,
                                       pattern=[[-1, P]], channel_multiplier=1).then_inc(consts_made, 1)
                    pool.affine_select(out=tri[:, :], in_=tri[:, :], compare_op=ALU.is_gt, fill=0.0, base=0,
                                       pattern=[[1, P]], channel_multiplier=-1).then_inc(consts_made, 1)
                    pool.memset(acc[:, :, :], 0.0).then_inc(acc_cleared, 1)
                    pool.wait_ge(acc_cleared, 1)

                @block.vector
                def _(dve):
                    steps = 0

                    def link(ins):
                        nonlocal steps
                        steps += 1
                        ins.then_inc(a_steps, 1)
                        dve.wait_ge(a_steps, steps)

                    def norm(i, first=False):
                        dve.wait_ge(x_landed, i * 16 + 16)
                        for j in range(BATCH):
                            dve.bn_stats(stats[:, j, :], x_all[:, bass.ds(i * BATCH + j, 1), :]).then_inc(a_steps, 1)
                        dve.wait_ge(a_steps, i * 2 * BATCH + BATCH)
                        dve.sem_inc(dve_tick, 1)
                        for j in range(BATCH):
                            dve.bn_aggr(moments[:, j, :], stats[:, j, :]).then_inc(a_steps, 1)
                        dve.wait_ge(rooted, i + 1)
                        dve.reciprocal(rstd[:, :], rstd[:, :]).then_inc(rstd_made, 1)
                        dve.wait_ge(rstd_made, i + 1)
                        for j in range(BATCH):
                            if not first:
                                dve.wait_ge(turned, i * BATCH + j + 1 - BATCH)
                            dve.tensor_scalar(xn[:, j, :], x_all[:, bass.ds(i * BATCH + j, 1), :], moments[:, j, 0:1], rstd[:, j:j + 1],
                                              ALU.subtract, ALU.mult).then_inc(xn_made, 1)

                    def add_bias(i, first=False):
                        for j in range(BATCH):
                            dve.wait_ge(y_summed, i * BATCH + min(j | 1, BATCH - 1) + 1)
                            if not first:
                                dve.wait_ge(y_stored[j], i * 16)
                            dve.tensor_tensor(y[:, j, :], banks[:, 2 + j // 2, (j % 2) * D:(j % 2 + 1) * D],
                                              b_rows[:, :], ALU.add).then_inc(y_made, 1)

                    norm(0, first=True)
                    dve.wait_ge(first_landed, 16 * 2)
                    norm(1)
                    add_bias(0, first=True)
                    with dve.Fori(2, NB) as i:
                        norm(i)
                        add_bias(i - 1)
                    add_bias(NB - 1)

                    steps = NB * 2 * BATCH
                    dve.wait_ge(consts_landed, 16 * n_consts)
                    dve.wait_ge(consts_made, 7)
                    dve.wait_ge(edges_landed, 16 * (2 + GROUPS))
                    w_heads = wkv.rearrange("p k (h d) -> p (k h) d", d=DH)
                    link(dve.tensor_reduce(wkv_mean[:, :], w_heads, AX.X, ALU.add))
                    link(dve.tensor_scalar(wkv_mean[:, :], wkv_mean[:, :], 1.0 / DH, None, ALU.mult))
                    link(dve.tensor_tensor(w_heads, w_heads, wkv_mean[:, :, None].to_broadcast([P, KC * 2 * HEADS, DH]), ALU.subtract))
                    link(dve.tensor_tensor(beta_rows[:, :], beta_rows[:, :], bout_rows[:, :], ALU.add))
                    link(dve.tensor_copy(iota[:, :], iota_i[:, :]))
                    link(dve.tensor_copy(row[:, :], row_i[:, :]))
                    link(dve.tensor_copy(dst_f[:, :, :, :], dst_i.rearrange("p (s k g) -> p s k g", k=QUADS, g=GROUPS)))
                    link(dve.tensor_copy(base_f[:, :, :], base_i.rearrange("p (s g) -> p s g", g=GROUPS)))
                    link(dve.tensor_copy(row_node[:, :], base_row_i[:, :]))
                    link(dve.tensor_scalar(block_i[:, :], base_i.rearrange("p (s g) -> p s g", g=GROUPS)[:, :, 0], 7, None,
                                           ALU.arith_shift_right))
                    link(dve.tensor_copy(block_f[:, :], block_i[:, :]))
                    link(dve.tensor_scalar(block_f[:, :], block_f[:, :], float(NT - 1), 0.0, ALU.min, ALU.max))
                    link(dve.tensor_copy(block_i[:, :], block_f[:, :]))
                    link(dve.tensor_scalar(block_f[:, :], block_f[:, :], float(P), None, ALU.mult))
                    link(dve.tensor_tensor(rel.rearrange("p s (k g) -> p s k g", g=GROUPS), dst_f[:, :, :, :],
                                           base_f[:, :, None, :].to_broadcast([P, NS, QUADS, GROUPS]), ALU.subtract))
                    for g in range(GROUPS):
                        rows = slice(g * WINDOW, (g + 1) * WINDOW)
                        link(dve.tensor_scalar(row_node[rows, :], row_node[rows, :], row[rows, :], float(-g * WINDOW), ALU.add, ALU.add))
                    link(dve.tensor_tensor(place[:, :], row_node[:, :], block_f[:, :], ALU.subtract))
                    dst_s = dst_f.rearrange("p s k g -> p s (k g)")
                    link(dve.tensor_tensor(work[:, :, :], dst_s, block_f[:, :, None].to_broadcast([P, NS, TILES]), ALU.subtract))
                    link(dve.tensor_scalar(missed[:, :, :], work[:, :, :], 0.0, None, ALU.is_ge))
                    link(dve.scalar_tensor_tensor(out=missed[:, :, :], in0=work[:, :, :], scalar=float(2 * P), in1=missed[:, :, :],
                                                  op0=ALU.is_lt, op1=ALU.mult))
                    link(dve.scalar_tensor_tensor(out=missed[:, :, :], in0=rel[:, :, :], scalar=0.0, in1=missed[:, :, :],
                                                  op0=ALU.is_ge, op1=ALU.mult))
                    link(dve.scalar_tensor_tensor(out=missed[:, :, :], in0=rel[:, :, :], scalar=float(WINDOW), in1=missed[:, :, :],
                                                  op0=ALU.is_lt, op1=ALU.mult))
                    link(dve.tensor_scalar(missed[:, :, :], missed[:, :, :], -1.0, 1.0, ALU.mult, ALU.add))
                    link(dve.scalar_tensor_tensor(out=missed[:, :, :], in0=dst_s, scalar=float(PAD_DST), in1=missed[:, :, :],
                                                  op0=ALU.is_lt, op1=ALU.mult))
                    link(dve.tensor_reduce(miss_sum[:, 0:1], missed[:, :, :].rearrange("p s t -> p (s t)"), AX.X, ALU.add))

                @block.scalar
                def _(act):
                    def copy_turned(i, first=False):
                        for j in range(BATCH):
                            act.wait_ge(turned, i * BATCH + j + 1)
                            if not first:
                                act.wait_ge(xt_stored[j], i * 16)
                                act.wait_ge(y_summed, i * BATCH + j + 1 - BATCH)
                            act.copy(xt[:, j, :], banks[:, j % 2, 0:D]).then_inc(xt_made, 1)

                    def root(i):
                        act.wait_ge(a_steps, (i + 1) * 2 * BATCH)
                        act.activation(rstd[:, :], moments[:, :, 1], ACT.Sqrt, bias=eps[:, 0:1]).then_inc(rooted, 1)
                    act.wait_ge(consts_made, 7)
                    root(0)
                    copy_turned(0, first=True)
                    with act.Fori(1, NB) as i:
                        act.wait_ge(xn_made, i * BATCH)
                        root(i)
                        copy_turned(i)

                @block.tensor
                def _(pe):
                    def turn(i, j, first=False):
                        pe.wait_ge(xn_made, i * BATCH + j + 1)
                        if not (first and j < 2):
                            pe.wait_ge(xt_made, i * BATCH + j - 1)
                        for k in range(KC):
                            ins = pe.transpose(banks[:, j % 2, k * P:(k + 1) * P], xn[:, j, k * P:(k + 1) * P], ident[:, :])
                        ins.then_inc(turned, 1)

                    def multiply(i, j, first=False):
                        pe.wait_ge(xt_made, i * BATCH + j + 1)
                        if not first:
                            pe.wait_ge(y_made, i * BATCH + min(j | 1, BATCH - 1) + 1 - BATCH)
                        for k in range(KC):
                            ins = pe.matmul(banks[:, 2 + j // 2, (j % 2) * D:(j % 2 + 1) * D], xt[:, j, k * P:(k + 1) * P],
                                            w_node[:, k, :], start=(k == 0), stop=(k == KC - 1))
                        ins.then_inc(y_summed, 1)

                    def batch(i, first=False):
                        for j in range(BATCH + 1):
                            if j < BATCH:
                                turn(i, j, first)
                            if j >= 1:
                                multiply(i, j - 1, first)
                    pe.wait_ge(consts_made, 7)
                    pe.wait_ge(first_landed, 16 * 2)
                    batch(0, first=True)
                    with pe.Fori(1, NB) as i:
                        batch(i)


        dots_t = sb("dots_t", [P, PAIRS, P])
        with ExitStack() as ctx_b:
            def sb_b(name, shape, dt=F32):
                return ctx_b.enter_context(nc.sbuf_tensor(name, shape, dt))

            gather_index = sb_b("gather_index", [P, 2, TILES], I32)
            attr_sb = sb_b("attr_sb", [P, 2, TILES // 2 * P])
            msg = sb_b("msg", [P, 2 * QUADS, GROUPS, D])
            mask = sb_b("mask", [P, 2, TILES, WINDOW])
            place_mask = sb_b("place_mask", [P, 2, 2 * P])
            window = sb_b("window", [P, 2, D])
            kv_xt = sb_b("kv_xt", [P, 2, D])
            kv = sb_b("kv", [P, 2, 2 * INNER])
            squares = sb_b("squares", [P, 2 * INNER])
            head_var = sb_b("head_var", [P, 2 * HEADS])
            kv_scale = sb_b("kv_scale", [P, HEADS])

            index_landed = [sem(f"index_landed{h}") for h in range(2)]
            attr_landed = [sem(f"attr_landed{h}") for h in range(2)]
            kv_xt_landed = [sem(f"kv_xt_landed{h}") for h in range(2)]
            gathered = [sem(f"gathered{c}") for c in range(2 * QUADS)]
            edge_summed = sem("edge_summed")
            msg_added = sem("msg_added")
            silu_done = sem("silu_done")
            segments_summed = sem("segments_summed")
            mask_made = sem("mask_made")
            place_made = sem("place_made")
            window_copied = sem("window_copied")
            placed = sem("placed")
            acc_added = sem("acc_added")
            kv_multiplied = sem("kv_multiplied")
            kv_copied = sem("kv_copied")
            squared = sem("squared")
            var_summed = sem("var_summed")
            heads_rooted = sem("heads_rooted")
            heads_inverted = sem("heads_inverted")
            scale_made = sem("scale_made")
            v_scaled = sem("v_scaled")
            dots_done = sem("dots_done")
            miss_found = sem("miss_found")
            miss_known = sem("miss_known")
            NQ = 2 * QUADS

            with nc.Block() as block:
                @block.sync
                def _(sp):
                    def load(i, h, kv_part, first=False):
                        s = i * 2 + h
                        if not first:
                            sp.wait_ge(segments_summed, i * NQ + (h - 1) * QUADS)
                        sp.dma_start(gather_index[:, h, :], src[bass.ds(s, 1)].rearrange("s p t -> (s p) t")).then_inc(index_landed[h], 16)
                        sp.dma_start(attr_sb[:, h:h + 1, :], attr[:, bass.ds(s, 1), :]).then_inc(attr_landed[h], 16)
                        if kv_part:
                            if not first:
                                sp.wait_ge(kv_multiplied, i * 4 + 2 * h - 2)
                            sp.dma_start(kv_xt[:, h:h + 1, :], xt_tiles[:, bass.ds(s, 1), :]).then_inc(kv_xt_landed[h], 16)
                    for h in range(2):
                        load(0, h, True, first=True)
                    with sp.Fori(1, KV_ITERS) as i:
                        for h in range(2):
                            load(i, h, True)
                    with sp.Fori(KV_ITERS, NI) as i:
                        for h in range(2):
                            load(i, h, False)

                @block.gpsimd
                def _(pool):
                    def gather(i, h, first=False):
                        for k in range(QUADS):
                            c = h * QUADS + k
                            if k == 0:
                                pool.wait_ge(index_landed[h], i * 16 + 16)
                            if not first:
                                pool.wait_ge(segments_summed, i * NQ + c + 1 - NQ)
                            pool.sem_inc(pool_tick, 1)
                            for g in range(GROUPS):
                                t = k * GROUPS + g
                                pool.indirect_dma_start(
                                    msg[:, c, g, :], None, y_dram,
                                    bass.IndirectOffsetOnAxis(ap=gather_index[:, h, t:t + 1], axis=0),
                                    bounds_check=N_NODES - 1, oob_is_err=False).then_inc(gathered[c], 16)

                    for h in range(2):
                        gather(0, h, first=True)
                    with pool.Fori(1, NI) as i:
                        for h in range(2):
                            gather(i, h)

                @block.tensor
                def _(pe):
                    def edge_products(i, c, first=False):
                        h, k = divmod(c, QUADS)
                        if k == 0:
                            pe.wait_ge(attr_landed[h], i * 16 + 16)
                        if not (first and c < 2):
                            pe.wait_ge(msg_added, i * NQ + c - 1)
                        for g in range(GROUPS):
                            half, pair = g % 2, g // 2
                            rows = slice(half * D_EDGE, (half + 1) * D_EDGE)
                            col = (k * (GROUPS // 2) + pair) * P
                            ins = pe.matmul(banks[:, (c % 2) * 2 + half, pair * D:(pair + 1) * D],
                                            attr_sb[rows, h, col:col + P], w_edge[rows, :], start=True, stop=True)
                        ins.then_inc(edge_summed, 1)

                    def segment_sums(i, c, first=False):
                        h, k = divmod(c, QUADS)
                        pe.wait_ge(silu_done, i * NQ + c + 1)
                        if k == 0:
                            pe.wait_ge(mask_made, i * 2 + h + 1)
                            if not (first and h == 0):
                                pe.wait_ge(window_copied, i * 2 + h)
                        for g in range(GROUPS):
                            ins = pe.matmul(banks[g * WINDOW:(g + 1) * WINDOW, 4, 0:D], mask[:, h, k * GROUPS + g, :],
                                            msg[:, c, g, :], start=(k == 0), stop=(k == QUADS - 1))
                        ins.then_inc(segments_summed, 1)

                    def place_windows(i, h, first=False):
                        pe.wait_ge(window_copied, i * 2 + h + 1)
                        pe.wait_ge(place_made, i * 2 + h + 1)
                        if not (first and h == 0):
                            pe.wait_ge(acc_added, i * 2 + h)
                        for b in range(2):
                            ins = pe.matmul(banks[:, 5, b * D:(b + 1) * D], place_mask[:, h, b * P:(b + 1) * P],
                                            window[:, h, :], start=True, stop=True)
                        ins.then_inc(placed, 1)

                    def keys_values(i, h, part, first=False):
                        if part == 0:
                            pe.wait_ge(kv_xt_landed[h], i * 16 + 16)
                        if not (first and h == 0 and part == 0):
                            pe.wait_ge(kv_copied, i * 4 + 2 * h + part)
                        for k in range(KC):
                            ins = pe.matmul(banks[:, 6, :], kv_xt[:, h, k * P:(k + 1) * P],
                                            wkv[:, k, part * INNER:(part + 1) * INNER], start=(k == 0), stop=(k == KC - 1))
                        ins.then_inc(kv_multiplied, 1)

                    def dots(i, h, first=False):
                        pe.wait_ge(v_scaled, i * 2 + h + 1)
                        for q in range(PAIRS):
                            ins = pe.matmul(banks[:, 7, q * P:(q + 1) * P], kv[:, h, INNER + q * P:INNER + (q + 1) * P],
                                            kv[:, h, q * P:(q + 1) * P], start=(first and h == 0 and q == 0), stop=True,
                                            skip_group_check=True)
                        ins.then_inc(dots_done, 1)

                    def supertiles(i, kv_part, first=False, before=True):
                        for c in range(NQ):
                            h, k = divmod(c, QUADS)
                            edge_products(i, c, first)
                            if c >= 1:
                                segment_sums(i, c - 1, first)
                            elif before:
                                segment_sums(i - 1, NQ - 1)
                            if k == 1:
                                if h == 1:
                                    place_windows(i, 0, first)
                                elif before:
                                    place_windows(i - 1, 1)
                            if kv_part and k == 0:
                                keys_values(i, h, 0, first)
                            if kv_part and k == 1:
                                keys_values(i, h, 1, first)
                            if kv_part and k == 2:
                                if h == 1:
                                    dots(i, 0, first)
                                elif before:
                                    dots(i - 1, 1)

                    supertiles(0, True, first=True, before=False)
                    supertiles(1, True)
                    with pe.Fori(2, KV_ITERS) as i:
                        supertiles(i, True)
                    dots(KV_ITERS - 1, 1)
                    with pe.Fori(KV_ITERS, NI) as i:
                        supertiles(i, False)
                    segment_sums(NI - 1, NQ - 1)
                    place_windows(NI - 1, 1)
                    pe.wait_ge(dots_copied, 1)
                    pe.matmul(banks[:, 6, 0:1], ones[:, :], miss_sum[:, 0:1], start=True, stop=True).then_inc(miss_found, 1)

                @block.vector
                def _(dve):
                    def add_products(i, c):
                        dve.wait_ge(edge_summed, i * NQ + c + 1)
                        dve.wait_ge(gathered[c], (i + 1) * 16 * GROUPS)
                        b = (c % 2) * 2
                        by_bank = msg[:, c, :, :].rearrange("p (q h) d -> p h q d", h=2)
                        dve.tensor_tensor(by_bank, by_bank, banks[:, b:b + 2, :].rearrange("p h (q d) -> p h q d", q=2),
                                          ALU.add).then_inc(msg_added, 1)

                    def masks(i, h, first=False):
                        s = i * 2 + h
                        if not first:
                            dve.wait_ge(segments_summed, i * NQ + (h - 1) * QUADS)
                        dve.tensor_tensor(mask[:, h, :, :], iota[:, None, 0:WINDOW].to_broadcast([P, TILES, WINDOW]),
                                          rel[:, bass.ds(s, 1), :].rearrange("p s t -> p (s t)")[:, :, None].to_broadcast([P, TILES, WINDOW]),
                                          ALU.is_equal).then_inc(mask_made, 1)
                        if not first:
                            dve.wait_ge(placed, i * 2 + h - 1)
                        dve.tensor_scalar(place_mask[:, h, :], iota[:, :], place[:, bass.ds(s, 1)], None,
                                          ALU.is_equal).then_inc(place_made, 1)

                    def add_blocks(i, h, first=False):
                        block = dve.value_load(block_i[0:1, bass.ds(i * 2 + h, 1)], min_val=0, max_val=NT - 1)
                        dve.wait_ge(placed, i * 2 + h + 1)
                        if not (first and h == 0):
                            dve.wait_ge(acc_added, i * 2 + h)
                        both = acc[:, bass.ds(block, 2), :]
                        dve.tensor_tensor(both, both, banks[:, 5, :].rearrange("p (b d) -> p b d", b=2), ALU.add).then_inc(acc_added, 1)

                    def head_scales(i, h, first=False):
                        t = i * 2 + h
                        dve.wait_ge(squared, t + 1)
                        if not (first and h == 0):
                            dve.wait_ge(scale_made, t)
                        dve.tensor_reduce(head_var[:, :], squares.rearrange("p (g d) -> p g d", d=DH), AX.X, ALU.add).then_inc(var_summed, 1)

                    def scale_values(i, h, first=False):
                        t = i * 2 + h
                        dve.wait_ge(heads_rooted, t + 1)
                        dve.reciprocal(head_var[:, :], head_var[:, :]).then_inc(heads_inverted, 1)
                        dve.wait_ge(heads_inverted, t + 1)
                        if not (first and h == 0):
                            dve.wait_ge(v_scaled, t)
                        dve.tensor_tensor(kv_scale[:, :], head_var[:, 0:HEADS], head_var[:, HEADS:2 * HEADS], ALU.mult).then_inc(scale_made, 1)
                        dve.wait_ge(scale_made, t + 1)
                        v = kv[:, h, INNER:2 * INNER].rearrange("p (g d) -> p g d", d=DH)
                        dve.tensor_tensor(v, v, kv_scale[:, :, None].to_broadcast([P, HEADS, DH]), ALU.mult).then_inc(v_scaled, 1)

                    def supertiles(i, kv_part, first=False, before=True):
                        for c in range(NQ):
                            h, k = divmod(c, QUADS)
                            if k == 0:
                                masks(i, h, first)
                            add_products(i, c)
                            if k == 2:
                                if h == 1:
                                    add_blocks(i, 0, first)
                                elif before:
                                    add_blocks(i - 1, 1)
                            if kv_part and k == 0 and (h == 1 or before):
                                scale_values(*((i, 0) if h == 1 else (i - 1, 1)), first)
                            if kv_part and k == 2:
                                head_scales(i, h, first)

                    supertiles(0, True, first=True, before=False)
                    supertiles(1, True)
                    with dve.Fori(2, KV_ITERS) as i:
                        supertiles(i, True)
                    scale_values(KV_ITERS - 1, 1)
                    dve.wait_ge(dots_done, NKV)
                    dve.tensor_copy(dots_t[:, :, :], banks[:, 7, :].rearrange("p (q d) -> p q d", q=PAIRS)).then_inc(dots_copied, 1)
                    with dve.Fori(KV_ITERS, NI) as i:
                        supertiles(i, False)
                    add_blocks(NI - 1, 1)
                    dve.wait_ge(miss_found, 1)
                    dve.tensor_scalar(miss_i[:, :], banks[:, 6, 0:1], 1.0, None, ALU.min).then_inc(miss_known, 1)
                    dve.wait_ge(miss_known, 1)
                    dve.wait_ge(acc_added, NS)

                @block.scalar
                def _(act):
                    def silu(i, c):
                        act.wait_ge(msg_added, i * NQ + c + 1)
                        act.activation(msg[:, c, :, :], msg[:, c, :, :], ACT.Silu).then_inc(silu_done, 1)

                    def copy_window(i, h, first=False):
                        act.wait_ge(segments_summed, i * NQ + (h + 1) * QUADS)
                        if not first:
                            act.wait_ge(placed, i * 2 + h - 1)
                        act.copy(window[:, h, :], banks[:, 4, 0:D]).then_inc(window_copied, 1)

                    def copy_kv(i, h, part, first=False):
                        act.wait_ge(kv_multiplied, i * 4 + 2 * h + part + 1)
                        if not first and part == 0:
                            act.wait_ge(dots_done, i * 2 + h - 1)
                        act.copy(kv[:, h, part * INNER:(part + 1) * INNER], banks[:, 6, :]).then_inc(kv_copied, 1)

                    def square(i, h, first=False):
                        act.wait_ge(kv_copied, i * 4 + 2 * h + 2)
                        if not (first and h == 0):
                            act.wait_ge(var_summed, i * 2 + h)
                        act.activation(squares[:, :], kv[:, h, :], ACT.Square).then_inc(squared, 1)

                    def root(i, h):
                        act.wait_ge(var_summed, i * 2 + h + 1)
                        act.activation(head_var[:, :], head_var[:, :], ACT.Sqrt, bias=eps[:, 0:1], scale=1.0 / DH).then_inc(heads_rooted, 1)

                    def supertiles(i, kv_part, first=False, before=True):
                        for c in range(NQ):
                            h, k = divmod(c, QUADS)
                            if kv_part and k == 0 and (h == 1 or before):
                                root(*((i, 0) if h == 1 else (i - 1, 1)))
                            silu(i, c)
                            if k == 0:
                                if h == 1:
                                    copy_window(i, 0, first)
                                elif before:
                                    copy_window(i - 1, 1, first=(isinstance(i, int) and i == 1))
                            if kv_part and k == 0:
                                copy_kv(i, h, 0, first)
                            if kv_part and k == 1:
                                copy_kv(i, h, 1, first)
                                square(i, h, first)

                    supertiles(0, True, first=True, before=False)
                    supertiles(1, True)
                    with act.Fori(2, KV_ITERS) as i:
                        supertiles(i, True)
                    root(KV_ITERS - 1, 1)
                    with act.Fori(KV_ITERS, NI) as i:
                        supertiles(i, False)
                    copy_window(NI - 1, 1)

        with ExitStack() as ctx_g:
            def sb_g(name, shape, dt=F32):
                return ctx_g.enter_context(nc.sbuf_tensor(name, shape, dt))

            any_missed = nc.values_load(miss_i[0:1, 0:1], min_val=0, max_val=1)
            index_g = sb_g("index_g", [P, 1], I32)
            attr_g = sb_g("attr_g", [P, P])
            msg_g = sb_g("msg_g", [P, D])
            wanted = sb_g("wanted", [P, 1])
            mask_g = sb_g("mask_g", [P, P])
            edges_loaded_g = sem("edges_loaded_g")
            gathered_g = sem("gathered_g")
            product_g = sem("product_g")
            added_g = sem("added_g")
            silu_g = sem("silu_g")
            wanted_g = sem("wanted_g")
            mask_made_g = sem("mask_made_g")
            summed_g = sem("summed_g")
            acc_g = sem("acc_g")
            tile_done_g = sem("tile_done_g")

            with nc.If(any_missed):
                with nc.Block() as block:
                    def each_tile(engine, body):
                        with engine.Fori(0, NS) as s:
                            with engine.Fori(0, TILES // 2) as pair:
                                for half in range(2):
                                    body(s, pair, half, (s * (TILES // 2) + pair) * 2 + half)

                    @block.sync
                    def _(sp):
                        def load(s, pair, half, u):
                            sp.wait_ge(tile_done_g, u + 1)
                            with nc.allow_non_contiguous_dma(reason="one column of indices"):
                                sp.dma_start(index_g[:, :], src[bass.ds(s, 1), :, bass.ds(pair * 2 + half, 1)].rearrange("s p t -> (s p) t")).then_inc(edges_loaded_g, 16)
                            rows = slice(half * D_EDGE, (half + 1) * D_EDGE)
                            sp.dma_start(attr_g[rows, :], attr[rows, bass.ds(s, 1), bass.ds(pair * P, P)].rearrange("p s e -> p (s e)")).then_inc(edges_loaded_g, 16)
                        sp.sem_inc(tile_done_g, 1)
                        each_tile(sp, load)

                    @block.gpsimd
                    def _(pool):
                        def gather(s, pair, half, u):
                            pool.wait_ge(edges_loaded_g, (u + 1) * 32)
                            pool.sem_inc(pool_tick, 1)
                            pool.indirect_dma_start(msg_g[:, :], None, y_dram, bass.IndirectOffsetOnAxis(ap=index_g[:, 0:1], axis=0),
                                                    bounds_check=N_NODES - 1, oob_is_err=False).then_inc(gathered_g, 16)
                        each_tile(pool, gather)

                    @block.tensor
                    def _(pe):
                        def products(s, pair, half, u):
                            rows = slice(half * D_EDGE, (half + 1) * D_EDGE)
                            pe.wait_ge(edges_loaded_g, (u + 1) * 32)
                            pe.matmul(banks[:, 0, 0:D], attr_g[rows, :], w_edge[rows, :], start=True, stop=True).then_inc(product_g, 1)
                            pe.wait_ge(silu_g, u + 1)
                            pe.sem_inc(pe_tick, 1)
                            with pe.Fori(0, NT) as b:
                                v = u * NT + b
                                pe.wait_ge(mask_made_g, v + 1)
                                pe.matmul(banks[:, 1, 0:D], mask_g[:, :], msg_g[:, :], start=True, stop=True).then_inc(summed_g, 1)
                        each_tile(pe, products)

                    @block.scalar
                    def _(act):
                        def silu(s, pair, half, u):
                            act.wait_ge(added_g, u + 1)
                            act.activation(msg_g[:, :], msg_g[:, :], ACT.Silu).then_inc(silu_g, 1)
                        each_tile(act, silu)

                    @block.vector
                    def _(dve):
                        def add(s, pair, half, u):
                            dve.wait_ge(product_g, u + 1)
                            dve.wait_ge(gathered_g, (u + 1) * 16)
                            dve.tensor_tensor(msg_g[:, :], msg_g[:, :], banks[:, 0, 0:D], ALU.add).then_inc(added_g, 1)
                            dst_tile = dst_f.rearrange("p s k g -> p s (k g)")[:, bass.ds(s, 1), bass.ds(pair * 2 + half, 1)].rearrange("p s t -> p (s t)")
                            missed_tile = missed[:, bass.ds(s, 1), bass.ds(pair * 2 + half, 1)].rearrange("p s t -> p (s t)")
                            dve.scalar_tensor_tensor(out=wanted[:, :], in0=dst_tile, scalar=1.0, in1=missed_tile,
                                                     op0=ALU.add, op1=ALU.mult).then_inc(wanted_g, 1)
                            dve.wait_ge(wanted_g, u * (NT + 2) + 1)
                            dve.tensor_scalar(wanted[:, :], wanted[:, :], 1.0, None, ALU.subtract).then_inc(wanted_g, 1)
                            with dve.Fori(0, NT) as b:
                                v = u * NT + b
                                dve.wait_ge(wanted_g, u * (NT + 2) + b + 2)
                                dve.tensor_scalar(mask_g[:, :], iota[:, 0:P], wanted[:, :], None, ALU.is_equal).then_inc(mask_made_g, 1)
                                dve.wait_ge(mask_made_g, v + 1)
                                dve.tensor_scalar(wanted[:, :], wanted[:, :], float(P), None, ALU.subtract).then_inc(wanted_g, 1)
                                dve.wait_ge(summed_g, v + 1)
                                block_b = acc[:, bass.ds(b, 1), :]
                                dve.tensor_tensor(block_b, block_b, banks[:, 1:2, 0:D], ALU.add).then_inc(acc_g, 1)
                            dve.wait_ge(acc_g, (u + 1) * NT)
                            dve.sem_inc(tile_done_g, 1)
                        each_tile(dve, add)

        node_rows = sb("node_rows", [P, NT, ROW])
        onehot = sb("onehot", [P, NT, EXPERTS])
        rank = sb("rank", [P, NT])
        before = sb("before", [P, BATCH + 1, EXPERTS])
        slot_i = sb("slot_i", [P, NT], I32)
        tile_expert = sb("tile_expert", [P, SLOT_TILES], I32)
        with ExitStack() as ctx_c:
            def sb_c(name, shape, dt=F32):
                return ctx_c.enter_context(nc.sbuf_tensor(name, shape, dt))

            dots_blocks = sb_c("dots_blocks", [P, PAIRS, P])
            dots_out = sb_c("dots_out", [P, PAIRS, D])
            w_mix = sb_c("w_mix", [P, KC, D])
            mix_xt = sb_c("mix_xt", [P, BATCH, D])
            x_rows = sb_c("x_rows", [P, BATCH, D])
            stats2 = sb_c("stats2", [P, BATCH, 6])
            moments2 = sb_c("moments2", [P, BATCH, 2])
            rstd2 = sb_c("rstd2", [P, BATCH])
            xf_t = sb_c("xf_t", [P, BATCH, D])
            xf_ring = sb_c("xf_ring", [P, BATCH, D])
            own_rank = sb_c("own_rank", [P, BATCH, EXPERTS])
            logits = sb_c("logits", [P, BATCH, EXPERTS])
            best = sb_c("best", [P, BATCH])
            reversed_iota = sb_c("reversed_iota", [P, EXPERTS])
            counts = sb_c("counts", [P, EXPERTS])
            counts_i = sb_c("counts_i", [P, EXPERTS], I32)
            ends = sb_c("ends", [P, 2, EXPERTS])
            tile_iota_i = sb_c("tile_iota_i", [P, SLOT_TILES], I32)
            node_i = sb_c("node_i", [P, NT], I32)
            tile_iota = sb_c("tile_iota", [P, SLOT_TILES])
            ended = sb_c("ended", [P, SLOT_TILES, EXPERTS])
            expert_f = sb_c("expert_f", [P, SLOT_TILES])
            slot_f = sb_c("slot_f", [P, NT])

            c_steps = sem("c_steps")
            dots_masked = sem("dots_masked")
            dots_out_summed = sem("dots_out_summed")
            dots_out_copied = sem("dots_out_copied")
            w_mix_summed = sem("w_mix_summed")
            w_mix_copied = sem("w_mix_copied")
            mix_xt_landed = [sem(f"mix_xt_landed{j}") for j in range(BATCH)]
            rows_landed = [sem(f"rows_landed{j}") for j in range(BATCH)]
            rows_added = sem("rows_added")
            mix_summed = sem("mix_summed")
            mix_added = sem("mix_added")
            aggregated = sem("aggregated")
            rooted2 = sem("rooted2")
            x2_made = sem("x2_made")
            xf_made = sem("xf_made")
            xf_turned = sem("xf_turned")
            xf_t_made = sem("xf_t_made")
            logits_summed = sem("logits_summed")
            logits_read = sem("logits_read")
            chosen = sem("chosen")
            ranked = sem("ranked")
            ranks_read = sem("ranks_read")
            tile_iota_made = sem("tile_iota_made")
            stats_made = sem("stats_made")
            inverted2 = sem("inverted2")
            centred = sem("centred")
            row_made = sem("row_made")
            choosing = sem("choosing")
            one_made = sem("one_made")
            carried = sem("carried")
            summed_before = sem("summed_before")
            rank_kept = sem("rank_kept")

            with nc.Block() as block:
                @block.sync
                def _(sp):
                    def load(i, first=False):
                        for j in range(BATCH):
                            if not first:
                                sp.wait_ge(mix_summed, (i - 1) * BATCH + j + 1)
                            sp.dma_start(mix_xt[:, j:j + 1, :], xt_tiles[:, bass.ds(i * BATCH + j, 1), :]).then_inc(mix_xt_landed[j], 16)
                            if not first:
                                sp.wait_ge(x2_made, (i - 1) * BATCH + j + 1)
                            sp.dma_start(x_rows[:, j:j + 1, :], x_tiles[:, bass.ds(i * BATCH + j, 1), :]).then_inc(rows_landed[j], 16)
                    load(0, first=True)
                    with sp.Fori(1, NB) as i:
                        load(i)

                @block.gpsimd
                def _(pool):
                    pool.iota(tile_iota_i[:, :], [[1, SLOT_TILES]], base=0, channel_multiplier=0).then_inc(tile_iota_made, 1)
                    pool.iota(node_i[:, :], [[P, NT]], base=0, channel_multiplier=1).then_inc(tile_iota_made, 1)

                    def add_rows(i):
                        for j in range(BATCH):
                            pool.wait_ge(rows_landed[j], i * 16 + 16)
                            pool.tensor_tensor(x_rows[:, j, :], x_rows[:, j, :], beta_rows[:, :], ALU.add).then_inc(rows_added, 1)
                    with pool.Fori(0, NB) as i:
                        add_rows(i)

                @block.tensor
                def _(pe):
                    pe.wait_ge(dots_masked, 1)
                    for q in range(PAIRS):
                        ins = pe.matmul(banks[:, q // 2, (q % 2) * D:(q % 2 + 1) * D], dots_blocks[:, q, :], wo_sb[:, q, :],
                                        start=True, stop=True)
                    ins.then_inc(dots_out_summed, 1)
                    pe.wait_ge(dots_out_copied, 1)
                    for k in range(KC):
                        for q in range(PAIRS):
                            ins = pe.matmul(banks[:, 2, k * D:(k + 1) * D], wq_sb[:, q, k * P:(k + 1) * P], dots_out[:, q, :],
                                            start=(q == 0), stop=(q == PAIRS - 1))
                    ins.then_inc(w_mix_summed, 1)
                    pe.wait_ge(w_mix_copied, 1)

                    def mix(i, first=False):
                        for j in range(BATCH):
                            pe.wait_ge(mix_xt_landed[j], i * 16 + 16)
                            if not first:
                                pe.wait_ge(mix_added, (i - 1) * BATCH + min(j | 1, BATCH - 1) + 1)
                            for k in range(KC):
                                ins = pe.matmul(banks[:, j // 2, (j % 2) * D:(j % 2 + 1) * D], mix_xt[:, j, k * P:(k + 1) * P],
                                                w_mix[:, k, :], start=(k == 0), stop=(k == KC - 1))
                            ins.then_inc(mix_summed, 1)

                    def turn(i, first=False):
                        for j in range(BATCH):
                            pe.wait_ge(xf_made, i * BATCH + j + 1)
                            if not (first and j < 2):
                                pe.wait_ge(xf_t_made, i * BATCH + j - 1)
                            for k in range(KC):
                                ins = pe.transpose(banks[:, 4 + j % 2, k * P:(k + 1) * P],
                                                   xf_ring[:, j, k * P:(k + 1) * P], ident[:, :])
                            ins.then_inc(xf_turned, 1)

                    def route(i, first=False):
                        if not first:
                            pe.wait_ge(logits_read, i)
                        for j in range(BATCH):
                            pe.wait_ge(xf_t_made, i * BATCH + j + 1)
                            for k in range(KC):
                                ins = pe.matmul(banks[:, 6, j * EXPERTS:(j + 1) * EXPERTS], xf_t[:, j, k * P:(k + 1) * P],
                                                router[:, k, :], start=(k == 0), stop=(k == KC - 1))
                        ins.then_inc(logits_summed, 1)

                    def count(i, first=False):
                        pe.wait_ge(chosen, i + 1)
                        if not first:
                            pe.wait_ge(ranks_read, i)
                        for j in range(BATCH):
                            out_j = banks[:, 7, j * EXPERTS:(j + 1) * EXPERTS]
                            pe.matmul(out_j, tri[:, :], logits[:, j, :], start=True, stop=False)
                            ins = pe.matmul(out_j, ones[:, :], before[:, j, :], start=False, stop=True)
                        ins.then_inc(ranked, 1)

                    mix(0, first=True)
                    turn(0, first=True)
                    route(0, first=True)
                    mix(1)
                    turn(1)
                    count(0, first=True)
                    route(1)
                    with pe.Fori(2, NB) as i:
                        mix(i)
                        turn(i)
                        count(i - 1)
                        route(i)
                    count(NB - 1)
                    pe.wait_ge(ranks_read, NB)
                    pe.matmul(banks[:, 7, 0:EXPERTS], ones[:, :], before[:, BATCH, :], start=True, stop=True).then_inc(ranked, 1)

                @block.scalar
                def _(act):
                    act.wait_ge(dots_out_summed, 1)
                    act.copy(dots_out[:, :, :], banks[:, 0:2, :].rearrange("p b (h d) -> p (b h) d", h=2)).then_inc(dots_out_copied, 1)
                    act.wait_ge(w_mix_summed, 1)
                    act.mul(w_mix[:, :, :], banks[:, 2, :].rearrange("p (k d) -> p k d", k=KC), 1.0 / N_NODES).then_inc(w_mix_copied, 1)

                    def root(i, n):
                        act.wait_ge(aggregated, i * 2 + n + 1)
                        act.activation(rstd2[:, :], moments2[:, :, 1], ACT.Sqrt,
                                       bias=eps[:, 1 - n:2 - n]).then_inc(rooted2, 1)

                    def copies(i):
                        for j in range(BATCH):
                            act.wait_ge(xf_turned, i * BATCH + j + 1)
                            act.copy(xf_t[:, j, :], banks[:, 4 + j % 2, 0:D]).then_inc(xf_t_made, 1)
                    root(0, 0)
                    root(0, 1)
                    act.wait_ge(xf_made, BATCH)
                    copies(0)
                    with act.Fori(1, NB) as i:
                        root(i, 0)
                        root(i, 1)
                        act.wait_ge(logits_summed, i)
                        act.wait_ge(xf_made, (i + 1) * BATCH)
                        copies(i)

                @block.vector
                def _(dve):
                    dve.memset(dots_blocks[:, :, :], 0.0).then_inc(c_steps, 1)
                    dve.wait_ge(c_steps, 1)
                    for h in range(2):
                        rows = slice(h * DH, (h + 1) * DH)
                        ins = dve.tensor_copy(dots_blocks[rows, :, rows], dots_t[rows, :, rows])
                    ins.then_inc(dots_masked, 1)
                    dve.wait_ge(tile_iota_made, 2)
                    dve.tensor_copy(node_rows[:, :, NODE], node_i[:, :])
                    dve.memset(node_rows[:, :, NODE + 1:ROW], 0.0)
                    dve.tensor_copy(tile_iota[:, :], tile_iota_i[:, :])
                    dve.tensor_scalar(reversed_iota[:, :], iota[:, 0:EXPERTS], -1.0, float(EXPERTS), ALU.mult, ALU.add)
                    dve.memset(before[:, 0, :], 0.0).then_inc(c_steps, 1)
                    dve.wait_ge(c_steps, 2)

                    def tile(i, j):
                        return node_rows[:, bass.ds(i * BATCH + j, 1), 0:D]

                    def acc_tile(i, j):
                        return acc[:, bass.ds(i * BATCH + j, 1), :]

                    def moments(i, n):
                        dve.sem_inc(dve_tick, 1)
                        for j in range(BATCH):
                            ins = dve.bn_stats(stats2[:, j, :], tile(i, j) if n else acc_tile(i, j))
                        ins.then_inc(stats_made, 1)
                        dve.wait_ge(stats_made, i * 2 + n + 1)
                        dve.sem_inc(dve_tick, 1)
                        for j in range(BATCH):
                            ins = dve.bn_aggr(moments2[:, j, :], stats2[:, j, :])
                        ins.then_inc(aggregated, 1)
                        dve.wait_ge(rooted2, i * 2 + n + 1)
                        dve.reciprocal(rstd2[:, :], rstd2[:, :]).then_inc(inverted2, 1)
                        dve.wait_ge(inverted2, i * 2 + n + 1)

                    def sum_and_norm(i, first=False):
                        moments(i, 0)
                        for j in range(BATCH):
                            dve.scalar_tensor_tensor(out=tile(i, j), in0=acc_tile(i, j), scalar=moments2[:, j, 0:1],
                                                     in1=gamma_rows[:, None, :], op0=ALU.subtract, op1=ALU.mult).then_inc(centred, 1)
                        for j in range(BATCH):
                            dve.wait_ge(centred, i * BATCH + j + 1)
                            dve.wait_ge(mix_summed, i * BATCH + min(j | 1, BATCH - 1) + 1)
                            dve.scalar_tensor_tensor(out=tile(i, j), in0=tile(i, j), scalar=rstd2[:, j:j + 1],
                                                     in1=banks[:, j // 2:j // 2 + 1, (j % 2) * D:(j % 2 + 1) * D],
                                                     op0=ALU.mult, op1=ALU.add).then_inc(mix_added, 1)
                        for j in range(BATCH):
                            dve.wait_ge(mix_added, i * BATCH + j + 1)
                            dve.wait_ge(rows_added, i * BATCH + j + 1)
                            dve.tensor_tensor(tile(i, j), tile(i, j), x_rows[:, j:j + 1, :], ALU.add).then_inc(x2_made, 1)
                        dve.wait_ge(x2_made, (i + 1) * BATCH)
                        moments(i, 1)
                        if not first:
                            dve.wait_ge(xf_turned, i * BATCH)
                        for j in range(BATCH):
                            dve.tensor_scalar(xf_ring[:, j:j + 1, :], tile(i, j), moments2[:, j, 0:1], rstd2[:, j:j + 1],
                                              ALU.subtract, ALU.mult).then_inc(xf_made, 1)
                        dve.tensor_copy(node_rows[:, bass.ds(i * BATCH, BATCH), MEAN], moments2[:, :, 0])
                        dve.tensor_copy(node_rows[:, bass.ds(i * BATCH, BATCH), RSTD], rstd2[:, :]).then_inc(row_made, 1)

                    def choose(i, first=False):
                        dve.wait_ge(logits_summed, i + 1)
                        if not first:
                            dve.wait_ge(ranked, i)
                        wide = [P, BATCH, EXPERTS]
                        ins = dve.tensor_tensor(logits[:, :, :], banks[:, 6, 0:BATCH * EXPERTS].rearrange("p (j e) -> p j e", j=BATCH),
                                                rb_rows[:, None, :].to_broadcast(wide), ALU.add)
                        ins.then_inc(logits_read, 1)
                        dve.wait_ge(logits_read, i + 1)
                        dve.tensor_reduce(best[:, :], logits[:, :, :], AX.X, ALU.max).then_inc(choosing, 1)
                        dve.wait_ge(choosing, i * 4 + 1)
                        dve.tensor_tensor(logits[:, :, :], logits[:, :, :], best[:, :, None].to_broadcast(wide), ALU.is_ge).then_inc(choosing, 1)
                        dve.wait_ge(choosing, i * 4 + 2)
                        dve.tensor_tensor(logits[:, :, :], logits[:, :, :], reversed_iota[:, None, :].to_broadcast(wide), ALU.mult).then_inc(choosing, 1)
                        dve.wait_ge(choosing, i * 4 + 3)
                        dve.tensor_reduce(best[:, :], logits[:, :, :], AX.X, ALU.max).then_inc(choosing, 1)
                        dve.wait_ge(choosing, i * 4 + 4)
                        dve.tensor_tensor(logits[:, :, :], logits[:, :, :], best[:, :, None].to_broadcast(wide), ALU.is_equal).then_inc(one_made, 1)
                        dve.wait_ge(one_made, i + 1)
                        if not first:
                            dve.tensor_copy(before[:, 0, :], before[:, BATCH, :]).then_inc(carried, 1)
                            dve.wait_ge(carried, i)
                        for j in range(BATCH):
                            dve.tensor_tensor(before[:, j + 1, :], before[:, j, :], logits[:, j, :], ALU.add).then_inc(summed_before, 1)
                            dve.wait_ge(summed_before, i * BATCH + j + 1)
                        dve.tensor_copy(onehot[:, bass.ds(i * BATCH, BATCH), :], logits[:, :, :]).then_inc(chosen, 1)

                    def read_ranks(i):
                        dve.wait_ge(ranked, i + 1)
                        dve.wait_ge(chosen, i + 1)
                        dve.tensor_tensor(own_rank[:, :, :], banks[:, 7, 0:BATCH * EXPERTS].rearrange("p (j e) -> p j e", j=BATCH),
                                          onehot[:, bass.ds(i * BATCH, BATCH), :], ALU.mult).then_inc(ranks_read, 1)
                        dve.wait_ge(ranks_read, i + 1)
                        dve.tensor_reduce(rank[:, bass.ds(i * BATCH, BATCH)], own_rank[:, :, :], AX.X, ALU.add).then_inc(rank_kept, 1)
                        dve.wait_ge(rank_kept, i + 1)

                    sum_and_norm(0, first=True)
                    sum_and_norm(1)
                    choose(0, first=True)
                    with dve.Fori(2, NB) as i:
                        sum_and_norm(i)
                        read_ranks(i - 2)
                        choose(i - 1)
                    read_ranks(NB - 2)
                    choose(NB - 1)
                    read_ranks(NB - 1)

                    steps = 2

                    def link(ins):
                        nonlocal steps
                        steps += 1
                        ins.then_inc(c_steps, 1)
                        dve.wait_ge(c_steps, steps)

                    dve.wait_ge(ranked, NB + 1)
                    link(dve.tensor_scalar(counts[:, :], banks[:, 7, 0:EXPERTS], float(P - 1), None, ALU.add))
                    link(dve.tensor_copy(counts_i[:, :], counts[:, :]))
                    link(dve.tensor_scalar(counts_i[:, :], counts_i[:, :], 7, None, ALU.arith_shift_right))
                    link(dve.tensor_copy(counts[:, :], counts_i[:, :]))
                    link(dve.tensor_copy(ends[:, 0, :], counts[:, :]))
                    a, shift = 0, 1
                    while shift < EXPERTS:
                        link(dve.tensor_copy(ends[:, 1 - a, 0:shift], ends[:, a, 0:shift]))
                        link(dve.tensor_tensor(ends[:, 1 - a, shift:], ends[:, a, shift:], ends[:, a, :EXPERTS - shift], ALU.add))
                        a, shift = 1 - a, 2 * shift
                    wide = [P, SLOT_TILES, EXPERTS]
                    link(dve.tensor_tensor(ended[:, :, :], tile_iota[:, :, None].to_broadcast(wide), ends[:, a:a + 1, :].to_broadcast(wide), ALU.is_ge))
                    link(dve.tensor_reduce(expert_f[:, :], ended[:, :, :], AX.X, ALU.add))
                    link(dve.tensor_scalar(expert_f[:, :], expert_f[:, :], float(EXPERTS - 1), None, ALU.min))
                    link(dve.tensor_copy(tile_expert[:, :], expert_f[:, :]))
                    link(dve.tensor_tensor(ends[:, 1 - a, :], ends[:, a, :], counts[:, :], ALU.subtract))
                    link(dve.tensor_tensor(ended[:, 0:NT, :], onehot[:, :, :], ends[:, 1 - a:2 - a, :].to_broadcast([P, NT, EXPERTS]), ALU.mult))
                    link(dve.tensor_reduce(slot_f[:, :], ended[:, 0:NT, :], AX.X, ALU.add))
                    link(dve.scalar_tensor_tensor(out=slot_f[:, :], in0=slot_f[:, :], scalar=float(P), in1=rank[:, :], op0=ALU.mult, op1=ALU.add))
                    link(dve.tensor_copy(slot_i[:, :], slot_f[:, :]))

        RING = 8
        ITERS = SLOT_TILES // RING
        assert SLOT_TILES == ITERS * RING
        with ExitStack() as ctx_d:
            def sb_d(name, shape, dt=F32):
                return ctx_d.enter_context(nc.sbuf_tensor(name, shape, dt))

            slot_rows = sb_d("slot_rows", [P, RING, ROW])
            weights = sb_d("weights", [P, RING, PACK])
            node = sb_d("node", [P, RING], I32)
            slot_xf = sb_d("slot_xf", [P, 2, D])
            slot_xt = sb_d("slot_xt", [P, 2, D])
            hidden_t = sb_d("hidden_t", [HID + 1, 2, P])
            result = sb_d("result", [P, RING, D])

            scattered = sem("scattered")
            loaded = [sem(f"loaded{c}") for c in range(RING)]
            result_stored = [sem(f"result_stored{c}") for c in range(RING)]
            ones_row_made = sem("ones_row_made")
            slots_normed = sem("slots_normed")
            slots_turned = sem("slots_turned")
            slots_t_made = sem("slots_t_made")
            hidden_summed = sem("hidden_summed")
            hidden_t_made = sem("hidden_t_made")
            result_summed = sem("result_summed")
            result_made = sem("result_made")
            LOADS = 2

            with nc.Block() as block:
                @block.sync
                def _(sp):
                    def load(i, first=False):
                        for c in range(RING):
                            expert = sp.value_load(tile_expert[0:1, bass.ds(i * RING + c, 1)], min_val=0, max_val=EXPERTS - 1)
                            if not first:
                                sp.wait_ge(result_made, i * RING + c + 1 - RING)
                            sp.dma_start(weights[:, c, :], experts[bass.ds(expert, 1)].rearrange("e p n -> (e p) n")).then_inc(loaded[c], 16)
                            if first and c == 0:
                                sp.wait_ge(scattered, 16 * NT)
                            sp.dma_start(slot_rows[:, c:c + 1, :], slot_tiles[:, bass.ds(i * RING + c, 1), :]).then_inc(loaded[c], 16)
                    load(0, first=True)
                    with sp.Fori(1, ITERS) as i:
                        load(i)

                @block.gpsimd
                def _(pool):
                    for t in range(NT):
                        pool.indirect_dma_start(sorted_in, bass.IndirectOffsetOnAxis(ap=slot_i[:, t:t + 1], axis=0), node_rows[:, t, :], None,
                                                bounds_check=SLOT_TILES * P - 1, oob_is_err=False).then_inc(scattered, 16)
                    with pool.Fori(0, ITERS) as i:
                        for c in range(RING):
                            pool.wait_ge(result_made, i * RING + c + 1)
                            pool.sem_inc(pool_tick, 1)
                            pool.indirect_dma_start(out, bass.IndirectOffsetOnAxis(ap=node[:, c:c + 1], axis=0), result[:, c, :], None,
                                                    bounds_check=NT * P - 1, oob_is_err=False).then_inc(result_stored[c], 16)
                    for c in range(RING):
                        pool.wait_ge(result_stored[c], 16 * ITERS)

                @block.tensor
                def _(pe):
                    def turn(i, c, first=False):
                        pe.wait_ge(slots_normed, i * RING + c + 1)
                        if not (first and c < 2):
                            pe.wait_ge(slots_t_made, i * RING + c - 1)
                        for k in range(KC):
                            ins = pe.transpose(banks[:, c % 2, k * P:(k + 1) * P], slot_xf[:, c % 2, k * P:(k + 1) * P], ident[:, :])
                        ins.then_inc(slots_turned, 1)

                    def first_layer(i, c, first=False):
                        pe.wait_ge(slots_t_made, i * RING + c + 1)
                        if not (first and c < 2):
                            pe.wait_ge(hidden_t_made, i * RING + c - 1)
                        for k in range(KC):
                            ins = pe.matmul(banks[0:HID, 2 + c % 2, 0:P], weights[:, c, k * HID:(k + 1) * HID],
                                            slot_xt[:, c % 2, k * P:(k + 1) * P], start=(k == 0), stop=(k == KC - 1))
                        ins.then_inc(hidden_summed, 1)

                    def second_layer(i, c, first=False):
                        pe.wait_ge(hidden_t_made, i * RING + c + 1)
                        if not (first and c < 2):
                            pe.wait_ge(result_made, i * RING + c - 1)
                        pe.matmul(banks[:, 6 + c % 2, 0:D], hidden_t[:, c % 2, :], weights[0:HID + 1, c, KC * HID:KC * HID + D], start=True, stop=True).then_inc(result_summed, 1)

                    stages = (turn, first_layer, second_layer)

                    def tiles(i, first=False):
                        for c in range(RING):
                            for lag, stage in enumerate(stages):
                                if c >= lag:
                                    stage(i, c - lag, first)
                                elif not first:
                                    stage(i - 1, c - lag + RING)

                    pe.wait_ge(ones_row_made, 1)
                    tiles(0, first=True)
                    with pe.Fori(1, ITERS) as i:
                        tiles(i)
                    for c in range(RING, RING + len(stages) - 1):
                        for lag, stage in enumerate(stages):
                            if c - lag < RING:
                                stage(ITERS - 1, c - lag)

                @block.scalar
                def _(act):
                    def copies(i, c, first=False):
                        act.wait_ge(slots_turned, i * RING + c + 1)
                        if not (first and c < 2):
                            act.wait_ge(hidden_summed, i * RING + c - 1)
                        act.copy(slot_xt[:, c % 2, :], banks[:, c % 2, 0:D]).then_inc(slots_t_made, 1)

                    for c in range(RING):
                        copies(0, c, first=True)
                    with act.Fori(1, ITERS) as i:
                        for c in range(RING):
                            copies(i, c)

                @block.vector
                def _(dve):
                    dve.memset(hidden_t[HID:HID + 1, :, :], 1.0).then_inc(ones_row_made, 1)

                    def norm_slots(i, c, first=False):
                        dve.wait_ge(loaded[c], (i + 1) * 16 * LOADS)
                        if not (first and c < 2):
                            dve.wait_ge(slots_turned, i * RING + c - 1)
                        dve.tensor_scalar(slot_xf[:, c % 2, :], slot_rows[:, c, 0:D], slot_rows[:, c, MEAN:MEAN + 1],
                                          slot_rows[:, c, RSTD:RSTD + 1], ALU.subtract, ALU.mult).then_inc(slots_normed, 1)

                    def relu_hidden(i, c, first=False):
                        dve.wait_ge(hidden_summed, i * RING + c + 1)
                        if not (first and c < 2):
                            dve.wait_ge(result_summed, i * RING + c - 1)
                        dve.tensor_scalar(hidden_t[0:HID, c % 2, :], banks[0:HID, 2 + c % 2, 0:P], weights[0:HID, c, PACK - 1:PACK], 0.0,
                                          ALU.add, ALU.max).then_inc(hidden_t_made, 1)

                    def add_result(i, c, first=False):
                        dve.wait_ge(result_summed, i * RING + c + 1)
                        if not first:
                            dve.wait_ge(result_stored[c], i * 16)
                        dve.tensor_copy(node[:, c:c + 1], slot_rows[:, c, NODE:NODE + 1])
                        dve.scalar_tensor_tensor(out=result[:, c, :], in0=banks[:, 6 + c % 2, 0:D], scalar=0.0, in1=slot_rows[:, c, 0:D],
                                                 op0=ALU.max, op1=ALU.add).then_inc(result_made, 1)

                    stages = ((0, norm_slots), (2, relu_hidden), (3, add_result))

                    def tiles(i, first=False, second=False):
                        for c in range(RING):
                            for lag, stage in stages:
                                if c >= lag:
                                    stage(i, c - lag, first)
                                elif not first:
                                    stage(i - 1, c - lag + RING, first=second)
                    tiles(0, first=True)
                    tiles(1, second=True)
                    with dve.Fori(2, ITERS) as i:
                        tiles(i)
                    for c in range(RING, RING + 3):
                        for lag, stage in stages:
                            if c - lag < RING:
                                stage(ITERS - 1, c - lag)


def _layout(inputs):
    import numpy as np
    x = np.asarray(inputs["x"])
    a = {}
    a["x"] = np.concatenate([x, np.zeros((NT * P - N_NODES, D), x.dtype)])
    E = NS * SUPER_EDGES

    def edges(v, fill):
        v = np.asarray(v)
        pad = np.full((E - N_EDGES,) + v.shape[1:], fill, v.dtype)
        return np.concatenate([v, pad]).reshape((NS, GROUPS, QUADS, P) + v.shape[1:])

    src = edges(inputs["src"], 0)
    dst = edges(inputs["dst"], PAD_DST)
    attr = edges(inputs["edge_attr_64"], 0)
    a["src"] = np.ascontiguousarray(src.transpose(0, 3, 2, 1)).reshape(NS, P, TILES)
    a["dst"] = np.ascontiguousarray(dst.transpose(3, 0, 2, 1)).reshape(P, NS * TILES)
    at = attr.reshape(NS, GROUPS // 2, 2, QUADS, P, D_EDGE).transpose(2, 5, 0, 3, 1, 4)
    a["attr"] = np.ascontiguousarray(at).reshape(2 * D_EDGE, NS, TILES // 2 * P)
    a["base_group"] = np.ascontiguousarray(dst[:, :, 0, 0]).reshape(1, NS * GROUPS)
    a["base_row"] = np.ascontiguousarray(dst[:, :, 0, 0].T)
    a["w_gnn"] = inputs["L0_gnn_W"]
    a["b_gnn"] = np.asarray(inputs["L0_gnn_b"]).reshape(1, D)
    a["gamma"] = np.asarray(inputs["L0_gnn_gamma"]).reshape(1, D)
    a["beta"] = np.asarray(inputs["L0_gnn_beta"]).reshape(1, D)
    wqkv = np.asarray(inputs["L0_mix_Wqkv"])
    a["wq"] = wqkv[:INNER]
    a["wk_t"] = wqkv[INNER:2 * INNER].T
    a["wv_t"] = wqkv[2 * INNER:].T
    a["wout_t"] = np.asarray(inputs["L0_mix_Wout"]).T
    a["bout"] = np.asarray(inputs["L0_mix_bout"]).reshape(1, D)
    a["router_t"] = np.asarray(inputs["L0_ffn_router_w"]).T
    a["router_b"] = np.asarray(inputs["L0_ffn_router_b"]).reshape(1, EXPERTS)
    pack = np.zeros((EXPERTS, P, PACK), np.float32)
    pack[:, :, :KC * HID] = np.asarray(inputs["L0_ffn_W1"]).reshape(EXPERTS, KC, P, HID).transpose(0, 2, 1, 3).reshape(EXPERTS, P, KC * HID)
    pack[:, :HID, KC * HID:KC * HID + D] = np.asarray(inputs["L0_ffn_W2"])
    pack[:, HID, KC * HID:KC * HID + D] = np.asarray(inputs["L0_ffn_b2"])
    pack[:, :HID, PACK - 1] = np.asarray(inputs["L0_ffn_b1"])
    a["experts"] = pack
    return {k: np.ascontiguousarray(v) for k, v in a.items()}


def kernel(**inputs):
    import concourse.bacc as bacc
    from concourse.bass_utils import run_bass_kernel_spmd

    nc = bacc.Bacc("TRN2", target_bir_lowering=False, num_devices=1)
    arrays, args = {}, {}
    for name, a in _layout(inputs).items():
        arrays[f"in_{name}"] = a
        args[name] = nc.dram_tensor(f"in_{name}", a.shape, mybir.dt.from_np(a.dtype), kind="ExternalInput").ap()
    args["out"] = nc.dram_tensor("out_0", (NT * P, D), F32, kind="ExternalOutput").ap()
    program(nc, **args)
    r = run_bass_kernel_spmd(nc, [arrays], core_ids=[0])
    return r.results[0]["out_0"][:N_NODES]
```

```python
from contextlib import ExitStack

import numpy as np

import concourse.bass as bass
from concourse import mybir

ALU = mybir.AluOpType
ACT = mybir.ActivationFunctionType
AX = mybir.AxisListType
F32 = mybir.dt.float32
F32R = mybir.dt.float32r
I32 = mybir.dt.int32

P = 128
N_NODES = 6250
D = 256
KC = D // P
N_EDGES = 106250
D_EDGE = 64
BATCH = 7
NT = -(-N_NODES // P)
NB = NT // BATCH
assert NT == NB * BATCH
WINDOW = 32
GROUPS = P // WINDOW
QUADS = 3
TILES = GROUPS * QUADS
GROUP_EDGES = QUADS * P
SUPER_EDGES = GROUPS * GROUP_EDGES
NS = 2 * -(-N_EDGES // (2 * SUPER_EDGES))
NI = NS // 2
KV = 3
KV_ITERS = -(-NT // KV)
NKV = KV * KV_ITERS
CB = 3
CN = -(-NT // CB)
C_LAST = NT - CB * (CN - 1)
C_FIRST = NI + 1 - CN
HEADS = 8
DH = 64
INNER = HEADS * DH
PAIRS = INNER // P
EXPERTS = 32
HID = 64
MEAN, RSTD, NODE = D, D + 1, D + 2
ROW = D + 4
PACK = KC * HID + D + 1
SLOT_TILES = (NT * P + EXPERTS * (P - 1)) // P
PAD_DST = 1 << 20
NO_NODE = 1 << 20
LN_EPS = 1e-5
GNN_EPS = 1e-3
HEAD_EPS = LN_EPS


def program(nc, x, attr, src, dst, base_group, base_row, w_gnn, b_gnn, gamma, beta, wq, wk_t, wv_t,
            wout_t, bout, router_t, router_b, experts, out):
    with ExitStack() as ctx:
        def sb(name, shape, dt=F32):
            return ctx.enter_context(nc.sbuf_tensor(name, shape, dt))

        def sem(name):
            return ctx.enter_context(nc.semaphore(name))

        y_dram = nc.dram_tensor("y_dram", [NT * P, D], F32).ap()
        xt_dram = nc.dram_tensor("xt_dram", [NKV, P, D], F32).ap()
        sorted_in = nc.dram_tensor("sorted_in", [SLOT_TILES * P, ROW], F32).ap()
        x_tiles = x.rearrange("(t p) c -> p t c", p=P)
        xt_tiles = xt_dram.rearrange("t p c -> p t c")
        slot_tiles = sorted_in.rearrange("(t p) c -> p t c", p=P)
        y_tiles = y_dram.rearrange("(t p) c -> p t c", p=P)

        banks = ctx.enter_context(nc.psum_tensor("banks", [P, 8, 512], F32))

        acc = sb("acc", [P, NT + 1, D])
        ident = sb("ident", [P, P])
        iota = sb("iota", [P, D])
        eps = sb("eps", [P, 2])
        row = sb("row", [P, 1])
        tri = sb("tri", [P, P])
        ones = sb("ones", [P, P])
        w_edge = sb("w_edge", [P, D])
        bout_rows = sb("bout_rows", [P, D])
        gamma_rows = sb("gamma_rows", [P, D])
        beta_rows = sb("beta_rows", [P, D])
        rb_rows = sb("rb_rows", [P, EXPERTS])
        router = sb("router", [P, KC, EXPERTS])
        dst_i = sb("dst_i", [P, NS * TILES], I32)
        src_i = sb("src_i", [P, NS * TILES], I32)
        base_i = sb("base_i", [P, NS * GROUPS], I32)
        base_row_i = sb("base_row_i", [P, NS], I32)
        base_f = sb("base_f", [P, NS, GROUPS])
        block_i = sb("block_i", [P, NS], I32)
        block_f = sb("block_f", [P, NS])
        row_node = sb("row_node", [P, NS])
        rel = sb("rel", [P, NS, TILES])
        place = sb("place", [P, NS])
        missed = sb("missed", [P, NS, TILES])
        miss_sum = sb("miss_sum", [P, 2])
        miss_i = sb("miss_i", [P, 1], I32)

        node_i = sb("node_i", [P, NT], I32)
        tile_iota_i = sb("tile_iota_i", [P, SLOT_TILES], I32)
        node_rows = sb("node_rows", [P, NT, ROW])
        kv_space = node_rows.rearrange("p t c -> p (t c)")
        taken = 0

        def in_rows(shape):
            nonlocal taken
            begin, taken = taken, taken + int(np.prod(shape))
            assert taken <= NT * ROW
            names = "abc"[:len(shape)]
            flat = kv_space[:, begin:taken]
            return flat if len(shape) == 1 else flat.rearrange(
                f"p ({' '.join(names)}) -> p {' '.join(names)}", **dict(zip(names[1:], shape[1:])))

        wkv = in_rows([KC, 2 * INNER])
        kv = in_rows([KV, 2 * INNER])
        scaled_v = in_rows([KV, INNER])
        squares = in_rows([2 * INNER])
        kv_xt = in_rows([KV, D])
        wq_sb = in_rows([PAIRS, D])
        wo_sb = in_rows([PAIRS, D])
        dots_t = in_rows([PAIRS, P])
        dots_blocks = in_rows([PAIRS, P])
        dots_out = in_rows([PAIRS, D])
        window_work = squares[:, 0:NS * TILES].rearrange("p (s t) -> p s t", t=TILES)

        empty_row = sb("empty_row", [P, ROW])

        dve_tick = sem("dve_tick")
        pe_tick = sem("pe_tick")
        pool_tick = sem("pool_tick")
        consts_landed = sem("consts_landed")
        first_landed = sem("first_landed")
        src_landed = sem("src_landed")
        edges_landed = sem("edges_landed")
        consts_made = sem("consts_made")

        with ExitStack() as ctx_a:
            def sb_a(name, shape, dt=F32):
                return ctx_a.enter_context(nc.sbuf_tensor(name, shape, dt))

            x_all = node_rows[:, :, 0:D]
            w_node = sb_a("w_node", [P, KC, D])
            b_rows = sb_a("b_rows", [P, D])
            iota_i = sb_a("iota_i", [P, D], I32)
            row_i = sb_a("row_i", [P, 1], I32)
            stats = sb_a("stats", [P, BATCH, 6])
            moments = sb_a("moments", [P, BATCH, 2])
            rstd = sb_a("rstd", [P, BATCH])
            xn = sb_a("xn", [P, BATCH, D])
            xt = sb_a("xt", [P, BATCH, D])
            y = sb_a("y", [P, BATCH, D])
            zeros = sb_a("zeros", [P, D])
            x_landed = sem("x_landed")
            a_steps = sem("a_steps")
            xn_made = sem("xn_made")
            rstd_made = sem("rstd_made")
            rooted = sem("rooted")
            turned = sem("turned")
            xt_made = sem("xt_made")
            y_summed = sem("y_summed")
            y_made = sem("y_made")
            zeroed = sem("zeroed")
            acc_cleared = sem("acc_cleared")
            zeros_stored = sem("zeros_stored")
            pool_consts = sem("pool_consts")
            xt_stored = [sem(f"xt_stored{j}") for j in range(BATCH)]
            y_stored = [sem(f"y_stored{j}") for j in range(BATCH)]
            n_consts = 11

            with nc.Block() as block:
                @block.sync
                def _(sp):
                    def load_x(i):
                        sp.dma_start(x_all[:, bass.ds(i * BATCH, BATCH), :],
                                     x_tiles[:, bass.ds(i * BATCH, BATCH), :]).then_inc(x_landed, 16)

                    def store_turned(i):
                        for j in range(BATCH):
                            sp.wait_ge(xt_made, i * BATCH + j + 1)
                            sp.dma_start(xt_tiles[:, bass.ds(i * BATCH + j, 1), :], xt[:, j:j + 1, :]).then_inc(xt_stored[j], 16)

                    def store_y(i):
                        for j in range(BATCH):
                            sp.wait_ge(y_made, i * BATCH + j + 1)
                            sp.dma_start(y_tiles[:, bass.ds(i * BATCH + j, 1), :], y[:, j:j + 1, :]).then_inc(y_stored[j], 16)

                    sp.dma_start(w_node[:, :, :], w_gnn[0:D, :].rearrange("(k p) n -> p k n", p=P)).then_inc(first_landed, 16)
                    sp.dma_start(b_rows[:, :], b_gnn.to_broadcast([P, D])).then_inc(first_landed, 16)
                    load_x(0)
                    sp.wait_ge(x_landed, 16)
                    load_x(1)
                    store_turned(0)
                    with sp.Fori(1, NB - 1) as i:
                        sp.wait_ge(x_landed, i * 16 + 16)
                        load_x(i + 1)
                        store_y(i - 1)
                        store_turned(i)
                    store_y(NB - 2)
                    store_turned(NB - 1)
                    for h in range(2):
                        sp.dma_start(w_edge[h * D_EDGE:(h + 1) * D_EDGE, :], w_gnn[D:D + D_EDGE, :]).then_inc(consts_landed, 16)
                    sp.dma_start(gamma_rows[:, :], gamma.to_broadcast([P, D])).then_inc(consts_landed, 16)
                    sp.dma_start(beta_rows[:, :], beta.to_broadcast([P, D])).then_inc(consts_landed, 16)
                    sp.dma_start(rb_rows[:, :], router_b.to_broadcast([P, EXPERTS])).then_inc(consts_landed, 16)
                    sp.dma_start(router[:, :, :], router_t.rearrange("(k p) n -> p k n", p=P)).then_inc(consts_landed, 16)
                    sp.wait_ge(xn_made, NT)
                    sp.dma_start(bout_rows[:, :], bout.to_broadcast([P, D])).then_inc(consts_landed, 16)
                    sp.dma_start(wkv[:, :, 0:INNER], wv_t.rearrange("(k p) n -> p k n", p=P)).then_inc(consts_landed, 16)
                    sp.dma_start(wkv[:, :, INNER:2 * INNER], wk_t.rearrange("(k p) n -> p k n", p=P)).then_inc(consts_landed, 16)
                    sp.dma_start(wq_sb[:, :, :], wq.rearrange("(k p) n -> p k n", p=P)).then_inc(consts_landed, 16)
                    sp.dma_start(wo_sb[:, :, :], wout_t.rearrange("(k p) n -> p k n", p=P)).then_inc(consts_landed, 16)
                    sp.wait_ge(zeroed, 1)
                    for t in range(NT, NKV):
                        sp.dma_start(xt_dram[t], zeros[:, :]).then_inc(zeros_stored, 16)
                    store_y(NB - 1)
                    sp.wait_ge(zeros_stored, 16 * (NKV - NT))
                    sp.wait_ge(consts_landed, 16 * n_consts)
                    for j in range(BATCH):
                        sp.wait_ge(xt_stored[j], 16 * NB)
                        sp.wait_ge(y_stored[j], 16 * NB)

                @block.gpsimd
                def _(pool):
                    pool.dma_start(src_i[:, :], src).then_inc(src_landed, 16)
                    pool.dma_start(dst_i[:, :], dst).then_inc(edges_landed, 16)
                    pool.dma_start(base_i[:, :], base_group.to_broadcast([P, NS * GROUPS])).then_inc(edges_landed, 16)
                    for g in range(GROUPS):
                        pool.dma_start(base_row_i[g * WINDOW:(g + 1) * WINDOW, :],
                                       base_row[g:g + 1, :].to_broadcast([WINDOW, NS])).then_inc(edges_landed, 16)
                    pool.memset(ident[:, :], 0.0).then_inc(pool_consts, 1)
                    pool.memset(tri[:, :], 1.0).then_inc(pool_consts, 1)
                    pool.memset(ones[:, :], 1.0).then_inc(consts_made, 1)
                    pool.memset(zeros[:, :], 0.0).then_inc(zeroed, 1)
                    pool.memset(empty_row[:, :], 0.0).then_inc(zeroed, 1)
                    pool.wait_ge(zeroed, 2)
                    pool.memset(empty_row[:, NODE:NODE + 1], float(NO_NODE)).then_inc(zeroed, 1)
                    pool.iota(iota_i[:, :], [[1, D]], base=0, channel_multiplier=0).then_inc(consts_made, 1)
                    pool.iota(row_i[:, :], [[0, 1]], base=0, channel_multiplier=1).then_inc(consts_made, 1)
                    pool.memset(eps[:, 0:1], LN_EPS).then_inc(consts_made, 1)
                    pool.memset(eps[:, 1:2], GNN_EPS).then_inc(consts_made, 1)
                    pool.wait_ge(pool_consts, 2)
                    pool.affine_select(out=ident[:, :], in_=ident[:, :], compare_op=ALU.not_equal, fill=1.0, base=0,
                                       pattern=[[-1, P]], channel_multiplier=1).then_inc(consts_made, 1)
                    pool.affine_select(out=tri[:, :], in_=tri[:, :], compare_op=ALU.is_gt, fill=0.0, base=0,
                                       pattern=[[1, P]], channel_multiplier=-1).then_inc(consts_made, 1)
                    pool.iota(tile_iota_i[:, :], [[1, SLOT_TILES]], base=0, channel_multiplier=0).then_inc(acc_cleared, 1)
                    pool.iota(node_i[:, :], [[P, NT]], base=0, channel_multiplier=1).then_inc(acc_cleared, 1)
                    pool.memset(acc[:, :, :], 0.0).then_inc(acc_cleared, 1)
                    pool.wait_ge(acc_cleared, 3)

                @block.vector
                def _(dve):
                    steps = 0

                    def link(ins):
                        nonlocal steps
                        steps += 1
                        ins.then_inc(a_steps, 1)
                        dve.wait_ge(a_steps, steps)

                    def norm(i, first=False):
                        dve.wait_ge(x_landed, i * 16 + 16)
                        for j in range(BATCH):
                            dve.bn_stats(stats[:, j, :], x_all[:, bass.ds(i * BATCH + j, 1), :]).then_inc(a_steps, 1)
                        dve.wait_ge(a_steps, i * 2 * BATCH + BATCH)
                        dve.sem_inc(dve_tick, 1)
                        for j in range(BATCH):
                            dve.bn_aggr(moments[:, j, :], stats[:, j, :]).then_inc(a_steps, 1)
                        dve.wait_ge(rooted, i + 1)
                        dve.reciprocal(rstd[:, :], rstd[:, :]).then_inc(rstd_made, 1)
                        dve.wait_ge(rstd_made, i + 1)
                        for j in range(BATCH):
                            if not first:
                                dve.wait_ge(turned, i * BATCH + j + 1 - BATCH)
                            dve.tensor_scalar(xn[:, j, :], x_all[:, bass.ds(i * BATCH + j, 1), :], moments[:, j, 0:1], rstd[:, j:j + 1],
                                              ALU.subtract, ALU.mult).then_inc(xn_made, 1)

                    def add_bias(i, first=False):
                        for j in range(BATCH):
                            dve.wait_ge(y_summed, i * BATCH + min(j | 1, BATCH - 1) + 1)
                            if not first:
                                dve.wait_ge(y_stored[j], i * 16)
                            dve.tensor_tensor(y[:, j, :], banks[:, 2 + j // 2, (j % 2) * D:(j % 2 + 1) * D],
                                              b_rows[:, :], ALU.add).then_inc(y_made, 1)

                    norm(0, first=True)
                    dve.wait_ge(first_landed, 16 * 2)
                    norm(1)
                    add_bias(0, first=True)
                    with dve.Fori(2, NB) as i:
                        norm(i)
                        add_bias(i - 1)
                    add_bias(NB - 1)

                    steps = NB * 2 * BATCH
                    link(dve.tensor_copy(iota[:, :], iota_i[:, :]))
                    link(dve.tensor_copy(row[:, :], row_i[:, :]))

                @block.scalar
                def _(act):
                    def copy_turned(i, first=False):
                        for j in range(BATCH):
                            act.wait_ge(turned, i * BATCH + j + 1)
                            if not first:
                                act.wait_ge(xt_stored[j], i * 16)
                                act.wait_ge(y_summed, i * BATCH + j + 1 - BATCH)
                            act.copy(xt[:, j, :], banks[:, j % 2, 0:D]).then_inc(xt_made, 1)

                    def root(i):
                        act.wait_ge(a_steps, (i + 1) * 2 * BATCH)
                        act.activation(rstd[:, :], moments[:, :, 1], ACT.Sqrt, bias=eps[:, 0:1]).then_inc(rooted, 1)
                    act.wait_ge(consts_made, 7)
                    root(0)
                    copy_turned(0, first=True)
                    with act.Fori(1, NB) as i:
                        act.wait_ge(xn_made, i * BATCH)
                        root(i)
                        copy_turned(i)

                @block.tensor
                def _(pe):
                    def turn(i, j, first=False):
                        pe.wait_ge(xn_made, i * BATCH + j + 1)
                        if not (first and j < 2):
                            pe.wait_ge(xt_made, i * BATCH + j - 1)
                        for k in range(KC):
                            ins = pe.transpose(banks[:, j % 2, k * P:(k + 1) * P], xn[:, j, k * P:(k + 1) * P], ident[:, :])
                        ins.then_inc(turned, 1)

                    def multiply(i, j, first=False):
                        pe.wait_ge(xt_made, i * BATCH + j + 1)
                        if not first:
                            pe.wait_ge(y_made, i * BATCH + min(j | 1, BATCH - 1) + 1 - BATCH)
                        for k in range(KC):
                            ins = pe.matmul(banks[:, 2 + j // 2, (j % 2) * D:(j % 2 + 1) * D], xt[:, j, k * P:(k + 1) * P],
                                            w_node[:, k, :], start=(k == 0), stop=(k == KC - 1))
                        ins.then_inc(y_summed, 1)

                    def batch(i, first=False):
                        for j in range(BATCH + 1):
                            if j < BATCH:
                                turn(i, j, first)
                            if j >= 1:
                                multiply(i, j - 1, first)
                    pe.wait_ge(consts_made, 7)
                    pe.wait_ge(first_landed, 16 * 2)
                    batch(0, first=True)
                    with pe.Fori(1, NB) as i:
                        batch(i)


        class Buffers:
            mix_xt = sb("mix_xt", [P, CB, D])
            x_rows = sb("x_rows", [P, CB, D])
            w_mix = sb("w_mix", [P, KC, D])
            stats = sb("c_stats", [P, CB, 6])
            moments = sb("c_moments", [P, CB, 2])
            rstd = sb("c_rstd", [P, CB])
            xf = sb("xf", [P, CB, D])
            xf_t = sb("xf_t", [P, CB, D])
            choice = sb("choice", [P, CB, EXPERTS])
            best = sb("best", [P, CB])
            counted = sb("counted", [P, EXPERTS], F32R)
            tri = sb("tri_count", [P, P], F32R)
            ones = sb("ones_count", [P, P], F32R)
            bias = sb("bias", [2 * WINDOW, D], F32R)
            bias_rows = sb("bias_rows", [2 * WINDOW, P], F32R)
            bias_row = sb("bias_row", [2 * WINDOW, 2])
            batch_count = sb("batch_count", [P, EXPERTS])
            own_rank = sb("own_rank", [P, CB, EXPERTS])

        c_buf = Buffers()
        onehot = sb("onehot", [P, NT, EXPERTS], F32R)
        rank = sb("rank", [P, NT])
        reversed_iota = sb("reversed_iota", [P, EXPERTS])

        class Semaphores:
            def __init__(self, tag):
                self.nodes_landed = sem(f"nodes_landed_{tag}")
                self.mix_summed = sem(f"mix_summed_{tag}")
                self.mix_read = sem(f"mix_read_{tag}")
                self.aggregated = sem(f"aggregated_{tag}")
                self.stats_made = sem(f"stats_made_{tag}")
                self.rooted = sem(f"rooted_{tag}")
                self.inverted = sem(f"inverted_{tag}")
                self.centred = sem(f"centred_{tag}")
                self.xf_made = sem(f"xf_made_{tag}")
                self.turned = sem(f"turned_{tag}")
                self.copied = sem(f"copied_{tag}")
                self.logits_summed = sem(f"logits_summed_{tag}")
                self.choosing = sem(f"choosing_{tag}")
                self.cleared = sem(f"cleared_{tag}")
                self.chosen = sem(f"chosen_{tag}")
                self.ranked = sem(f"ranked_{tag}")
                self.ranks_read = sem(f"ranks_read_{tag}")
                self.rank_kept = sem(f"rank_kept_{tag}")
                self.batch_counted = sem(f"batch_counted_{tag}")
                self.batch_added = sem(f"batch_added_{tag}")

        def parts_of(m):
            return [range(0, min(m, 2))] + ([range(2, m)] if m > 2 else [])

        def c_load(sp, S, n, m=CB, first=False):
            if not first:
                sp.wait_ge(S.mix_summed, n * 2)
            tiles = bass.ds(n * CB, m)
            sp.dma_start(c_buf.mix_xt[:, 0:m, :], xt_tiles[:, tiles, :]).then_inc(S.nodes_landed, 16)
            sp.dma_start(c_buf.x_rows[:, 0:m, :], x_tiles[:, tiles, :]).then_inc(S.nodes_landed, 16)

        def c_mix(pe, S, n, part, m=CB, first=False):
            if part == 0:
                pe.wait_ge(S.nodes_landed, n * 32 + 32)
            if not (first and part == 0):
                pe.wait_ge(*((S.copied, n * 2) if part == 0 else (S.mix_read, n * 2 + 1)))
            for j in parts_of(m)[part]:
                out_j = banks[:, 6, (j % 2) * D:(j % 2 + 1) * D]
                pe.matmul(out_j, c_buf.bias_rows[:, :], c_buf.bias[:, :], start=True, stop=False)
                pe.matmul(out_j, ident[:, :], c_buf.x_rows[:, j, :], start=False, stop=False)
                for k in range(KC):
                    ins = pe.matmul(out_j, c_buf.mix_xt[:, j, k * P:(k + 1) * P], c_buf.w_mix[:, k, :],
                                    start=False, stop=(k == KC - 1))
            ins.then_inc(S.mix_summed, 1)

        def c_turn(pe, S, n, part, m=CB):
            if part == 0:
                pe.wait_ge(S.xf_made, n + 1)
            else:
                pe.wait_ge(S.copied, n * 2 + 1)
            for j in parts_of(m)[part]:
                for k in range(KC):
                    ins = pe.transpose(banks[:, 6, (j % 2) * D + k * P:(j % 2) * D + (k + 1) * P],
                                       c_buf.xf[:, j, k * P:(k + 1) * P], ident[:, :])
            ins.then_inc(S.turned, 1)

        def c_logits(pe, S, n, m=CB, first=False):
            pe.wait_ge(S.copied, n * 2 + len(parts_of(m)))
            if not first:
                pe.wait_ge(S.ranks_read, n)
            pe.matmul(banks[:, 7, 0:m * EXPERTS], ones[0:1, :], rb_rows[0:1, None, :].to_broadcast([1, m, EXPERTS]), start=True, stop=True)
            for j in range(m):
                for k in range(KC):
                    ins = pe.matmul(banks[:, 7, j * EXPERTS:(j + 1) * EXPERTS], c_buf.xf_t[:, j, k * P:(k + 1) * P], router[:, k, :],
                                    start=False, stop=True, skip_group_check=True)
            ins.then_inc(S.logits_summed, 1)

        def c_count(pe, S, n, m=CB, first=False):
            pe.wait_ge(S.chosen, n + 1)
            if first:
                pe.wait_ge(S.cleared, 1)
            else:
                pe.wait_ge(S.batch_added, n)
            pe.matmul(banks[:, 7, 0:m * EXPERTS], c_buf.ones[:, :], c_buf.counted[:, None, :].to_broadcast([P, m, EXPERTS]), start=True, stop=True)
            for before in range(m - 1):
                pe.matmul(banks[:, 7, (before + 1) * EXPERTS:m * EXPERTS], c_buf.ones[:, :],
                          onehot[:, bass.ds(n * CB + before, 1), :].to_broadcast([P, m - 1 - before, EXPERTS]), start=False, stop=True,
                          skip_group_check=True)
            ins = pe.matmul(banks[:, 7, 0:m * EXPERTS], c_buf.tri[:, :], onehot[:, bass.ds(n * CB, m), :], start=False, stop=True,
                            skip_group_check=True)
            ins.then_inc(S.ranked, 1)

        def c_root(act, S, n, which, m=CB):
            act.wait_ge(S.aggregated, n * 2 + which + 1)
            act.activation(c_buf.rstd[:, 0:m], c_buf.moments[:, 0:m, 1], ACT.Sqrt,
                           bias=eps[:, 1 - which:2 - which]).then_inc(S.rooted, 1)

        def c_copy(act, S, n, part, m=CB, first=False):
            if part == 0 and not first:
                act.wait_ge(S.logits_summed, n)
            act.wait_ge(S.turned, n * 2 + part + 1)
            tiles = parts_of(m)[part]
            act.copy(c_buf.xf_t[:, tiles.start:tiles.stop, :],
                     banks[:, 6, 0:len(tiles) * D].rearrange("p (j d) -> p j d", d=D)).then_inc(S.copied, 1)

        def c_rows(n, m=CB):
            return node_rows[:, bass.ds(n * CB, m), :]

        def c_moments(dve, S, n, which, m=CB, first=False):
            dve.sem_inc(dve_tick, 1)
            for j in range(m):
                source = node_rows[:, bass.ds(n * CB + j, 1), 0:D] if which else acc[:, bass.ds(n * CB + j, 1), :]
                ins = dve.bn_stats(c_buf.stats[:, j, :], source)
            ins.then_inc(S.stats_made, 1)
            dve.wait_ge(S.stats_made, n * 2 + which + 1)
            if which == 0 and not first:
                dve.wait_ge(S.xf_made, n)
            dve.sem_inc(dve_tick, 1)
            for j in range(m):
                ins = dve.bn_aggr(c_buf.moments[:, j, :], c_buf.stats[:, j, :])
            ins.then_inc(S.aggregated, 1)

        def c_invert(dve, S, n, which, m=CB):
            dve.wait_ge(S.rooted, n * 2 + which + 1)
            dve.reciprocal(c_buf.rstd[:, 0:m], c_buf.rstd[:, 0:m]).then_inc(S.inverted, 1)
            dve.wait_ge(S.inverted, n * 2 + which + 1)

        def c_centre(dve, S, n, m=CB):
            c_invert(dve, S, n, 0, m)
            for j in range(m):
                ins = dve.scalar_tensor_tensor(out=node_rows[:, bass.ds(n * CB + j, 1), 0:D], in0=acc[:, bass.ds(n * CB + j, 1), :],
                                               scalar=c_buf.moments[:, j, 0:1], in1=gamma_rows[:, None, :],
                                               op0=ALU.subtract, op1=ALU.mult)
            ins.then_inc(S.centred, 1)

        def c_sum(dve, S, n, part, m=CB):
            dve.wait_ge(S.centred, n + 1)
            dve.wait_ge(S.mix_summed, n * 2 + part + 1)
            for j in parts_of(m)[part]:
                tile = node_rows[:, bass.ds(n * CB + j, 1), 0:D]
                ins = dve.scalar_tensor_tensor(out=tile, in0=tile, scalar=c_buf.rstd[:, j:j + 1],
                                               in1=banks[:, 6:7, (j % 2) * D:(j % 2 + 1) * D], op0=ALU.mult, op1=ALU.add)
            ins.then_inc(S.mix_read, 1)
            if part == len(parts_of(m)) - 1:
                dve.wait_ge(S.mix_read, n * 2 + part + 1)

        def c_norm(dve, S, n, m=CB, first=False):
            c_invert(dve, S, n, 1, m)
            if not first:
                dve.wait_ge(S.turned, n * 2)
            dve.tensor_copy(c_rows(n, m)[:, :, MEAN], c_buf.moments[:, 0:m, 0])
            dve.tensor_copy(c_rows(n, m)[:, :, RSTD], c_buf.rstd[:, 0:m])
            for j in range(m):
                ins = dve.tensor_scalar(c_buf.xf[:, j:j + 1, :], node_rows[:, bass.ds(n * CB + j, 1), 0:D],
                                        c_buf.moments[:, j, 0:1], c_buf.rstd[:, j:j + 1], ALU.subtract, ALU.mult)
            ins.then_inc(S.xf_made, 1)

        def c_choose(dve, S, n, m=CB, first=False):
            dve.wait_ge(S.logits_summed, n + 1)
            wide = [P, m, EXPERTS]
            logits = banks[:, 7, 0:m * EXPERTS].rearrange("p (j e) -> p j e", j=m)
            choice, best = c_buf.choice[:, 0:m, :], c_buf.best[:, 0:m]
            dve.tensor_reduce(best, logits, AX.X, ALU.max).then_inc(S.choosing, 1)
            dve.wait_ge(S.choosing, n * 3 + 1)
            for j in range(m):
                ins = dve.scalar_tensor_tensor(out=choice[:, j, :], in0=logits[:, j, :], scalar=best[:, j:j + 1], in1=reversed_iota[:, :],
                                               op0=ALU.is_ge, op1=ALU.mult)
            ins.then_inc(S.choosing, 1)
            dve.wait_ge(S.choosing, n * 3 + 2)
            dve.tensor_reduce(best, choice, AX.X, ALU.max).then_inc(S.choosing, 1)
            dve.wait_ge(S.choosing, n * 3 + 3)
            dve.tensor_tensor(onehot[:, bass.ds(n * CB, m), :], choice, best[:, :, None].to_broadcast(wide), ALU.is_equal).then_inc(S.chosen, 1)
            if first:
                dve.tensor_scalar(c_buf.counted[:, :], reversed_iota[:, :], 0.0, None, ALU.mult).then_inc(S.cleared, 1)

        def c_ranks(dve, S, n, m=CB):
            dve.wait_ge(S.ranked, n + 1)
            dve.wait_ge(S.chosen, n + 1)
            chosen = onehot[:, bass.ds(n * CB, m), :]
            dve.tensor_tensor(c_buf.own_rank[:, 0:m, :], banks[:, 7, 0:m * EXPERTS].rearrange("p (j e) -> p j e", j=m),
                              chosen, ALU.mult).then_inc(S.ranks_read, 1)
            dve.tensor_reduce(c_buf.batch_count[:, :], chosen.rearrange("p j e -> p e j"), AX.X, ALU.add).then_inc(S.batch_counted, 1)
            dve.wait_ge(S.ranks_read, n + 1)
            dve.tensor_reduce(rank[:, bass.ds(n * CB, m)], c_buf.own_rank[:, 0:m, :], AX.X, ALU.add).then_inc(S.rank_kept, 1)
            dve.wait_ge(S.batch_counted, n + 1)
            dve.tensor_tensor(c_buf.counted[:, :], c_buf.counted[:, :], c_buf.batch_count[:, :], ALU.add).then_inc(S.batch_added, 1)

        def c_pe(pe, S, n, m=CB, first=False):
            for part in range(len(parts_of(m))):
                c_mix(pe, S, n, part, m, first)
            for part in range(len(parts_of(m))):
                c_turn(pe, S, n, part, m)
            c_logits(pe, S, n, m, first)
            c_count(pe, S, n, m, first)

        def c_act(act, S, n, m=CB, first=False):
            c_root(act, S, n, 0, m)
            c_root(act, S, n, 1, m)
            for part in range(len(parts_of(m))):
                c_copy(act, S, n, part, m, first)

        def c_dve(dve, S, n, m=CB, first=False):
            c_moments(dve, S, n, 0, m, first)
            c_centre(dve, S, n, m)
            for part in range(len(parts_of(m))):
                c_sum(dve, S, n, part, m)
            c_moments(dve, S, n, 1, m)
            c_norm(dve, S, n, m, first)
            c_choose(dve, S, n, m, first)
            c_ranks(dve, S, n, m)

        with ExitStack() as ctx_b:
            def sb_b(name, shape, dt=F32):
                return ctx_b.enter_context(nc.sbuf_tensor(name, shape, dt))

            gather_index = sb_b("gather_index", [P, 2 * TILES], I32)
            attr_sb = sb_b("attr_sb", [D_EDGE, 2, TILES * P])
            attr_split = sb_b("attr_split", [P, 2, TILES * P], F32R)
            w_edge_split = sb_b("w_edge_split", [P, 2, D], F32R)
            msg = sb_b("msg", [P, 2 * QUADS, GROUPS, D])
            mask = sb_b("mask", [P, 2, TILES, WINDOW])
            place_mask = sb_b("place_mask", [P, 2, 2 * P])
            window = sb_b("window", [P, 2, D])
            head_var = sb_b("head_var", [P, KV, 2 * HEADS])
            kv_scale = sb_b("kv_scale", [P, KV, HEADS])
            wkv_mean = sb_b("wkv_mean", [P, KC * 2 * HEADS])

            b_steps = sem("b_steps")
            index_made = sem("index_made")
            attr_landed = [sem(f"attr_landed{h}") for h in range(2)]
            high_made = sem("high_made")
            low_made = sem("low_made")
            w_split_made = sem("w_split_made")
            kv_xt_landed = [sem(f"kv_xt_landed{which}") for which in range(2)]
            gathered = [sem(f"gathered{c}") for c in range(2 * QUADS)]
            edge_summed = sem("edge_summed")
            msg_added = sem("msg_added")
            silu_done = sem("silu_done")
            segments_summed = sem("segments_summed")
            mask_made = sem("mask_made")
            place_made = sem("place_made")
            window_copied = sem("window_copied")
            placed = sem("placed")
            acc_added = sem("acc_added")
            centred_weights = sem("centred_weights")
            kv_multiplied = sem("kv_multiplied")
            kv_copied = sem("kv_copied")
            squared = sem("squared")
            var_summed = sem("var_summed")
            heads_rooted = sem("heads_rooted")
            heads_inverted = sem("heads_inverted")
            scale_made = sem("scale_made")
            v_scaled = sem("v_scaled")
            dots_done = sem("dots_done")
            dots_masked = sem("dots_masked")
            dots_out_summed = sem("dots_out_summed")
            dots_out_copied = sem("dots_out_copied")
            w_mix_summed = sem("w_mix_summed")
            w_mix_made = sem("w_mix_made")
            c_ready = sem("c_ready")
            assert C_FIRST == KV_ITERS + 2
            miss_found = sem("miss_found")
            miss_known = sem("miss_known")
            NQ = 2 * QUADS
            assert NQ == 2 * KV
            S = Semaphores("b")
            slots_emptied = sem("slots_emptied")
            EMPTIED = SLOT_TILES // (KV_ITERS - 1)
            assert SLOT_TILES == EMPTIED * (KV_ITERS - 1)

            with nc.Block() as block:
                @block.sync
                def _(sp):
                    def load(i, h, first=False):
                        s = i * 2 + h
                        if not first:
                            sp.wait_ge(low_made, s - 1)
                        sp.dma_start(attr_sb[:, h:h + 1, :], attr[:, bass.ds(s, 1), :]).then_inc(attr_landed[h], 16)

                    def load_kv(i, first=False):
                        for which, (lo, hi) in enumerate(((0, KV - 1), (KV - 1, KV))):
                            if not first:
                                sp.wait_ge(kv_multiplied, i * 2 * KV - (2 * KV - 2 * hi))
                            sp.dma_start(kv_xt[:, lo:hi, :], xt_tiles[:, bass.ds(i * KV + lo, hi - lo), :]).then_inc(kv_xt_landed[which], 16)

                    def loads(i, kv_part=False, first=False):
                        load(i, 0, first)
                        load(i, 1, first)
                        if kv_part:
                            load_kv(i, first)

                    loads(0, True, first=True)
                    with sp.Fori(1, KV_ITERS) as i:
                        loads(i, True)
                        sp.dma_start(slot_tiles[:, bass.ds((i - 1) * EMPTIED, EMPTIED), :],
                                     empty_row[:, None, :].to_broadcast([P, EMPTIED, ROW])).then_inc(slots_emptied, 16)
                    with sp.Fori(KV_ITERS, C_FIRST + 1) as i:
                        loads(i)
                    load(C_FIRST + 1, 0)
                    c_load(sp, S, 0, first=True)
                    with sp.Fori(C_FIRST + 1, NI - 1) as i:
                        load(i, 1)
                        load(i + 1, 0)
                        c_load(sp, S, i - C_FIRST)
                    load(NI - 1, 1)
                    c_load(sp, S, NI - 1 - C_FIRST)
                    c_load(sp, S, CN - 1, C_LAST)
                    sp.wait_ge(slots_emptied, 16 * (KV_ITERS - 1))

                @block.gpsimd
                def _(pool):
                    def gather(i, h, first=False):
                        for k in range(QUADS):
                            c = h * QUADS + k
                            pool.wait_ge(index_made, i * NQ + c + 1)
                            if not first:
                                pool.wait_ge(segments_summed, i * NQ + c + 1 - NQ)
                            pool.sem_inc(pool_tick, 1)
                            for g in range(GROUPS):
                                t = k * GROUPS + g
                                pool.indirect_dma_start(
                                    msg[:, c, g, :], None, y_dram,
                                    bass.IndirectOffsetOnAxis(ap=gather_index[:, h * TILES + t:h * TILES + t + 1], axis=0),
                                    bounds_check=N_NODES - 1, oob_is_err=False).then_inc(gathered[c], 16)

                    for h in range(2):
                        gather(0, h, first=True)
                    with pool.Fori(1, NI) as i:
                        for h in range(2):
                            gather(i, h)

                @block.tensor
                def _(pe):
                    def edge_products(i, c, first=False):
                        h, k = divmod(c, QUADS)
                        if k == 0:
                            pe.wait_ge(low_made, i * 2 + h + 1)
                        if not (first and c < 2):
                            pe.wait_ge(msg_added, i * NQ + c - 1)
                        for g in range(GROUPS):
                            col = (k * GROUPS + g) * P
                            for part in range(2):
                                ins = pe.matmul(banks[:, (c % 2) * 2 + g // 2, (g % 2) * D:(g % 2 + 1) * D],
                                                attr_split[:, h, col:col + P], w_edge_split[:, part, :],
                                                start=(part == 0), stop=(part == 1))
                        ins.then_inc(edge_summed, 1)

                    def segment_sums(i, c, first=False):
                        h, k = divmod(c, QUADS)
                        pe.wait_ge(silu_done, i * NQ + c + 1)
                        if k == 0:
                            pe.wait_ge(mask_made, i * 2 + h + 1)
                            if not (first and h == 0):
                                pe.wait_ge(window_copied, i * 2 + h)
                        for g in range(GROUPS):
                            ins = pe.matmul(banks[g * WINDOW:(g + 1) * WINDOW, 4, 0:D], mask[:, h, k * GROUPS + g, :],
                                            msg[:, c, g, :], start=(k == 0), stop=(k == QUADS - 1))
                        ins.then_inc(segments_summed, 1)

                    def place_windows(i, h, first=False):
                        pe.wait_ge(window_copied, i * 2 + h + 1)
                        pe.wait_ge(place_made, i * 2 + h + 1)
                        if not (first and h == 0):
                            pe.wait_ge(acc_added, i * 2 + h)
                        for b in range(2):
                            ins = pe.matmul(banks[:, 5, b * D:(b + 1) * D], place_mask[:, h, b * P:(b + 1) * P],
                                            window[:, h, :], start=True, stop=True)
                        ins.then_inc(placed, 1)

                    def keys_values(i, r, part, first=False):
                        if part == 0 and r in (0, KV - 1):
                            pe.wait_ge(kv_xt_landed[r // (KV - 1)], i * 16 + 16)
                        if not (first and r == 0 and part == 0):
                            pe.wait_ge(kv_copied, (i * KV + r) * 2 + part)
                        for k in range(KC):
                            ins = pe.matmul(banks[:, 6, :], kv_xt[:, r, k * P:(k + 1) * P],
                                            wkv[:, k, part * INNER:(part + 1) * INNER], start=(k == 0), stop=(k == KC - 1))
                        ins.then_inc(kv_multiplied, 1)

                    def dots(i, r, first=False):
                        if r == 0:
                            pe.wait_ge(v_scaled, i + 1)
                        for q in range(PAIRS):
                            ins = pe.matmul(banks[:, 7, q * P:(q + 1) * P], scaled_v[:, r, q * P:(q + 1) * P],
                                            kv[:, r, INNER + q * P:INNER + (q + 1) * P], start=(first and r == 0 and q == 0), stop=True,
                                            skip_group_check=True)
                        ins.then_inc(dots_done, 1)

                    def mix_weights(c):
                        if c in (2, 3):
                            part = c - 2
                            pe.wait_ge(dots_masked, 1)
                            if part == 1:
                                pe.wait_ge(dots_out_copied, 1)
                            for q in range(2):
                                ins = pe.matmul(banks[:, 6, q * D:(q + 1) * D], dots_blocks[:, part * 2 + q, :], wo_sb[:, part * 2 + q, :],
                                                start=True, stop=True)
                            ins.then_inc(dots_out_summed, 1)
                        if c == 5:
                            pe.wait_ge(dots_out_copied, 2)
                            for k in range(KC):
                                for q in range(PAIRS):
                                    ins = pe.matmul(banks[:, 6, k * D:(k + 1) * D], wq_sb[:, q, k * P:(k + 1) * P], dots_out[:, q, :],
                                                    start=(q == 0), stop=(q == PAIRS - 1))
                            ins.then_inc(w_mix_summed, 1)

                    def supertiles(i, first=False, before=True, kv_part=False, kv_before=False, n=None, c_first=0,
                                   last=False, mixing=False):
                        for c in range(NQ):
                            h, k = divmod(c, QUADS)
                            if c < NQ - 1:
                                edge_products(i, c + 1, first)
                            elif not last:
                                edge_products(i + 1, 0)
                            if c >= 1:
                                segment_sums(i, c - 1, first)
                            elif before:
                                segment_sums(i - 1, NQ - 1)
                            if k == 1:
                                if h == 1:
                                    place_windows(i, 0, first)
                                elif before:
                                    place_windows(i - 1, 1)
                            if kv_before and c == 0:
                                keys_values(i - 1, KV - 1, 1)
                            if kv_before and 2 <= c < 2 + KV:
                                dots(i - 1, c - 2, first=(c_first == -1))
                            if kv_part and c >= 1:
                                keys_values(i, *divmod(c - 1, 2), first)
                            if mixing:
                                mix_weights(c)
                            if n is not None:
                                if c <= 1 and c_first != 1:
                                    c_turn(pe, S, n - 1, c)
                                if c == 2:
                                    if c_first != 1:
                                        c_logits(pe, S, n - 1, first=(c_first == 2))
                                    c_mix(pe, S, n, 0, first=(c_first == 1))
                                if c == 3:
                                    c_mix(pe, S, n, 1)
                                if c == 4 and c_first != 1:
                                    c_count(pe, S, n - 1, first=(c_first == 2))

                    pe.wait_ge(w_split_made, 2)
                    edge_products(0, 0, first=True)
                    pe.wait_ge(centred_weights, 1)
                    supertiles(0, first=True, before=False, kv_part=True)
                    supertiles(1, kv_part=True, kv_before=True, c_first=-1)
                    with pe.Fori(2, KV_ITERS) as i:
                        supertiles(i, kv_part=True, kv_before=True)
                    supertiles(KV_ITERS, kv_before=True)
                    supertiles(KV_ITERS + 1, mixing=True)
                    supertiles(KV_ITERS + 2)
                    pe.wait_ge(w_mix_made, 1)
                    pe.wait_ge(c_ready, 1)
                    supertiles(C_FIRST + 1, n=0, c_first=1)
                    supertiles(C_FIRST + 2, n=1, c_first=2)
                    with pe.Fori(C_FIRST + 3, NI - 1) as i:
                        supertiles(i, n=i - (C_FIRST + 1))
                    supertiles(NI - 1, n=NI - 1 - (C_FIRST + 1), last=True)
                    segment_sums(NI - 1, NQ - 1)
                    place_windows(NI - 1, 1)
                    n = NI - 1 - (C_FIRST + 1)
                    pe.wait_ge(acc_added, NS)
                    pe.matmul(banks[:, 5, 0:1], ones[:, :], miss_sum[:, 0:1], start=True, stop=True).then_inc(miss_found, 1)
                    for part in range(2):
                        c_turn(pe, S, n, part)
                    c_logits(pe, S, n)
                    c_count(pe, S, n)
                    c_pe(pe, S, n + 1)
                    c_pe(pe, S, n + 2, C_LAST)

                @block.vector
                def _(dve):
                    def copy_index(i, c):
                        dve.tensor_copy(gather_index[:, c * GROUPS:(c + 1) * GROUPS],
                                        src_i[:, bass.ds(i * 2 * TILES + c * GROUPS, GROUPS)]).then_inc(index_made, 1)

                    def add_products(i, c, last=False):
                        dve.wait_ge(edge_summed, i * NQ + c + 1)
                        dve.wait_ge(gathered[c], (i + 1) * 16 * GROUPS)
                        b = (c % 2) * 2
                        m = msg[:, c, :, :].rearrange("p (b g) d -> p b (g d)", b=2)
                        dve.tensor_tensor(m, m, banks[:, b:b + 2, :], ALU.add).then_inc(msg_added, 1)
                        if not last:
                            copy_index(i + 1, c)

                    def masks(i, h, first=False):
                        s = i * 2 + h
                        if not first:
                            dve.wait_ge(segments_summed, i * NQ + (h - 1) * QUADS)
                        dve.tensor_tensor(mask[:, h, :, :], iota[:, None, 0:WINDOW].to_broadcast([P, TILES, WINDOW]),
                                          rel[:, bass.ds(s, 1), :].rearrange("p s t -> p (s t)")[:, :, None].to_broadcast([P, TILES, WINDOW]),
                                          ALU.is_equal).then_inc(mask_made, 1)
                        if not first:
                            dve.wait_ge(placed, i * 2 + h - 1)
                        dve.tensor_scalar(place_mask[:, h, :], iota[:, :], place[:, bass.ds(s, 1)], None,
                                          ALU.is_equal).then_inc(place_made, 1)

                    def split_low(s, h):
                        dve.wait_ge(high_made, s + 1)
                        dve.tensor_tensor(attr_split[D_EDGE:P, h, :], attr_sb[:, h, :], attr_split[0:D_EDGE, h, :], ALU.subtract).then_inc(low_made, 1)

                    def add_blocks(i, h, first=False):
                        block = dve.value_load(block_i[0:1, bass.ds(i * 2 + h, 1)], min_val=0, max_val=NT - 1)
                        dve.wait_ge(placed, i * 2 + h + 1)
                        if not (first and h == 0):
                            dve.wait_ge(acc_added, i * 2 + h)
                        both = acc[:, bass.ds(block, 2), :]
                        dve.tensor_tensor(both, both, banks[:, 5, :].rearrange("p (b d) -> p b d", b=2), ALU.add).then_inc(acc_added, 1)

                    def head_variances(i, r, first=False):
                        dve.wait_ge(squared, i * KV + r + 1)
                        if r == 0 and not first:
                            dve.wait_ge(scale_made, i)
                        dve.tensor_reduce(head_var[:, r, :], squares.rearrange("p (g d) -> p g d", d=DH), AX.X, ALU.add).then_inc(var_summed, 1)

                    def scale_values(i, first=False):
                        dve.wait_ge(heads_rooted, i + 1)
                        dve.reciprocal(head_var[:, :, :], head_var[:, :, :]).then_inc(heads_inverted, 1)
                        dve.wait_ge(heads_inverted, i + 1)
                        if not first:
                            dve.wait_ge(v_scaled, i)
                        dve.tensor_tensor(kv_scale[:, :, :], head_var[:, :, 0:HEADS], head_var[:, :, HEADS:2 * HEADS], ALU.mult).then_inc(scale_made, 1)
                        dve.wait_ge(scale_made, i + 1)
                        if not first:
                            dve.wait_ge(dots_done, i * KV)
                        for r in range(KV):
                            ins = dve.tensor_tensor(scaled_v[:, r, :].rearrange("p (g d) -> p g d", d=DH),
                                                    kv[:, r, 0:INNER].rearrange("p (g d) -> p g d", d=DH),
                                                    kv_scale[:, r, :, None].to_broadcast([P, HEADS, DH]), ALU.mult)
                        ins.then_inc(v_scaled, 1)

                    def supertiles(i, first=False, before=True, kv_part=False, kv_before=False, n=None, c_first=0,
                                   last=False, mixing=False, missing=False):
                        for c in range(NQ):
                            h, k = divmod(c, QUADS)
                            if c == 0:
                                masks(i, 0, first)
                            add_products(i, c, last)
                            if c == 2:
                                masks(i, 1, first)
                            if mixing and c == 1:
                                mask_dots()
                            if missing:
                                find_missed(c)
                            if kv_before and c == 1:
                                head_variances(i - 1, 2, first=(c_first == -1))
                                scale_values(i - 1, first=(c_first == -1))
                            if c == 0:
                                split_low(i * 2 + 1, 1)
                            if c == 4 and not last:
                                split_low(i * 2 + 2, 0)
                            if k == 2:
                                if h == 1:
                                    add_blocks(i, 0, first)
                                elif before:
                                    add_blocks(i - 1, 1)
                            if kv_part and c in (3, 5):
                                head_variances(i, (c - 3) // 2, first)
                            if n is not None:
                                if c == 1:
                                    dve.wait_ge(acc_added, i * 2 - 1)
                                    c_moments(dve, S, n, 0, first=(c_first == 1))
                                if c == 2:
                                    c_centre(dve, S, n)
                                if c == 3:
                                    if c_first != 1:
                                        c_choose(dve, S, n - 1, first=(c_first == 2))
                                    c_sum(dve, S, n, 0)
                                if c == 4:
                                    c_sum(dve, S, n, 1)
                                    c_moments(dve, S, n, 1)
                                if c == 5:
                                    c_norm(dve, S, n, first=(c_first == 1))
                                    if c_first != 1:
                                        c_ranks(dve, S, n - 1)

                    steps = 0

                    def link(ins, done=1):
                        nonlocal steps
                        steps += done
                        ins.then_inc(b_steps, 1)
                        dve.wait_ge(b_steps, steps)

                    def mask_dots():
                        dve.wait_ge(dots_done, KV_ITERS * KV)
                        dve.memset(dots_blocks[:, :, :], 0.0).then_inc(b_steps, 1)
                        link(dve.tensor_copy(dots_t[:, :, :], banks[:, 7, :].rearrange("p (q d) -> p q d", q=PAIRS)), 2)
                        for h in range(2):
                            lanes = slice(h * DH, (h + 1) * DH)
                            ins = dve.tensor_copy(dots_blocks[lanes, :, lanes], dots_t[lanes, :, lanes])
                        ins.then_inc(dots_masked, 1)
                        link(dve.tensor_scalar(reversed_iota[:, :], iota[:, 0:EXPERTS], -1.0, float(EXPERTS), ALU.mult, ALU.add))
                        dve.tensor_copy(c_buf.tri[:, :], tri[:, :])
                        dve.tensor_copy(c_buf.ones[:, :], ones[:, :])
                        lanes = slice(0, 2 * WINDOW)
                        dve.tensor_scalar(c_buf.bias_row[:, 0:1], row[lanes, :], 0.0, None, ALU.is_equal)
                        link(dve.tensor_scalar(c_buf.bias_row[:, 1:2], row[lanes, :], float(WINDOW), None, ALU.is_equal))
                        link(dve.tensor_tensor(c_buf.bias_row[:, 0:1], c_buf.bias_row[:, 0:1], c_buf.bias_row[:, 1:2], ALU.add))
                        dve.tensor_scalar(c_buf.bias_rows[:, :], ones[lanes, :], c_buf.bias_row[:, 0:1], None, ALU.mult)
                        link(dve.tensor_tensor(beta_rows[lanes, :], beta_rows[lanes, :], bout_rows[lanes, :], ALU.add))
                        link(dve.tensor_copy(c_buf.bias[:, :], beta_rows[lanes, :]))
                        low = slice(WINDOW, 2 * WINDOW)
                        link(dve.tensor_tensor(c_buf.bias[low, :], beta_rows[low, :], c_buf.bias[low, :], ALU.subtract))

                    def find_missed(c):
                        dst_s = dst_i.rearrange("p (s t) -> p s t", t=TILES)
                        wide = [P, NS, TILES]
                        work = window_work
                        if c == 0:
                            link(dve.tensor_tensor(work, dst_s, block_f[:, :, None].to_broadcast(wide), ALU.subtract))
                            link(dve.tensor_scalar(missed[:, :, :], work, 0.0, None, ALU.is_ge))
                        if c in (1, 2, 3):
                            values, bound, op = ((work, float(2 * P), ALU.is_lt), (rel[:, :, :], 0.0, ALU.is_ge),
                                                 (rel[:, :, :], float(WINDOW), ALU.is_lt))[c - 1]
                            link(dve.scalar_tensor_tensor(out=missed[:, :, :], in0=values, scalar=bound, in1=missed[:, :, :],
                                                          op0=op, op1=ALU.mult))
                        if c == 3:
                            link(dve.tensor_scalar(missed[:, :, :], missed[:, :, :], -1.0, 1.0, ALU.mult, ALU.add))
                        if c == 4:
                            link(dve.scalar_tensor_tensor(out=missed[:, :, :], in0=dst_s, scalar=float(PAD_DST), in1=missed[:, :, :],
                                                          op0=ALU.is_lt, op1=ALU.mult))
                            link(dve.tensor_reduce(miss_sum[:, 0:1], missed[:, :, :].rearrange("p s t -> p (s t)"), AX.X, ALU.add))
                        if c == 5:
                            slope = float(P * CB // 2)
                            link(dve.tensor_scalar(block_f[:, :], iota[:, 0:NS], slope, slope * (1 - 2 * C_FIRST), ALU.mult, ALU.add))
                            link(dve.tensor_scalar(block_f[:, :], block_f[:, :], float(P * CB * (NI - 1 - C_FIRST)), None, ALU.min))
                            link(dve.tensor_tensor(work, dst_s, block_f[:, :, None].to_broadcast(wide), ALU.is_lt))
                            link(dve.tensor_reduce(miss_sum[:, 1:2], work.rearrange("p s t -> p (s t)"), AX.X, ALU.add))
                            link(dve.tensor_tensor(miss_sum[:, 0:1], miss_sum[:, 0:1], miss_sum[:, 1:2], ALU.add))

                    dve.wait_ge(src_landed, 16)
                    for c in range(NQ):
                        copy_index(0, c)
                    dve.tensor_copy(w_edge_split[:, 0, :], w_edge[:, :]).then_inc(w_split_made, 1)
                    dve.wait_ge(w_split_made, 1)
                    dve.tensor_tensor(w_edge_split[:, 1, :], w_edge[:, :], w_edge_split[:, 0, :], ALU.subtract).then_inc(w_split_made, 1)
                    dve.wait_ge(edges_landed, 16 * (2 + GROUPS))
                    split_low(0, 0)
                    link(dve.tensor_copy(base_f[:, :, :], base_i.rearrange("p (s g) -> p s g", g=GROUPS)))
                    link(dve.tensor_tensor(rel.rearrange("p s (k g) -> p s k g", g=GROUPS), dst_i.rearrange("p (s k g) -> p s k g", k=QUADS, g=GROUPS),
                                           base_f[:, :, None, :].to_broadcast([P, NS, QUADS, GROUPS]), ALU.subtract))
                    link(dve.tensor_scalar(block_i[:, :], base_i.rearrange("p (s g) -> p s g", g=GROUPS)[:, :, 0], 7, None,
                                           ALU.arith_shift_right))
                    link(dve.tensor_copy(block_f[:, :], block_i[:, :]))
                    link(dve.tensor_scalar(block_f[:, :], block_f[:, :], float(NT - 1), 0.0, ALU.min, ALU.max))
                    link(dve.tensor_copy(block_i[:, :], block_f[:, :]))
                    link(dve.tensor_scalar(block_f[:, :], block_f[:, :], float(P), None, ALU.mult))
                    link(dve.tensor_copy(row_node[:, :], base_row_i[:, :]))
                    for g in range(GROUPS):
                        lanes = slice(g * WINDOW, (g + 1) * WINDOW)
                        ins = dve.tensor_scalar(row_node[lanes, :], row_node[lanes, :], row[lanes, :], float(-g * WINDOW), ALU.add, ALU.add)
                    link(ins)
                    link(dve.tensor_tensor(place[:, :], row_node[:, :], block_f[:, :], ALU.subtract))
                    w_heads = wkv.rearrange("p k (h d) -> p (k h) d", d=DH)
                    link(dve.tensor_reduce(wkv_mean[:, :], w_heads, AX.X, ALU.add))
                    link(dve.tensor_scalar(wkv_mean[:, :], wkv_mean[:, :], 1.0 / DH, None, ALU.mult))
                    dve.tensor_tensor(w_heads, w_heads, wkv_mean[:, :, None].to_broadcast([P, KC * 2 * HEADS, DH]), ALU.subtract).then_inc(centred_weights, 1)

                    supertiles(0, first=True, before=False, kv_part=True)
                    supertiles(1, kv_part=True, kv_before=True, c_first=-1)
                    with dve.Fori(2, KV_ITERS) as i:
                        supertiles(i, kv_part=True, kv_before=True)
                    supertiles(KV_ITERS, kv_before=True)

                    supertiles(KV_ITERS + 1, mixing=True)
                    supertiles(KV_ITERS + 2, missing=True)
                    dve.wait_ge(w_mix_made, 1)
                    dve.tensor_copy(node_rows[:, :, NODE], node_i[:, :])
                    dve.memset(node_rows[:, :, NODE + 1:ROW], 0.0).then_inc(c_ready, 1)
                    dve.wait_ge(c_ready, 1)
                    supertiles(C_FIRST + 1, n=0, c_first=1)
                    supertiles(C_FIRST + 2, n=1, c_first=2)
                    with dve.Fori(C_FIRST + 3, NI - 1) as i:
                        supertiles(i, n=i - (C_FIRST + 1))
                    n = NI - 1 - (C_FIRST + 1)
                    supertiles(NI - 1, n=n, last=True)
                    add_blocks(NI - 1, 1)
                    dve.wait_ge(acc_added, NS)
                    dve.wait_ge(miss_found, 1)
                    dve.tensor_scalar(miss_i[:, :], banks[:, 5, 0:1], 1.0, None, ALU.min).then_inc(miss_known, 1)
                    c_choose(dve, S, n)
                    c_ranks(dve, S, n)
                    c_dve(dve, S, n + 1)
                    c_dve(dve, S, n + 2, C_LAST)

                @block.scalar
                def _(act):
                    def silu(i, c):
                        act.wait_ge(msg_added, i * NQ + c + 1)
                        act.activation(msg[:, c, :, :], msg[:, c, :, :], ACT.Silu).then_inc(silu_done, 1)

                    def split_high(i, h, first=False):
                        act.wait_ge(attr_landed[h], i * 16 + 16)
                        if not first:
                            act.wait_ge(edge_summed, i * NQ + (h - 1) * QUADS)
                        act.copy(attr_split[0:D_EDGE, h, :], attr_sb[:, h, :]).then_inc(high_made, 1)

                    def copy_window(i, h, first=False):
                        act.wait_ge(segments_summed, i * NQ + (h + 1) * QUADS)
                        if not first:
                            act.wait_ge(placed, i * 2 + h - 1)
                        act.copy(window[:, h, :], banks[:, 4, 0:D]).then_inc(window_copied, 1)

                    def copy_kv(i, r, part, first=False):
                        act.wait_ge(kv_multiplied, (i * KV + r) * 2 + part + 1)
                        if not first:
                            act.wait_ge(*((v_scaled, i) if part == 0 else (dots_done, i * KV + r + 1 - KV)))
                        act.copy(kv[:, r, part * INNER:(part + 1) * INNER], banks[:, 6, :]).then_inc(kv_copied, 1)
                        if part == 1:
                            square(i, r, first)

                    def square(i, r, first=False):
                        act.wait_ge(kv_copied, (i * KV + r + 1) * 2)
                        if not (first and r == 0):
                            act.wait_ge(var_summed, i * KV + r)
                        act.activation(squares[:, :], kv[:, r, :], ACT.Square).then_inc(squared, 1)

                    def root(i):
                        act.wait_ge(var_summed, (i + 1) * KV)
                        act.activation(head_var[:, :, :], head_var[:, :, :], ACT.Sqrt, bias=eps[:, 0:1], scale=1.0 / DH).then_inc(heads_rooted, 1)

                    def supertiles(i, first=False, before=True, kv_part=False, kv_before=False, n=None, c_first=0, last=False,
                                   mixing=False):
                        for c in range(NQ):
                            h, k = divmod(c, QUADS)
                            if kv_before and c <= 1:
                                copy_kv(i - 1, KV - 1, c, first=(c_first == -1))
                            if kv_part and c >= 2:
                                copy_kv(i, *divmod(c - 2, 2), first)
                            if mixing and c in (3, 4):
                                act.wait_ge(dots_out_summed, c - 2)
                                part = slice((c - 3) * 2, (c - 2) * 2)
                                act.copy(dots_out[:, part, :], banks[:, 6, :].rearrange("p (q d) -> p q d", q=2)).then_inc(dots_out_copied, 1)
                            silu(i, c)
                            if kv_before and c == 1:
                                root(i - 1)
                            if c == 3 and not last:
                                split_high(i + 1, 0)
                            if c == 5 and not last:
                                split_high(i + 1, 1)
                            if k == 0:
                                if h == 1:
                                    copy_window(i, 0, first)
                                elif before:
                                    copy_window(i - 1, 1, first=(c_first == -1))
                            if n is not None:
                                if c <= 1 and c_first != 1:
                                    c_copy(act, S, n - 1, c, first=(c_first == 2))
                                if c == 1:
                                    c_root(act, S, n, 0)
                                if c == 4:
                                    c_root(act, S, n, 1)

                    for h in range(2):
                        split_high(0, h, first=True)
                    supertiles(0, first=True, before=False, kv_part=True)
                    supertiles(1, kv_part=True, kv_before=True, c_first=-1)
                    with act.Fori(2, KV_ITERS) as i:
                        supertiles(i, kv_part=True, kv_before=True)
                    supertiles(KV_ITERS, kv_before=True)
                    supertiles(KV_ITERS + 1, mixing=True)
                    act.wait_ge(w_mix_summed, 1)
                    act.mul(c_buf.w_mix[:, :, :], banks[:, 6, :].rearrange("p (k d) -> p k d", k=KC), 1.0 / N_NODES).then_inc(w_mix_made, 1)
                    supertiles(KV_ITERS + 2)
                    supertiles(C_FIRST + 1, n=0, c_first=1)
                    supertiles(C_FIRST + 2, n=1, c_first=2)
                    with act.Fori(C_FIRST + 3, NI - 1) as i:
                        supertiles(i, n=i - (C_FIRST + 1))
                    n = NI - 1 - (C_FIRST + 1)
                    supertiles(NI - 1, n=n, last=True)
                    copy_window(NI - 1, 1)
                    for part in range(2):
                        c_copy(act, S, n, part)
                    c_act(act, S, n + 1)
                    c_act(act, S, n + 2, C_LAST)

        with ExitStack() as ctx_g:
            def sb_g(name, shape, dt=F32):
                return ctx_g.enter_context(nc.sbuf_tensor(name, shape, dt))

            any_missed = nc.values_load(miss_i[0:1, 0:1], min_val=0, max_val=1)
            index_g = sb_g("index_g", [P, 1], I32)
            attr_g = sb_g("attr_g", [D_EDGE, P])
            msg_g = sb_g("msg_g", [P, D])
            wanted = sb_g("wanted", [P, 1])
            mask_g = sb_g("mask_g", [P, P])
            edges_loaded_g = sem("edges_loaded_g")
            gathered_g = sem("gathered_g")
            product_g = sem("product_g")
            added_g = sem("added_g")
            silu_g = sem("silu_g")
            wanted_g = sem("wanted_g")
            mask_made_g = sem("mask_made_g")
            summed_g = sem("summed_g")
            acc_g = sem("acc_g")
            tile_done_g = sem("tile_done_g")
            sp_tick = sem("sp_tick")

            with nc.If(any_missed):
                with nc.Block() as block:
                    def each_tile(engine, body):
                        with engine.Fori(0, NS) as s:
                            with engine.Fori(0, TILES // 2) as pair:
                                for half in range(2):
                                    body(s, pair, half, (s * (TILES // 2) + pair) * 2 + half)

                    @block.sync
                    def _(sp):
                        def load(s, pair, half, u):
                            sp.wait_ge(tile_done_g, u + 1)
                            sp.sem_inc(sp_tick, 1)
                            with nc.allow_non_contiguous_dma(reason="one column of indices"):
                                sp.dma_start(index_g[:, :], src[:, bass.ds(u, 1)]).then_inc(edges_loaded_g, 16)
                            sp.dma_start(attr_g[:, :], attr[:, bass.ds(s, 1), bass.ds((pair * 2 + half) * P, P)].rearrange("p s e -> p (s e)")).then_inc(edges_loaded_g, 16)
                        sp.sem_inc(tile_done_g, 1)
                        each_tile(sp, load)

                    @block.gpsimd
                    def _(pool):
                        def gather(s, pair, half, u):
                            pool.wait_ge(edges_loaded_g, (u + 1) * 32)
                            pool.sem_inc(pool_tick, 1)
                            pool.indirect_dma_start(msg_g[:, :], None, y_dram, bass.IndirectOffsetOnAxis(ap=index_g[:, 0:1], axis=0),
                                                    bounds_check=N_NODES - 1, oob_is_err=False).then_inc(gathered_g, 16)
                        each_tile(pool, gather)

                    @block.tensor
                    def _(pe):
                        def products(s, pair, half, u):
                            pe.wait_ge(edges_loaded_g, (u + 1) * 32)
                            pe.matmul(banks[:, 0, 0:D], attr_g[:, :], w_edge[0:D_EDGE, :], start=True, stop=True).then_inc(product_g, 1)
                            pe.wait_ge(silu_g, u + 1)
                            pe.sem_inc(pe_tick, 1)
                            with pe.Fori(0, NT) as b:
                                v = u * NT + b
                                pe.wait_ge(mask_made_g, v + 1)
                                pe.matmul(banks[:, 1, 0:D], mask_g[:, :], msg_g[:, :], start=True, stop=True).then_inc(summed_g, 1)
                        each_tile(pe, products)

                    @block.scalar
                    def _(act):
                        def silu(s, pair, half, u):
                            act.wait_ge(added_g, u + 1)
                            act.activation(msg_g[:, :], msg_g[:, :], ACT.Silu).then_inc(silu_g, 1)
                        each_tile(act, silu)

                    @block.vector
                    def _(dve):
                        def add(s, pair, half, u):
                            dve.wait_ge(product_g, u + 1)
                            dve.wait_ge(gathered_g, (u + 1) * 16)
                            dve.tensor_tensor(msg_g[:, :], msg_g[:, :], banks[:, 0, 0:D], ALU.add).then_inc(added_g, 1)
                            dst_tile = dst_i.rearrange("p (s t) -> p s t", t=TILES)[:, bass.ds(s, 1), bass.ds(pair * 2 + half, 1)].rearrange("p s t -> p (s t)")
                            missed_tile = missed[:, bass.ds(s, 1), bass.ds(pair * 2 + half, 1)].rearrange("p s t -> p (s t)")
                            dve.scalar_tensor_tensor(out=wanted[:, :], in0=dst_tile, scalar=1.0, in1=missed_tile,
                                                     op0=ALU.add, op1=ALU.mult).then_inc(wanted_g, 1)
                            dve.wait_ge(wanted_g, u * (NT + 2) + 1)
                            dve.tensor_scalar(wanted[:, :], wanted[:, :], 1.0, None, ALU.subtract).then_inc(wanted_g, 1)
                            with dve.Fori(0, NT) as b:
                                v = u * NT + b
                                dve.wait_ge(wanted_g, u * (NT + 2) + b + 2)
                                dve.tensor_scalar(mask_g[:, :], iota[:, 0:P], wanted[:, :], None, ALU.is_equal).then_inc(mask_made_g, 1)
                                dve.wait_ge(mask_made_g, v + 1)
                                dve.tensor_scalar(wanted[:, :], wanted[:, :], float(P), None, ALU.subtract).then_inc(wanted_g, 1)
                                dve.wait_ge(summed_g, v + 1)
                                block_b = acc[:, bass.ds(b, 1), :]
                                dve.tensor_tensor(block_b, block_b, banks[:, 1:2, 0:D], ALU.add).then_inc(acc_g, 1)
                            dve.wait_ge(acc_g, (u + 1) * NT)
                            dve.sem_inc(tile_done_g, 1)
                        each_tile(dve, add)

                R = Semaphores("again")
                with nc.Block() as block:
                    @block.sync
                    def _(sp):
                        c_load(sp, R, 0, first=True)
                        with sp.Fori(1, CN - 1) as n:
                            c_load(sp, R, n)
                        c_load(sp, R, CN - 1, C_LAST)

                    @block.tensor
                    def _(pe):
                        c_pe(pe, R, 0, first=True)
                        with pe.Fori(1, CN - 1) as n:
                            c_pe(pe, R, n)
                        c_pe(pe, R, CN - 1, C_LAST)

                    @block.scalar
                    def _(act):
                        c_act(act, R, 0, first=True)
                        with act.Fori(1, CN - 1) as n:
                            c_act(act, R, n)
                        c_act(act, R, CN - 1, C_LAST)

                    @block.vector
                    def _(dve):
                        c_dve(dve, R, 0, first=True)
                        with dve.Fori(1, CN - 1) as n:
                            c_dve(dve, R, n)
                        c_dve(dve, R, CN - 1, C_LAST)

        slot_i = sb("slot_i", [P, NT], I32)
        tile_expert = sb("tile_expert", [P, SLOT_TILES], I32)
        with ExitStack() as ctx_s:
            def sb_s(name, shape, dt=F32):
                return ctx_s.enter_context(nc.sbuf_tensor(name, shape, dt))

            counts = sb_s("counts", [P, EXPERTS])
            counts_i = sb_s("counts_i", [P, EXPERTS], I32)
            ends = sb_s("ends", [P, 2, EXPERTS])
            tile_iota = sb_s("tile_iota", [P, SLOT_TILES])
            ended = sb_s("ended", [P, SLOT_TILES, EXPERTS])
            expert_f = sb_s("expert_f", [P, SLOT_TILES])
            slot_f = sb_s("slot_f", [P, NT])
            s_steps = sem("s_steps")
            counted = sem("counted")

            with nc.Block() as block:
                @block.tensor
                def _(pe):
                    pe.matmul(banks[:, 0, 0:EXPERTS], c_buf.ones[:, :], c_buf.counted[:, :], start=True, stop=True).then_inc(counted, 1)

                @block.vector
                def _(dve):
                    steps = 0

                    def link(ins):
                        nonlocal steps
                        steps += 1
                        ins.then_inc(s_steps, 1)
                        dve.wait_ge(s_steps, steps)

                    link(dve.tensor_copy(tile_iota[:, :], tile_iota_i[:, :]))
                    dve.wait_ge(counted, 1)
                    link(dve.tensor_scalar(counts[:, :], banks[:, 0, 0:EXPERTS], float(P - 1), None, ALU.add))
                    link(dve.tensor_copy(counts_i[:, :], counts[:, :]))
                    link(dve.tensor_scalar(counts_i[:, :], counts_i[:, :], 7, None, ALU.arith_shift_right))
                    link(dve.tensor_copy(counts[:, :], counts_i[:, :]))
                    link(dve.tensor_copy(ends[:, 0, :], counts[:, :]))
                    a, shift = 0, 1
                    while shift < EXPERTS:
                        link(dve.tensor_copy(ends[:, 1 - a, 0:shift], ends[:, a, 0:shift]))
                        link(dve.tensor_tensor(ends[:, 1 - a, shift:], ends[:, a, shift:], ends[:, a, :EXPERTS - shift], ALU.add))
                        a, shift = 1 - a, 2 * shift
                    wide = [P, SLOT_TILES, EXPERTS]
                    link(dve.tensor_tensor(ended[:, :, :], tile_iota[:, :, None].to_broadcast(wide), ends[:, a:a + 1, :].to_broadcast(wide), ALU.is_ge))
                    link(dve.tensor_reduce(expert_f[:, :], ended[:, :, :], AX.X, ALU.add))
                    link(dve.tensor_scalar(expert_f[:, :], expert_f[:, :], float(EXPERTS - 1), None, ALU.min))
                    link(dve.tensor_copy(tile_expert[:, :], expert_f[:, :]))
                    link(dve.tensor_tensor(ends[:, 1 - a, :], ends[:, a, :], counts[:, :], ALU.subtract))
                    link(dve.tensor_tensor(ended[:, 0:NT, :], onehot[:, :, :], ends[:, 1 - a:2 - a, :].to_broadcast([P, NT, EXPERTS]), ALU.mult))
                    link(dve.tensor_reduce(slot_f[:, :], ended[:, 0:NT, :], AX.X, ALU.add))
                    link(dve.scalar_tensor_tensor(out=slot_f[:, :], in0=slot_f[:, :], scalar=float(P), in1=rank[:, :], op0=ALU.mult, op1=ALU.add))
                    link(dve.tensor_copy(slot_i[:, :], slot_f[:, :]))

        RING = 8
        ITERS = SLOT_TILES // RING
        assert SLOT_TILES == ITERS * RING
        with ExitStack() as ctx_d:
            def sb_d(name, shape, dt=F32):
                return ctx_d.enter_context(nc.sbuf_tensor(name, shape, dt))

            slot_rows = sb_d("slot_rows", [P, RING, ROW])
            weights = sb_d("weights", [P, RING, PACK])
            node = sb_d("node", [P, RING], I32)
            slot_xf = sb_d("slot_xf", [P, 2, D])
            slot_xt = sb_d("slot_xt", [P, 2, D])
            hidden_t = sb_d("hidden_t", [HID + 1, 2, P])
            result = sb_d("result", [P, RING, D])

            scattered = sem("scattered")
            loaded = [sem(f"loaded{c}") for c in range(RING)]
            result_stored = [sem(f"result_stored{c}") for c in range(RING)]
            ones_row_made = sem("ones_row_made")
            slots_normed = sem("slots_normed")
            slots_turned = sem("slots_turned")
            slots_t_made = sem("slots_t_made")
            hidden_summed = sem("hidden_summed")
            hidden_t_made = sem("hidden_t_made")
            result_summed = sem("result_summed")
            result_made = sem("result_made")
            LOADS = 2

            with nc.Block() as block:
                @block.sync
                def _(sp):
                    def load(i, first=False):
                        for c in range(RING):
                            expert = sp.value_load(tile_expert[0:1, bass.ds(i * RING + c, 1)], min_val=0, max_val=EXPERTS - 1)
                            if not first:
                                sp.wait_ge(result_made, i * RING + c + 1 - RING)
                            sp.dma_start(weights[:, c, :], experts[bass.ds(expert, 1)].rearrange("e p n -> (e p) n")).then_inc(loaded[c], 16)
                            if first and c == 0:
                                sp.wait_ge(scattered, 16 * NT)
                            sp.dma_start(slot_rows[:, c:c + 1, :], slot_tiles[:, bass.ds(i * RING + c, 1), :]).then_inc(loaded[c], 16)
                    load(0, first=True)
                    with sp.Fori(1, ITERS) as i:
                        load(i)

                @block.gpsimd
                def _(pool):
                    for t in range(NT):
                        pool.indirect_dma_start(sorted_in, bass.IndirectOffsetOnAxis(ap=slot_i[:, t:t + 1], axis=0), node_rows[:, t, :], None,
                                                bounds_check=SLOT_TILES * P - 1, oob_is_err=False).then_inc(scattered, 16)
                    with pool.Fori(0, ITERS) as i:
                        for c in range(RING):
                            pool.wait_ge(result_made, i * RING + c + 1)
                            pool.sem_inc(pool_tick, 1)
                            pool.indirect_dma_start(out, bass.IndirectOffsetOnAxis(ap=node[:, c:c + 1], axis=0), result[:, c, :], None,
                                                    bounds_check=NT * P - 1, oob_is_err=False).then_inc(result_stored[c], 16)
                    for c in range(RING):
                        pool.wait_ge(result_stored[c], 16 * ITERS)

                @block.tensor
                def _(pe):
                    def turn(i, c, first=False):
                        pe.wait_ge(slots_normed, i * RING + c + 1)
                        if not (first and c < 2):
                            pe.wait_ge(slots_t_made, i * RING + c - 1)
                        for k in range(KC):
                            ins = pe.transpose(banks[:, c % 2, k * P:(k + 1) * P], slot_xf[:, c % 2, k * P:(k + 1) * P], ident[:, :])
                        ins.then_inc(slots_turned, 1)

                    def first_layer(i, c, first=False):
                        pe.wait_ge(slots_t_made, i * RING + c + 1)
                        if not (first and c < 2):
                            pe.wait_ge(hidden_t_made, i * RING + c - 1)
                        for k in range(KC):
                            ins = pe.matmul(banks[0:HID, 2 + c % 2, 0:P], weights[:, c, k * HID:(k + 1) * HID],
                                            slot_xt[:, c % 2, k * P:(k + 1) * P], start=(k == 0), stop=(k == KC - 1))
                        ins.then_inc(hidden_summed, 1)

                    def second_layer(i, c, first=False):
                        pe.wait_ge(hidden_t_made, i * RING + c + 1)
                        if not (first and c < 2):
                            pe.wait_ge(result_made, i * RING + c - 1)
                        pe.matmul(banks[:, 6 + c % 2, 0:D], hidden_t[:, c % 2, :], weights[0:HID + 1, c, KC * HID:KC * HID + D], start=True, stop=True).then_inc(result_summed, 1)

                    stages = (turn, first_layer, second_layer)

                    def tiles(i, first=False):
                        for c in range(RING):
                            for lag, stage in enumerate(stages):
                                if c >= lag:
                                    stage(i, c - lag, first)
                                elif not first:
                                    stage(i - 1, c - lag + RING)

                    pe.wait_ge(ones_row_made, 1)
                    tiles(0, first=True)
                    with pe.Fori(1, ITERS) as i:
                        tiles(i)
                    for c in range(RING, RING + len(stages) - 1):
                        for lag, stage in enumerate(stages):
                            if c - lag < RING:
                                stage(ITERS - 1, c - lag)

                @block.scalar
                def _(act):
                    def copies(i, c, first=False):
                        act.wait_ge(slots_turned, i * RING + c + 1)
                        if not (first and c < 2):
                            act.wait_ge(hidden_summed, i * RING + c - 1)
                        act.copy(slot_xt[:, c % 2, :], banks[:, c % 2, 0:D]).then_inc(slots_t_made, 1)

                    for c in range(RING):
                        copies(0, c, first=True)
                    with act.Fori(1, ITERS) as i:
                        for c in range(RING):
                            copies(i, c)

                @block.vector
                def _(dve):
                    dve.memset(hidden_t[HID:HID + 1, :, :], 1.0).then_inc(ones_row_made, 1)

                    def norm_slots(i, c, first=False):
                        dve.wait_ge(loaded[c], (i + 1) * 16 * LOADS)
                        if not (first and c < 2):
                            dve.wait_ge(slots_turned, i * RING + c - 1)
                        dve.tensor_scalar(slot_xf[:, c % 2, :], slot_rows[:, c, 0:D], slot_rows[:, c, MEAN:MEAN + 1],
                                          slot_rows[:, c, RSTD:RSTD + 1], ALU.subtract, ALU.mult).then_inc(slots_normed, 1)

                    def relu_hidden(i, c, first=False):
                        dve.wait_ge(hidden_summed, i * RING + c + 1)
                        if not (first and c < 2):
                            dve.wait_ge(result_summed, i * RING + c - 1)
                        dve.tensor_scalar(hidden_t[0:HID, c % 2, :], banks[0:HID, 2 + c % 2, 0:P], weights[0:HID, c, PACK - 1:PACK], 0.0,
                                          ALU.add, ALU.max).then_inc(hidden_t_made, 1)

                    def add_result(i, c, first=False):
                        dve.wait_ge(result_summed, i * RING + c + 1)
                        if not first:
                            dve.wait_ge(result_stored[c], i * 16)
                        dve.tensor_copy(node[:, c:c + 1], slot_rows[:, c, NODE:NODE + 1])
                        dve.scalar_tensor_tensor(out=result[:, c, :], in0=banks[:, 6 + c % 2, 0:D], scalar=0.0, in1=slot_rows[:, c, 0:D],
                                                 op0=ALU.max, op1=ALU.add).then_inc(result_made, 1)

                    stages = ((0, norm_slots), (2, relu_hidden), (3, add_result))

                    def tiles(i, first=False, second=False):
                        for c in range(RING):
                            for lag, stage in stages:
                                if c >= lag:
                                    stage(i, c - lag, first)
                                elif not first:
                                    stage(i - 1, c - lag + RING, first=second)
                    tiles(0, first=True)
                    tiles(1, second=True)
                    with dve.Fori(2, ITERS) as i:
                        tiles(i)
                    for c in range(RING, RING + 3):
                        for lag, stage in stages:
                            if c - lag < RING:
                                stage(ITERS - 1, c - lag)


def _layout(inputs):
    import numpy as np
    x = np.asarray(inputs["x"])
    a = {}
    a["x"] = np.concatenate([x, np.zeros((NT * P - N_NODES, D), x.dtype)])
    E = NS * SUPER_EDGES

    def edges(v, fill):
        v = np.asarray(v)
        pad = np.full((E - N_EDGES,) + v.shape[1:], fill, v.dtype)
        return np.concatenate([v, pad]).reshape((NS, GROUPS, QUADS, P) + v.shape[1:])

    src = edges(inputs["src"], 0)
    dst = edges(inputs["dst"], PAD_DST)
    attr = edges(inputs["edge_attr_64"], 0)
    a["src"] = np.ascontiguousarray(src.transpose(3, 0, 2, 1)).reshape(P, NS * TILES)
    a["dst"] = np.ascontiguousarray(dst.transpose(3, 0, 2, 1)).reshape(P, NS * TILES)
    a["attr"] = np.ascontiguousarray(attr.transpose(4, 0, 2, 1, 3)).reshape(D_EDGE, NS, TILES * P)
    a["base_group"] = np.ascontiguousarray(dst[:, :, 0, 0]).reshape(1, NS * GROUPS)
    a["base_row"] = np.ascontiguousarray(dst[:, :, 0, 0].T)
    a["w_gnn"] = inputs["L0_gnn_W"]
    a["b_gnn"] = np.asarray(inputs["L0_gnn_b"]).reshape(1, D)
    a["gamma"] = np.asarray(inputs["L0_gnn_gamma"]).reshape(1, D)
    a["beta"] = np.asarray(inputs["L0_gnn_beta"]).reshape(1, D)
    wqkv = np.asarray(inputs["L0_mix_Wqkv"])
    a["wq"] = wqkv[:INNER]
    a["wk_t"] = wqkv[INNER:2 * INNER].T
    a["wv_t"] = wqkv[2 * INNER:].T
    a["wout_t"] = np.asarray(inputs["L0_mix_Wout"]).T
    a["bout"] = np.asarray(inputs["L0_mix_bout"]).reshape(1, D)
    a["router_t"] = np.asarray(inputs["L0_ffn_router_w"]).T
    a["router_b"] = np.asarray(inputs["L0_ffn_router_b"]).reshape(1, EXPERTS)
    pack = np.zeros((EXPERTS, P, PACK), np.float32)
    pack[:, :, :KC * HID] = np.asarray(inputs["L0_ffn_W1"]).reshape(EXPERTS, KC, P, HID).transpose(0, 2, 1, 3).reshape(EXPERTS, P, KC * HID)
    pack[:, :HID, KC * HID:KC * HID + D] = np.asarray(inputs["L0_ffn_W2"])
    pack[:, HID, KC * HID:KC * HID + D] = np.asarray(inputs["L0_ffn_b2"])
    pack[:, :HID, PACK - 1] = np.asarray(inputs["L0_ffn_b1"])
    a["experts"] = pack
    return {k: np.ascontiguousarray(v) for k, v in a.items()}


def kernel(**inputs):
    import concourse.bacc as bacc
    from concourse.bass_utils import run_bass_kernel_spmd

    nc = bacc.Bacc("TRN2", target_bir_lowering=False, num_devices=1)
    arrays, args = {}, {}
    for name, a in _layout(inputs).items():
        arrays[f"in_{name}"] = a
        args[name] = nc.dram_tensor(f"in_{name}", a.shape, mybir.dt.from_np(a.dtype), kind="ExternalInput").ap()
    args["out"] = nc.dram_tensor("out_0", (NT * P, D), F32, kind="ExternalOutput").ap()
    program(nc, **args)
    r = run_bass_kernel_spmd(nc, [arrays], core_ids=[0])
    return r.results[0]["out_0"][:N_NODES]
```

```python
from contextlib import ExitStack

import numpy as np

import concourse.bass as bass
from concourse import mybir

ALU = mybir.AluOpType
ACT = mybir.ActivationFunctionType
AX = mybir.AxisListType
F32 = mybir.dt.float32
F32R = mybir.dt.float32r
I32 = mybir.dt.int32

P = 128
N_NODES = 6250
D = 256
KC = D // P
N_EDGES = 106250
D_EDGE = 64
BATCH = 7
NT = -(-N_NODES // P)
NB = NT // BATCH
assert NT == NB * BATCH
WINDOW = 32
GROUPS = P // WINDOW
QUADS = 3
TILES = GROUPS * QUADS
GROUP_EDGES = QUADS * P
SUPER_EDGES = GROUPS * GROUP_EDGES
NS = 2 * -(-N_EDGES // (2 * SUPER_EDGES))
NI = NS // 2
LAST_GROUPS = -(-(N_EDGES - (NS - 1) * SUPER_EDGES) // GROUP_EDGES)
assert 0 < LAST_GROUPS <= GROUPS
KV = 3
KV_ITERS = -(-NT // KV)
NKV = KV * KV_ITERS
CB = 3
CN = NT // CB
C_LAST = NT - CB * (CN - 1)
C_FIRST = NI - CN
HEADS = 8
DH = 64
INNER = HEADS * DH
PAIRS = INNER // P
EXPERTS = 32
HID = 64
MEAN, RSTD, NODE = D, D + 1, D + 2
ROW = D + 4
PACK = KC * HID + D + 1
SLOT_TILES = (NT * P + EXPERTS * (P - 1)) // P
PAD_DST = 1 << 20
NO_NODE = 1 << 20
LN_EPS = 1e-5
GNN_EPS = 1e-3
HEAD_EPS = LN_EPS


def program(nc, x, attr, src, dst, base_group, base_row, w_gnn, b_gnn, gamma, beta, wq, wk_t, wv_t,
            wout_t, bout, router_t, router_b, experts, out):
    with ExitStack() as ctx:
        def sb(name, shape, dt=F32):
            return ctx.enter_context(nc.sbuf_tensor(name, shape, dt))

        def sem(name):
            return ctx.enter_context(nc.semaphore(name))

        y_dram = nc.dram_tensor("y_dram", [NT * P, D], F32).ap()
        xt_dram = nc.dram_tensor("xt_dram", [NKV, P, D], F32).ap()
        sorted_in = nc.dram_tensor("sorted_in", [SLOT_TILES * P, ROW], F32).ap()
        x_tiles = x.rearrange("(t p) c -> p t c", p=P)
        xt_tiles = xt_dram.rearrange("t p c -> p t c")
        slot_tiles = sorted_in.rearrange("(t p) c -> p t c", p=P)
        y_tiles = y_dram.rearrange("(t p) c -> p t c", p=P)

        banks = ctx.enter_context(nc.psum_tensor("banks", [P, 8, 512], F32))

        acc = sb("acc", [P, NT + 1, D])
        ident = sb("ident", [P, P])
        iota = sb("iota", [P, D])
        eps = sb("eps", [P, 2])
        row = sb("row", [P, 1])
        tri = sb("tri", [P, P])
        ones = sb("ones", [P, P])
        gamma_rows = sb("gamma_rows", [P, D])
        rb_rows = sb("rb_rows", [P, EXPERTS])
        router = sb("router", [P, KC, EXPERTS])
        dst_i = sb("dst_i", [P, NS * TILES], I32)
        src_i = sb("src_i", [P, NS * TILES], I32)
        base_i = sb("base_i", [P, NS * GROUPS], I32)
        base_row_i = sb("base_row_i", [P, NS], I32)
        block_i = sb("block_i", [P, NS], I32)
        block_f = sb("block_f", [P, NS])
        row_node = sb("row_node", [P, NS])
        rel = sb("rel", [P, NS, TILES])
        place = sb("place", [P, NS])
        missed = sb("missed", [P, NS, TILES])
        miss_sum = sb("miss_sum", [P, 2])
        miss_i = sb("miss_i", [P, 1], I32)

        node_i = sb("node_i", [P, NT], I32)
        tile_iota_i = sb("tile_iota_i", [P, SLOT_TILES], I32)
        node_rows = sb("node_rows", [P, NT, ROW])
        kv_space = node_rows.rearrange("p t c -> p (t c)")
        taken = 0

        def in_rows(shape):
            nonlocal taken
            begin, taken = taken, taken + int(np.prod(shape))
            assert taken <= NT * ROW
            names = "abc"[:len(shape)]
            flat = kv_space[:, begin:taken]
            return flat if len(shape) == 1 else flat.rearrange(
                f"p ({' '.join(names)}) -> p {' '.join(names)}", **dict(zip(names[1:], shape[1:])))

        wkv = in_rows([KC, 2 * INNER])
        kv = in_rows([KV, 2 * INNER])
        scaled_v = in_rows([KV, INNER])
        squares = in_rows([2 * INNER])
        kv_xt = in_rows([KV, D])
        wq_sb = in_rows([PAIRS, D])
        wo_sb = in_rows([PAIRS, D])
        dots_t = in_rows([PAIRS, P])
        dots_blocks = in_rows([PAIRS, P])
        dots_out = squares.rearrange("p (q d) -> p q d", q=PAIRS)
        bout_rows = in_rows([D])
        beta_rows = in_rows([D])
        w_edge = in_rows([D])
        base_f = in_rows([NS, GROUPS])
        window_work = squares[:, 0:NS * TILES].rearrange("p (s t) -> p s t", t=TILES)

        empty_row = sb("empty_row", [P, ROW])

        dve_tick = sem("dve_tick")
        pe_tick = sem("pe_tick")
        pool_tick = sem("pool_tick")
        consts_landed = sem("consts_landed")
        first_landed = sem("first_landed")
        src_landed = sem("src_landed")
        edges_landed = sem("edges_landed")
        consts_made = sem("consts_made")

        xt_stored = [sem(f"xt_stored{part}") for part in range(2)]
        zeros_stored = sem("zeros_stored")
        N_CONSTS = 11
        PARTS = ((0, BATCH - BATCH // 2), (BATCH - BATCH // 2, BATCH))

        with ExitStack() as ctx_a:
            def sb_a(name, shape, dt=F32):
                return ctx_a.enter_context(nc.sbuf_tensor(name, shape, dt))

            x_all = node_rows[:, :, 0:D]
            w_node = sb_a("w_node", [P, KC, D])
            b_rows = sb_a("b_rows", [P, D])
            iota_i = sb_a("iota_i", [P, D], I32)
            row_i = sb_a("row_i", [P, 1], I32)
            stats = sb_a("stats", [P, BATCH, 6])
            moments = sb_a("moments", [P, BATCH, 2])
            rstd = sb_a("rstd", [P, BATCH])
            xn = sb_a("xn", [P, BATCH, D])
            xt = sb_a("xt", [P, BATCH, D])
            y = sb_a("y", [P, BATCH, D])
            zeros = sb_a("zeros", [P, D])
            x_landed = sem("x_landed")
            a_steps = sem("a_steps")
            xn_made = sem("xn_made")
            rstd_made = sem("rstd_made")
            rooted = sem("rooted")
            turned = sem("turned")
            xt_made = sem("xt_made")
            y_summed = sem("y_summed")
            y_made = sem("y_made")
            zeroed = sem("zeroed")
            acc_cleared = sem("acc_cleared")
            pool_consts = sem("pool_consts")
            y_stored = [sem(f"y_stored{part}") for part in range(len(PARTS))]

            with nc.Block() as block:
                @block.sync
                def _(sp):
                    def store_turned(i):
                        for part, (lo, hi) in enumerate(PARTS):
                            sp.wait_ge(xt_made, i * BATCH + hi)
                            sp.dma_start(xt_tiles[:, bass.ds(i * BATCH + lo, hi - lo), :], xt[:, lo:hi, :]).then_inc(xt_stored[part], 16)

                    def store_y(i):
                        for part, (lo, hi) in enumerate(PARTS):
                            sp.wait_ge(y_made, i * BATCH + hi)
                            sp.dma_start(y_tiles[:, bass.ds(i * BATCH + lo, hi - lo), :], y[:, lo:hi, :]).then_inc(y_stored[part], 16)

                    sp.dma_start(w_node[:, :, :], w_gnn[0:D, :].rearrange("(k p) n -> p k n", p=P)).then_inc(first_landed, 16)
                    sp.dma_start(b_rows[:, :], b_gnn.to_broadcast([P, D])).then_inc(first_landed, 16)
                    store_turned(0)
                    with sp.Fori(1, NB) as i:
                        store_y(i - 1)
                        store_turned(i)
                    sp.dma_start(gamma_rows[:, :], gamma.to_broadcast([P, D])).then_inc(consts_landed, 16)
                    sp.dma_start(rb_rows[:, :], router_b.to_broadcast([P, EXPERTS])).then_inc(consts_landed, 16)
                    sp.dma_start(router[:, :, :], router_t.rearrange("(k p) n -> p k n", p=P)).then_inc(consts_landed, 16)
                    store_y(NB - 1)
                    sp.wait_ge(xn_made, NT)
                    for h in range(2):
                        sp.dma_start(w_edge[h * D_EDGE:(h + 1) * D_EDGE, :], w_gnn[D:D + D_EDGE, :]).then_inc(consts_landed, 16)
                    sp.dma_start(beta_rows[:, :], beta.to_broadcast([P, D])).then_inc(consts_landed, 16)
                    sp.dma_start(bout_rows[:, :], bout.to_broadcast([P, D])).then_inc(consts_landed, 16)
                    sp.dma_start(wkv[:, :, 0:INNER], wv_t.rearrange("(k p) n -> p k n", p=P)).then_inc(consts_landed, 16)
                    sp.dma_start(wkv[:, :, INNER:2 * INNER], wk_t.rearrange("(k p) n -> p k n", p=P)).then_inc(consts_landed, 16)
                    sp.dma_start(wq_sb[:, :, :], wq.rearrange("(k p) n -> p k n", p=P)).then_inc(consts_landed, 16)
                    sp.dma_start(wo_sb[:, :, :], wout_t.rearrange("(k p) n -> p k n", p=P)).then_inc(consts_landed, 16)
                    sp.wait_ge(zeroed, 1)
                    for t in range(NT, NKV):
                        sp.dma_start(xt_dram[t], zeros[:, :]).then_inc(zeros_stored, 16)
                    for part in range(len(PARTS)):
                        sp.wait_ge(y_stored[part], 16 * NB)

                @block.gpsimd
                def _(pool):
                    def load_x(i):
                        pool.dma_start(x_all[:, i * BATCH:(i + 1) * BATCH, :], x_tiles[:, i * BATCH:(i + 1) * BATCH, :]).then_inc(x_landed, 16)

                    load_x(0)
                    pool.memset(ident[:, :], 0.0).then_inc(pool_consts, 1)
                    pool.memset(tri[:, :], 1.0).then_inc(pool_consts, 1)
                    pool.memset(ones[:, :], 1.0).then_inc(consts_made, 1)
                    pool.memset(zeros[:, :], 0.0).then_inc(zeroed, 1)
                    pool.memset(empty_row[:, :], 0.0).then_inc(zeroed, 1)
                    pool.wait_ge(zeroed, 2)
                    pool.memset(empty_row[:, NODE:NODE + 1], float(NO_NODE)).then_inc(zeroed, 1)
                    pool.iota(iota_i[:, :], [[1, D]], base=0, channel_multiplier=0).then_inc(consts_made, 1)
                    pool.iota(row_i[:, :], [[0, 1]], base=0, channel_multiplier=1).then_inc(consts_made, 1)
                    pool.memset(eps[:, 0:1], LN_EPS).then_inc(consts_made, 1)
                    pool.memset(eps[:, 1:2], GNN_EPS).then_inc(consts_made, 1)
                    pool.wait_ge(pool_consts, 2)
                    pool.affine_select(out=ident[:, :], in_=ident[:, :], compare_op=ALU.not_equal, fill=1.0, base=0,
                                       pattern=[[-1, P]], channel_multiplier=1).then_inc(consts_made, 1)
                    pool.affine_select(out=tri[:, :], in_=tri[:, :], compare_op=ALU.is_gt, fill=0.0, base=0,
                                       pattern=[[1, P]], channel_multiplier=-1).then_inc(consts_made, 1)
                    for i in range(1, NB):
                        pool.wait_ge(x_landed, i * 16)
                        load_x(i)
                    pool.dma_start(src_i[:, :], src).then_inc(src_landed, 16)
                    pool.dma_start(dst_i[:, :], dst).then_inc(edges_landed, 16)
                    pool.dma_start(base_i[:, :], base_group.to_broadcast([P, NS * GROUPS])).then_inc(edges_landed, 16)
                    for g in range(GROUPS):
                        pool.dma_start(base_row_i[g * WINDOW:(g + 1) * WINDOW, :],
                                       base_row[g:g + 1, :].to_broadcast([WINDOW, NS])).then_inc(edges_landed, 16)
                    pool.iota(tile_iota_i[:, :], [[1, SLOT_TILES]], base=0, channel_multiplier=0).then_inc(acc_cleared, 1)
                    pool.iota(node_i[:, :], [[P, NT]], base=0, channel_multiplier=1).then_inc(acc_cleared, 1)
                    pool.memset(acc[:, :, :], 0.0).then_inc(acc_cleared, 1)
                    pool.wait_ge(acc_cleared, 3)

                @block.vector
                def _(dve):
                    steps = 0

                    def link(ins):
                        nonlocal steps
                        steps += 1
                        ins.then_inc(a_steps, 1)
                        dve.wait_ge(a_steps, steps)

                    def measure(i):
                        dve.wait_ge(x_landed, i * 16 + 16)
                        for j in range(BATCH):
                            dve.bn_stats(stats[:, j, :], x_all[:, bass.ds(i * BATCH + j, 1), :]).then_inc(a_steps, 1)
                        dve.wait_ge(a_steps, i * 2 * BATCH + BATCH)
                        dve.sem_inc(dve_tick, 1)
                        for j in range(BATCH):
                            dve.bn_aggr(moments[:, j, :], stats[:, j, :]).then_inc(a_steps, 1)
                        dve.wait_ge(rooted, i + 1)
                        dve.reciprocal(rstd[:, :], rstd[:, :]).then_inc(rstd_made, 1)
                        dve.wait_ge(rstd_made, i + 1)

                    def normalize(i, j, first=False):
                        if not first:
                            dve.wait_ge(turned, i * BATCH + j + 1 - BATCH)
                        dve.tensor_scalar(xn[:, j, :], x_all[:, bass.ds(i * BATCH + j, 1), :], moments[:, j, 0:1], rstd[:, j:j + 1],
                                          ALU.subtract, ALU.mult).then_inc(xn_made, 1)

                    def add_bias(i, j, first=False):
                        dve.wait_ge(y_summed, i * BATCH + min(j | 1, BATCH - 1) + 1)
                        if not first and j in (0, PARTS[1][0]):
                            dve.wait_ge(y_stored[j // PARTS[1][0]], i * 16)
                        dve.tensor_tensor(y[:, j, :], banks[:, 2 + j // 2, (j % 2) * D:(j % 2 + 1) * D],
                                          b_rows[:, :], ALU.add).then_inc(y_made, 1)

                    def batch(i, second=False):
                        measure(i)
                        for j in range(BATCH):
                            normalize(i, j)
                            add_bias(i - 1, j, first=second)

                    measure(0)
                    for j in range(BATCH):
                        normalize(0, j, first=True)
                    dve.wait_ge(first_landed, 16 * 2)
                    batch(1, second=True)
                    with dve.Fori(2, NB) as i:
                        batch(i)
                    for j in range(BATCH):
                        add_bias(NB - 1, j)

                    steps = NB * 2 * BATCH
                    link(dve.tensor_copy(iota[:, :], iota_i[:, :]))
                    link(dve.tensor_copy(row[:, :], row_i[:, :]))

                @block.scalar
                def _(act):
                    def copy_turned(i, first=False):
                        for j in range(BATCH):
                            act.wait_ge(turned, i * BATCH + j + 1)
                            if not first:
                                act.wait_ge(xt_stored[j // PARTS[1][0]], i * 16)
                                act.wait_ge(y_summed, i * BATCH + j + 1 - BATCH)
                            act.copy(xt[:, j, :], banks[:, j % 2, 0:D]).then_inc(xt_made, 1)

                    def root(i):
                        act.wait_ge(a_steps, (i + 1) * 2 * BATCH)
                        act.activation(rstd[:, :], moments[:, :, 1], ACT.Sqrt, bias=eps[:, 0:1]).then_inc(rooted, 1)
                    act.wait_ge(consts_made, 7)
                    root(0)
                    copy_turned(0, first=True)
                    with act.Fori(1, NB) as i:
                        act.wait_ge(xn_made, i * BATCH)
                        root(i)
                        copy_turned(i)

                @block.tensor
                def _(pe):
                    def turn(i, j, first=False):
                        pe.wait_ge(xn_made, i * BATCH + j + 1)
                        if not (first and j < 2):
                            pe.wait_ge(xt_made, i * BATCH + j - 1)
                        for k in range(KC):
                            ins = pe.transpose(banks[:, j % 2, k * P:(k + 1) * P], xn[:, j, k * P:(k + 1) * P], ident[:, :])
                        ins.then_inc(turned, 1)

                    def multiply(i, j, first=False):
                        pe.wait_ge(xt_made, i * BATCH + j + 1)
                        if not first:
                            pe.wait_ge(y_made, i * BATCH + min(j | 1, BATCH - 1) + 1 - BATCH)
                        for k in range(KC):
                            ins = pe.matmul(banks[:, 2 + j // 2, (j % 2) * D:(j % 2 + 1) * D], xt[:, j, k * P:(k + 1) * P],
                                            w_node[:, k, :], start=(k == 0), stop=(k == KC - 1))
                        ins.then_inc(y_summed, 1)

                    def batch(i, first=False):
                        for j in range(BATCH + 1):
                            if j < BATCH:
                                turn(i, j, first)
                            if j >= 1:
                                multiply(i, j - 1, first)
                    pe.wait_ge(consts_made, 7)
                    pe.wait_ge(first_landed, 16 * 2)
                    batch(0, first=True)
                    with pe.Fori(1, NB) as i:
                        batch(i)


        class Buffers:
            mix_xt = sb("mix_xt", [P, C_LAST, D])
            x_rows = sb("x_rows", [P, C_LAST, D])
            w_mix = sb("w_mix", [P, KC, D])
            stats = sb("c_stats", [P, C_LAST, 6])
            moments = sb("c_moments", [P, C_LAST, 2])
            rstd = sb("c_rstd", [P, C_LAST])
            xf = sb("xf", [P, C_LAST, D])
            xf_t = sb("xf_t", [P, C_LAST, D])
            choice = sb("choice", [P, C_LAST, EXPERTS])
            best = sb("best", [P, C_LAST])
            counted = sb("counted", [P, EXPERTS], F32R)
            tri = sb("tri_count", [P, P], F32R)
            ones = sb("ones_count", [P, P], F32R)
            bias = sb("bias", [2 * WINDOW, D], F32R)
            bias_rows = sb("bias_rows", [2 * WINDOW, P], F32R)
            bias_row = sb("bias_row", [2 * WINDOW, 2])
            batch_count = sb("batch_count", [P, EXPERTS])
            own_rank = sb("own_rank", [P, C_LAST, EXPERTS])

        c_buf = Buffers()
        onehot = sb("onehot", [P, NT, EXPERTS], F32R)
        rank = sb("rank", [P, NT])
        reversed_iota = sb("reversed_iota", [P, EXPERTS])

        class Semaphores:
            def __init__(self, tag):
                self.nodes_landed = sem(f"nodes_landed_{tag}")
                self.mix_summed = sem(f"mix_summed_{tag}")
                self.mix_read = sem(f"mix_read_{tag}")
                self.aggregated = sem(f"aggregated_{tag}")
                self.stats_made = sem(f"stats_made_{tag}")
                self.rooted = sem(f"rooted_{tag}")
                self.inverted = sem(f"inverted_{tag}")
                self.centred = sem(f"centred_{tag}")
                self.xf_made = sem(f"xf_made_{tag}")
                self.turned = sem(f"turned_{tag}")
                self.copied = sem(f"copied_{tag}")
                self.logits_summed = sem(f"logits_summed_{tag}")
                self.choosing = sem(f"choosing_{tag}")
                self.cleared = sem(f"cleared_{tag}")
                self.chosen = sem(f"chosen_{tag}")
                self.ranked = sem(f"ranked_{tag}")
                self.ranks_read = sem(f"ranks_read_{tag}")
                self.rank_kept = sem(f"rank_kept_{tag}")
                self.batch_counted = sem(f"batch_counted_{tag}")
                self.batch_added = sem(f"batch_added_{tag}")

        def parts_of(m):
            return [range(0, min(m, 2))] + ([range(2, m)] if m > 2 else [])

        def c_load(sp, S, n, m=CB, first=False):
            if not first:
                sp.wait_ge(S.mix_summed, n * 2)
            tiles = bass.ds(n * CB, m)
            sp.dma_start(c_buf.mix_xt[:, 0:m, :], xt_tiles[:, tiles, :]).then_inc(S.nodes_landed, 16)
            sp.dma_start(c_buf.x_rows[:, 0:m, :], x_tiles[:, tiles, :]).then_inc(S.nodes_landed, 16)

        def c_mix(pe, S, n, part, m=CB, first=False, bank=None):
            if part == 0:
                pe.wait_ge(S.nodes_landed, n * 32 + 32)
            if bank is None and not (first and part == 0):
                pe.wait_ge(*((S.copied, n * 2) if part == 0 else (S.mix_read, n * 2 + 1)))
            for j in parts_of(m)[part]:
                out_j = banks[:, 6 if bank is None else bank, (j % 2) * D:(j % 2 + 1) * D]
                pe.matmul(out_j, c_buf.bias_rows[:, :], c_buf.bias[:, :], start=True, stop=False)
                pe.matmul(out_j, ident[:, :], c_buf.x_rows[:, j, :], start=False, stop=False)
                for k in range(KC):
                    ins = pe.matmul(out_j, c_buf.mix_xt[:, j, k * P:(k + 1) * P], c_buf.w_mix[:, k, :],
                                    start=False, stop=(k == KC - 1))
            ins.then_inc(S.mix_summed, 1)

        def c_turn(pe, S, n, part, m=CB):
            if part == 0:
                pe.wait_ge(S.xf_made, n + 1)
            else:
                pe.wait_ge(S.copied, n * 2 + 1)
            for j in parts_of(m)[part]:
                for k in range(KC):
                    ins = pe.transpose(banks[:, 6, (j % 2) * D + k * P:(j % 2) * D + (k + 1) * P],
                                       c_buf.xf[:, j, k * P:(k + 1) * P], ident[:, :])
            ins.then_inc(S.turned, 1)

        def c_logits(pe, S, n, m=CB, first=False):
            pe.wait_ge(S.copied, n * 2 + len(parts_of(m)))
            if not first:
                pe.wait_ge(S.ranks_read, n)
            pe.matmul(banks[:, 7, 0:m * EXPERTS], ones[0:1, :], rb_rows[0:1, None, :].to_broadcast([1, m, EXPERTS]), start=True, stop=True)
            for j in range(m):
                for k in range(KC):
                    ins = pe.matmul(banks[:, 7, j * EXPERTS:(j + 1) * EXPERTS], c_buf.xf_t[:, j, k * P:(k + 1) * P], router[:, k, :],
                                    start=False, stop=True, skip_group_check=True)
            ins.then_inc(S.logits_summed, 1)

        def c_count(pe, S, n, m=CB, first=False):
            pe.wait_ge(S.chosen, n + 1)
            if first:
                pe.wait_ge(S.cleared, 1)
            else:
                pe.wait_ge(S.batch_added, n)
            pe.matmul(banks[:, 7, 0:m * EXPERTS], c_buf.ones[:, :], c_buf.counted[:, None, :].to_broadcast([P, m, EXPERTS]), start=True, stop=True)
            for before in range(m - 1):
                pe.matmul(banks[:, 7, (before + 1) * EXPERTS:m * EXPERTS], c_buf.ones[:, :],
                          onehot[:, bass.ds(n * CB + before, 1), :].to_broadcast([P, m - 1 - before, EXPERTS]), start=False, stop=True,
                          skip_group_check=True)
            ins = pe.matmul(banks[:, 7, 0:m * EXPERTS], c_buf.tri[:, :], onehot[:, bass.ds(n * CB, m), :], start=False, stop=True,
                            skip_group_check=True)
            ins.then_inc(S.ranked, 1)

        def c_root(act, S, n, which, m=CB):
            act.wait_ge(S.aggregated, n * 2 + which + 1)
            act.activation(c_buf.rstd[:, 0:m], c_buf.moments[:, 0:m, 1], ACT.Sqrt,
                           bias=eps[:, 1 - which:2 - which]).then_inc(S.rooted, 1)

        def c_copy(act, S, n, part, m=CB, first=False):
            if part == 0 and not first:
                act.wait_ge(S.logits_summed, n)
            act.wait_ge(S.turned, n * 2 + part + 1)
            tiles = parts_of(m)[part]
            act.copy(c_buf.xf_t[:, tiles.start:tiles.stop, :],
                     banks[:, 6, 0:len(tiles) * D].rearrange("p (j d) -> p j d", d=D)).then_inc(S.copied, 1)

        def c_rows(n, m=CB):
            return node_rows[:, bass.ds(n * CB, m), :]

        def c_moments(dve, S, n, which, m=CB, first=False):
            dve.sem_inc(dve_tick, 1)
            for j in range(m):
                source = node_rows[:, bass.ds(n * CB + j, 1), 0:D] if which else acc[:, bass.ds(n * CB + j, 1), :]
                ins = dve.bn_stats(c_buf.stats[:, j, :], source)
            ins.then_inc(S.stats_made, 1)
            dve.wait_ge(S.stats_made, n * 2 + which + 1)
            if which == 0 and not first:
                dve.wait_ge(S.xf_made, n)
            dve.sem_inc(dve_tick, 1)
            for j in range(m):
                ins = dve.bn_aggr(c_buf.moments[:, j, :], c_buf.stats[:, j, :])
            ins.then_inc(S.aggregated, 1)

        def c_invert(dve, S, n, which, m=CB):
            dve.wait_ge(S.rooted, n * 2 + which + 1)
            dve.reciprocal(c_buf.rstd[:, 0:m], c_buf.rstd[:, 0:m]).then_inc(S.inverted, 1)
            dve.wait_ge(S.inverted, n * 2 + which + 1)

        def c_centre(dve, S, n, m=CB):
            c_invert(dve, S, n, 0, m)
            for j in range(m):
                ins = dve.scalar_tensor_tensor(out=node_rows[:, bass.ds(n * CB + j, 1), 0:D], in0=acc[:, bass.ds(n * CB + j, 1), :],
                                               scalar=c_buf.moments[:, j, 0:1], in1=gamma_rows[:, None, :],
                                               op0=ALU.subtract, op1=ALU.mult)
            ins.then_inc(S.centred, 1)

        def c_sum(dve, S, n, part, m=CB, bank=6):
            dve.wait_ge(S.centred, n + 1)
            dve.wait_ge(S.mix_summed, n * 2 + part + 1)
            for j in parts_of(m)[part]:
                tile = node_rows[:, bass.ds(n * CB + j, 1), 0:D]
                ins = dve.scalar_tensor_tensor(out=tile, in0=tile, scalar=c_buf.rstd[:, j:j + 1],
                                               in1=banks[:, bank:bank + 1, (j % 2) * D:(j % 2 + 1) * D], op0=ALU.mult, op1=ALU.add)
            ins.then_inc(S.mix_read, 1)
            if part == len(parts_of(m)) - 1:
                dve.wait_ge(S.mix_read, n * 2 + part + 1)

        def c_norm(dve, S, n, m=CB, first=False):
            c_invert(dve, S, n, 1, m)
            if not first:
                dve.wait_ge(S.turned, n * 2)
            dve.tensor_copy(c_rows(n, m)[:, :, MEAN], c_buf.moments[:, 0:m, 0])
            dve.tensor_copy(c_rows(n, m)[:, :, RSTD], c_buf.rstd[:, 0:m])
            for j in range(m):
                ins = dve.tensor_scalar(c_buf.xf[:, j:j + 1, :], node_rows[:, bass.ds(n * CB + j, 1), 0:D],
                                        c_buf.moments[:, j, 0:1], c_buf.rstd[:, j:j + 1], ALU.subtract, ALU.mult)
            ins.then_inc(S.xf_made, 1)

        def c_choose(dve, S, n, m=CB, first=False):
            dve.wait_ge(S.logits_summed, n + 1)
            wide = [P, m, EXPERTS]
            logits = banks[:, 7, 0:m * EXPERTS].rearrange("p (j e) -> p j e", j=m)
            choice, best = c_buf.choice[:, 0:m, :], c_buf.best[:, 0:m]
            dve.tensor_reduce(best, logits, AX.X, ALU.max).then_inc(S.choosing, 1)
            dve.wait_ge(S.choosing, n * 3 + 1)
            for j in range(m):
                ins = dve.scalar_tensor_tensor(out=choice[:, j, :], in0=logits[:, j, :], scalar=best[:, j:j + 1], in1=reversed_iota[:, :],
                                               op0=ALU.is_ge, op1=ALU.mult)
            ins.then_inc(S.choosing, 1)
            dve.wait_ge(S.choosing, n * 3 + 2)
            dve.tensor_reduce(best, choice, AX.X, ALU.max).then_inc(S.choosing, 1)
            dve.wait_ge(S.choosing, n * 3 + 3)
            dve.tensor_tensor(onehot[:, bass.ds(n * CB, m), :], choice, best[:, :, None].to_broadcast(wide), ALU.is_equal).then_inc(S.chosen, 1)
            if first:
                dve.tensor_scalar(c_buf.counted[:, :], reversed_iota[:, :], 0.0, None, ALU.mult).then_inc(S.cleared, 1)

        def c_ranks(dve, S, n, m=CB):
            dve.wait_ge(S.ranked, n + 1)
            dve.wait_ge(S.chosen, n + 1)
            chosen = onehot[:, bass.ds(n * CB, m), :]
            dve.tensor_tensor(c_buf.own_rank[:, 0:m, :], banks[:, 7, 0:m * EXPERTS].rearrange("p (j e) -> p j e", j=m),
                              chosen, ALU.mult).then_inc(S.ranks_read, 1)
            dve.tensor_reduce(c_buf.batch_count[:, :], chosen.rearrange("p j e -> p e j"), AX.X, ALU.add).then_inc(S.batch_counted, 1)
            dve.wait_ge(S.ranks_read, n + 1)
            dve.tensor_reduce(rank[:, bass.ds(n * CB, m)], c_buf.own_rank[:, 0:m, :], AX.X, ALU.add).then_inc(S.rank_kept, 1)
            dve.wait_ge(S.batch_counted, n + 1)
            dve.tensor_tensor(c_buf.counted[:, :], c_buf.counted[:, :], c_buf.batch_count[:, :], ALU.add).then_inc(S.batch_added, 1)

        def c_pe(pe, S, n, m=CB, first=False, mixed=False):
            if not mixed:
                for part in range(len(parts_of(m))):
                    c_mix(pe, S, n, part, m, first)
            for part in range(len(parts_of(m))):
                c_turn(pe, S, n, part, m)
            c_logits(pe, S, n, m, first)
            c_count(pe, S, n, m, first)

        def c_act(act, S, n, m=CB, first=False):
            c_root(act, S, n, 0, m)
            c_root(act, S, n, 1, m)
            for part in range(len(parts_of(m))):
                c_copy(act, S, n, part, m, first)

        def c_dve(dve, S, n, m=CB, first=False):
            c_moments(dve, S, n, 0, m, first)
            c_centre(dve, S, n, m)
            for part in range(len(parts_of(m))):
                c_sum(dve, S, n, part, m)
            c_moments(dve, S, n, 1, m)
            c_norm(dve, S, n, m, first)
            c_choose(dve, S, n, m, first)
            c_ranks(dve, S, n, m)

        with ExitStack() as ctx_b:
            def sb_b(name, shape, dt=F32):
                return ctx_b.enter_context(nc.sbuf_tensor(name, shape, dt))

            gather_index = sb_b("gather_index", [P, 2 * TILES], I32)
            attr_sb = sb_b("attr_sb", [D_EDGE, 2, TILES * P])
            attr_split = sb_b("attr_split", [P, 2, TILES * P], F32R)
            w_edge_split = sb_b("w_edge_split", [P, 2, D], F32R)
            msg = sb_b("msg", [P, 2 * QUADS, GROUPS, D])
            mask = sb_b("mask", [P, 2, TILES, WINDOW])
            place_mask = sb_b("place_mask", [P, 2, 2 * P])
            window = sb_b("window", [P, 2, D])
            head_var = sb_b("head_var", [P, KV, 2 * HEADS])
            kv_scale = sb_b("kv_scale", [P, KV, HEADS])
            wkv_mean = sb_b("wkv_mean", [P, KC * 2 * HEADS])

            b_steps = sem("b_steps")
            index_made = sem("index_made")
            attr_landed = [sem(f"attr_landed{h}") for h in range(2)]
            high_made = sem("high_made")
            low_made = sem("low_made")
            w_split_made = sem("w_split_made")
            kv_xt_landed = [sem(f"kv_xt_landed{which}") for which in range(2)]
            gathered = [sem(f"gathered{c}") for c in range(2 * QUADS)]
            edge_summed = sem("edge_summed")
            msg_added = sem("msg_added")
            silu_done = sem("silu_done")
            segments_summed = sem("segments_summed")
            mask_made = sem("mask_made")
            place_made = sem("place_made")
            window_copied = sem("window_copied")
            placed = sem("placed")
            acc_added = sem("acc_added")
            centred_weights = sem("centred_weights")
            kv_multiplied = sem("kv_multiplied")
            kv_copied = sem("kv_copied")
            squared = sem("squared")
            var_summed = sem("var_summed")
            heads_rooted = sem("heads_rooted")
            heads_inverted = sem("heads_inverted")
            scale_made = sem("scale_made")
            v_scaled = sem("v_scaled")
            dots_done = sem("dots_done")
            dots_masked = sem("dots_masked")
            dots_out_summed = sem("dots_out_summed")
            dots_out_copied = sem("dots_out_copied")
            w_mix_summed = sem("w_mix_summed")
            w_mix_made = sem("w_mix_made")
            c_ready = sem("c_ready")
            assert C_FIRST == KV_ITERS + 2
            miss_found = sem("miss_found")
            miss_known = sem("miss_known")
            NQ = 2 * QUADS
            assert NQ == 2 * KV
            S = Semaphores("b")
            slots_emptied = sem("slots_emptied")
            EMPTIED = SLOT_TILES // (KV_ITERS - 1)
            assert SLOT_TILES == EMPTIED * (KV_ITERS - 1)

            with nc.Block() as block:
                @block.sync
                def _(sp):
                    def load(i, h, first=False):
                        s = i * 2 + h
                        if not first:
                            sp.wait_ge(low_made, s - 1)
                        sp.dma_start(attr_sb[:, h:h + 1, :], attr[:, bass.ds(s, 1), :]).then_inc(attr_landed[h], 16)

                    def load_kv(i, first=False):
                        for which, (lo, hi) in enumerate(((0, KV - 1), (KV - 1, KV))):
                            if not first:
                                sp.wait_ge(kv_multiplied, i * 2 * KV - (2 * KV - 2 * hi))
                            sp.dma_start(kv_xt[:, lo:hi, :], xt_tiles[:, bass.ds(i * KV + lo, hi - lo), :]).then_inc(kv_xt_landed[which], 16)

                    def loads(i, kv_part=False, first=False):
                        load(i, 0, first)
                        load(i, 1, first)
                        if kv_part:
                            load_kv(i, first)

                    for part in range(len(PARTS)):
                        sp.wait_ge(xt_stored[part], 16 * NB)
                    sp.wait_ge(zeros_stored, 16 * (NKV - NT))
                    loads(0, True, first=True)
                    with sp.Fori(1, KV_ITERS) as i:
                        loads(i, True)
                        sp.dma_start(slot_tiles[:, bass.ds((i - 1) * EMPTIED, EMPTIED), :],
                                     empty_row[:, None, :].to_broadcast([P, EMPTIED, ROW])).then_inc(slots_emptied, 16)
                    with sp.Fori(KV_ITERS, C_FIRST + 1) as i:
                        loads(i)
                    load(C_FIRST + 1, 0)
                    c_load(sp, S, 0, first=True)
                    with sp.Fori(C_FIRST + 1, NI - 1) as i:
                        load(i, 1)
                        load(i + 1, 0)
                        c_load(sp, S, i - C_FIRST)
                    load(NI - 1, 1)
                    c_load(sp, S, CN - 1, C_LAST)
                    sp.wait_ge(slots_emptied, 16 * (KV_ITERS - 1))

                @block.gpsimd
                def _(pool):
                    def gather(i, h, first=False, last=False):
                        for k in range(QUADS):
                            c = h * QUADS + k
                            pool.wait_ge(index_made, i * NQ + c + 1)
                            if not first:
                                pool.wait_ge(segments_summed, i * NQ + c + 1 - NQ)
                            pool.sem_inc(pool_tick, 1)
                            for g in range(LAST_GROUPS if last else GROUPS):
                                t = k * GROUPS + g
                                pool.indirect_dma_start(
                                    msg[:, c, g, :], None, y_dram,
                                    bass.IndirectOffsetOnAxis(ap=gather_index[:, h * TILES + t:h * TILES + t + 1], axis=0),
                                    bounds_check=N_NODES - 1, oob_is_err=False).then_inc(gathered[c], 16)

                    for h in range(2):
                        gather(0, h, first=True)
                    with pool.Fori(1, NI - 1) as i:
                        for h in range(2):
                            gather(i, h)
                    gather(NI - 1, 0)
                    gather(NI - 1, 1, last=True)

                @block.tensor
                def _(pe):
                    def edge_products(i, c, first=False):
                        h, k = divmod(c, QUADS)
                        if k == 0:
                            pe.wait_ge(low_made, i * 2 + h + 1)
                        if not (first and c < 2):
                            pe.wait_ge(msg_added, i * NQ + c - 1)
                        for g in range(GROUPS):
                            col = (k * GROUPS + g) * P
                            for part in range(2):
                                ins = pe.matmul(banks[:, (c % 2) * 2 + g // 2, (g % 2) * D:(g % 2 + 1) * D],
                                                attr_split[:, h, col:col + P], w_edge_split[:, part, :],
                                                start=(part == 0), stop=(part == 1))
                        ins.then_inc(edge_summed, 1)

                    def segment_sums(i, c, first=False):
                        h, k = divmod(c, QUADS)
                        pe.wait_ge(silu_done, i * NQ + c + 1)
                        if k == 0:
                            pe.wait_ge(mask_made, i * 2 + h + 1)
                            if not (first and h == 0):
                                pe.wait_ge(window_copied, i * 2 + h)
                        for g in range(GROUPS):
                            ins = pe.matmul(banks[g * WINDOW:(g + 1) * WINDOW, 4, 0:D], mask[:, h, k * GROUPS + g, :],
                                            msg[:, c, g, :], start=(k == 0), stop=(k == QUADS - 1))
                        ins.then_inc(segments_summed, 1)

                    def place_windows(i, h, first=False):
                        pe.wait_ge(window_copied, i * 2 + h + 1)
                        pe.wait_ge(place_made, i * 2 + h + 1)
                        if not (first and h == 0):
                            pe.wait_ge(acc_added, i * 2 + h)
                        for b in range(2):
                            ins = pe.matmul(banks[:, 5, b * D:(b + 1) * D], place_mask[:, h, b * P:(b + 1) * P],
                                            window[:, h, :], start=True, stop=True)
                        ins.then_inc(placed, 1)

                    def keys_values(i, r, part, first=False):
                        if part == 0 and r in (0, KV - 1):
                            pe.wait_ge(kv_xt_landed[r // (KV - 1)], i * 16 + 16)
                        if not (first and r == 0 and part == 0):
                            pe.wait_ge(kv_copied, (i * KV + r) * 2 + part)
                        for k in range(KC):
                            ins = pe.matmul(banks[:, 6, :], kv_xt[:, r, k * P:(k + 1) * P],
                                            wkv[:, k, part * INNER:(part + 1) * INNER], start=(k == 0), stop=(k == KC - 1))
                        ins.then_inc(kv_multiplied, 1)

                    def dots(i, r, first=False):
                        if r == 0:
                            pe.wait_ge(v_scaled, i + 1)
                        for q in range(PAIRS):
                            ins = pe.matmul(banks[:, 7, q * P:(q + 1) * P], scaled_v[:, r, q * P:(q + 1) * P],
                                            kv[:, r, INNER + q * P:INNER + (q + 1) * P], start=(first and r == 0 and q == 0), stop=True,
                                            skip_group_check=True)
                        ins.then_inc(dots_done, 1)

                    def mix_weights(c):
                        if c in (2, 3):
                            part = c - 2
                            pe.wait_ge(dots_masked, 1)
                            if part == 1:
                                pe.wait_ge(dots_out_copied, 1)
                            for q in range(2):
                                ins = pe.matmul(banks[:, 6, q * D:(q + 1) * D], dots_blocks[:, part * 2 + q, :], wo_sb[:, part * 2 + q, :],
                                                start=True, stop=True)
                            ins.then_inc(dots_out_summed, 1)
                        if c == 5:
                            pe.wait_ge(dots_out_copied, 2)
                            for k in range(KC):
                                for q in range(PAIRS):
                                    ins = pe.matmul(banks[:, 6, k * D:(k + 1) * D], wq_sb[:, q, k * P:(k + 1) * P], dots_out[:, q, :],
                                                    start=(q == 0), stop=(q == PAIRS - 1))
                            ins.then_inc(w_mix_summed, 1)

                    def supertiles(i, first=False, before=True, kv_part=False, kv_before=False, n=None, c_first=0,
                                   last=False, mixing=False):
                        for c in range(NQ):
                            h, k = divmod(c, QUADS)
                            if c < NQ - 1:
                                edge_products(i, c + 1, first)
                            elif not last:
                                edge_products(i + 1, 0)
                            if c >= 1:
                                segment_sums(i, c - 1, first)
                            elif before:
                                segment_sums(i - 1, NQ - 1)
                            if k == 1:
                                if h == 1:
                                    place_windows(i, 0, first)
                                elif before:
                                    place_windows(i - 1, 1)
                            if kv_before and c == 0:
                                keys_values(i - 1, KV - 1, 1)
                            if kv_before and 2 <= c < 2 + KV:
                                dots(i - 1, c - 2, first=(c_first == -1))
                            if kv_part and c >= 1:
                                keys_values(i, *divmod(c - 1, 2), first)
                            if mixing:
                                mix_weights(c)
                            if n is not None:
                                if c <= 1 and c_first != 1:
                                    c_turn(pe, S, n - 1, c)
                                if c == 2:
                                    if c_first != 1:
                                        c_logits(pe, S, n - 1, first=(c_first == 2))
                                    c_mix(pe, S, n, 0, first=(c_first == 1))
                                if c == 3:
                                    c_mix(pe, S, n, 1)
                                if c == 4 and c_first != 1:
                                    c_count(pe, S, n - 1, first=(c_first == 2))

                    pe.wait_ge(consts_landed, 16 * N_CONSTS)
                    pe.wait_ge(w_split_made, 2)
                    edge_products(0, 0, first=True)
                    pe.wait_ge(centred_weights, 1)
                    supertiles(0, first=True, before=False, kv_part=True)
                    supertiles(1, kv_part=True, kv_before=True, c_first=-1)
                    with pe.Fori(2, KV_ITERS) as i:
                        supertiles(i, kv_part=True, kv_before=True)
                    supertiles(KV_ITERS, kv_before=True)
                    supertiles(KV_ITERS + 1, mixing=True)
                    supertiles(KV_ITERS + 2)
                    pe.wait_ge(w_mix_made, 1)
                    pe.wait_ge(c_ready, 1)
                    supertiles(C_FIRST + 1, n=0, c_first=1)
                    supertiles(C_FIRST + 2, n=1, c_first=2)
                    with pe.Fori(C_FIRST + 3, NI - 1) as i:
                        supertiles(i, n=i - (C_FIRST + 1))
                    supertiles(NI - 1, n=NI - 1 - (C_FIRST + 1), last=True)
                    segment_sums(NI - 1, NQ - 1)
                    place_windows(NI - 1, 1)
                    pe.wait_ge(msg_added, NI * NQ - 1)
                    for part in range(2):
                        c_mix(pe, S, CN - 1, part, C_LAST, bank=part)
                    n = NI - 1 - (C_FIRST + 1)
                    pe.wait_ge(acc_added, NS)
                    pe.matmul(banks[:, 5, 0:1], ones[:, :], miss_sum[:, 0:1], start=True, stop=True).then_inc(miss_found, 1)
                    for part in range(2):
                        c_turn(pe, S, n, part)
                    c_logits(pe, S, n)
                    c_count(pe, S, n)
                    c_pe(pe, S, n + 1, C_LAST, mixed=True)

                @block.vector
                def _(dve):
                    def copy_index(i, c):
                        dve.tensor_copy(gather_index[:, c * GROUPS:(c + 1) * GROUPS],
                                        src_i[:, bass.ds(i * 2 * TILES + c * GROUPS, GROUPS)]).then_inc(index_made, 1)

                    def add_products(i, c, last=False):
                        dve.wait_ge(edge_summed, i * NQ + c + 1)
                        dve.wait_ge(gathered[c], (i + 1) * 16 * GROUPS if not last or c < QUADS else (i * GROUPS + LAST_GROUPS) * 16)
                        b = (c % 2) * 2
                        m = msg[:, c, :, :].rearrange("p (b g) d -> p b (g d)", b=2)
                        dve.tensor_tensor(m, m, banks[:, b:b + 2, :], ALU.add).then_inc(msg_added, 1)
                        if not last:
                            copy_index(i + 1, c)

                    def masks(i, h, first=False):
                        s = i * 2 + h
                        if not first:
                            dve.wait_ge(segments_summed, i * NQ + (h - 1) * QUADS)
                        dve.tensor_tensor(mask[:, h, :, :], iota[:, None, 0:WINDOW].to_broadcast([P, TILES, WINDOW]),
                                          rel[:, bass.ds(s, 1), :].rearrange("p s t -> p (s t)")[:, :, None].to_broadcast([P, TILES, WINDOW]),
                                          ALU.is_equal).then_inc(mask_made, 1)
                        if not first:
                            dve.wait_ge(placed, i * 2 + h - 1)
                        dve.tensor_scalar(place_mask[:, h, :], iota[:, :], place[:, bass.ds(s, 1)], None,
                                          ALU.is_equal).then_inc(place_made, 1)

                    def split_low(s, h):
                        dve.wait_ge(high_made, s + 1)
                        dve.tensor_tensor(attr_split[D_EDGE:P, h, :], attr_sb[:, h, :], attr_split[0:D_EDGE, h, :], ALU.subtract).then_inc(low_made, 1)

                    def add_blocks(i, h, first=False):
                        block = dve.value_load(block_i[0:1, bass.ds(i * 2 + h, 1)], min_val=0, max_val=NT - 1)
                        dve.wait_ge(placed, i * 2 + h + 1)
                        if not (first and h == 0):
                            dve.wait_ge(acc_added, i * 2 + h)
                        both = acc[:, bass.ds(block, 2), :]
                        dve.tensor_tensor(both, both, banks[:, 5, :].rearrange("p (b d) -> p b d", b=2), ALU.add).then_inc(acc_added, 1)

                    def head_variances(i, r, first=False):
                        dve.wait_ge(squared, i * KV + r + 1)
                        if r == 0 and not first:
                            dve.wait_ge(scale_made, i)
                        dve.tensor_reduce(head_var[:, r, :], squares.rearrange("p (g d) -> p g d", d=DH), AX.X, ALU.add).then_inc(var_summed, 1)

                    def scale_values(i, first=False):
                        dve.wait_ge(heads_rooted, i + 1)
                        dve.reciprocal(head_var[:, :, :], head_var[:, :, :]).then_inc(heads_inverted, 1)
                        dve.wait_ge(heads_inverted, i + 1)
                        if not first:
                            dve.wait_ge(v_scaled, i)
                        dve.tensor_tensor(kv_scale[:, :, :], head_var[:, :, 0:HEADS], head_var[:, :, HEADS:2 * HEADS], ALU.mult).then_inc(scale_made, 1)
                        dve.wait_ge(scale_made, i + 1)
                        if not first:
                            dve.wait_ge(dots_done, i * KV)
                        for r in range(KV):
                            ins = dve.tensor_tensor(scaled_v[:, r, :].rearrange("p (g d) -> p g d", d=DH),
                                                    kv[:, r, 0:INNER].rearrange("p (g d) -> p g d", d=DH),
                                                    kv_scale[:, r, :, None].to_broadcast([P, HEADS, DH]), ALU.mult)
                        ins.then_inc(v_scaled, 1)

                    def supertiles(i, first=False, before=True, kv_part=False, kv_before=False, n=None, c_first=0,
                                   last=False, mixing=False, missing=False):
                        for c in range(NQ):
                            h, k = divmod(c, QUADS)
                            if c == 0:
                                masks(i, 0, first)
                            add_products(i, c, last)
                            if c == 2:
                                masks(i, 1, first)
                            if mixing and c == 1:
                                mask_dots()
                            if missing:
                                find_missed(c)
                            if kv_before and c == 1:
                                head_variances(i - 1, 2, first=(c_first == -1))
                                scale_values(i - 1, first=(c_first == -1))
                            if c == 0:
                                split_low(i * 2 + 1, 1)
                            if c == 4 and not last:
                                split_low(i * 2 + 2, 0)
                            if k == 2:
                                if h == 1:
                                    add_blocks(i, 0, first)
                                elif before:
                                    add_blocks(i - 1, 1)
                            if kv_part and c in (3, 5):
                                head_variances(i, (c - 3) // 2, first)
                            if n is not None:
                                if c == 1:
                                    dve.wait_ge(acc_added, i * 2 - 1)
                                    c_moments(dve, S, n, 0, first=(c_first == 1))
                                if c == 2:
                                    c_centre(dve, S, n)
                                if c == 3:
                                    if c_first != 1:
                                        c_choose(dve, S, n - 1, first=(c_first == 2))
                                    c_sum(dve, S, n, 0)
                                if c == 4:
                                    c_sum(dve, S, n, 1)
                                    c_moments(dve, S, n, 1)
                                if c == 5:
                                    c_norm(dve, S, n, first=(c_first == 1))
                                    if c_first != 1:
                                        c_ranks(dve, S, n - 1)

                    steps = 0

                    def link(ins, done=1):
                        nonlocal steps
                        steps += done
                        ins.then_inc(b_steps, 1)
                        dve.wait_ge(b_steps, steps)

                    def mask_dots():
                        dve.wait_ge(dots_done, KV_ITERS * KV)
                        dve.memset(dots_blocks[:, :, :], 0.0).then_inc(b_steps, 1)
                        link(dve.tensor_copy(dots_t[:, :, :], banks[:, 7, :].rearrange("p (q d) -> p q d", q=PAIRS)), 2)
                        for h in range(2):
                            lanes = slice(h * DH, (h + 1) * DH)
                            ins = dve.tensor_copy(dots_blocks[lanes, :, lanes], dots_t[lanes, :, lanes])
                        ins.then_inc(dots_masked, 1)
                        link(dve.tensor_scalar(reversed_iota[:, :], iota[:, 0:EXPERTS], -1.0, float(EXPERTS), ALU.mult, ALU.add))
                        dve.tensor_copy(c_buf.tri[:, :], tri[:, :])
                        dve.tensor_copy(c_buf.ones[:, :], ones[:, :])
                        lanes = slice(0, 2 * WINDOW)
                        dve.tensor_scalar(c_buf.bias_row[:, 0:1], row[lanes, :], 0.0, None, ALU.is_equal)
                        link(dve.tensor_scalar(c_buf.bias_row[:, 1:2], row[lanes, :], float(WINDOW), None, ALU.is_equal))
                        link(dve.tensor_tensor(c_buf.bias_row[:, 0:1], c_buf.bias_row[:, 0:1], c_buf.bias_row[:, 1:2], ALU.add))
                        dve.tensor_scalar(c_buf.bias_rows[:, :], ones[lanes, :], c_buf.bias_row[:, 0:1], None, ALU.mult)
                        link(dve.tensor_tensor(beta_rows[lanes, :], beta_rows[lanes, :], bout_rows[lanes, :], ALU.add))
                        link(dve.tensor_copy(c_buf.bias[:, :], beta_rows[lanes, :]))
                        low = slice(WINDOW, 2 * WINDOW)
                        link(dve.tensor_tensor(c_buf.bias[low, :], beta_rows[low, :], c_buf.bias[low, :], ALU.subtract))

                    def find_missed(c):
                        dst_s = dst_i.rearrange("p (s t) -> p s t", t=TILES)
                        wide = [P, NS, TILES]
                        work = window_work
                        if c == 0:
                            dve.wait_ge(w_mix_made, 1)
                            link(dve.tensor_tensor(work, dst_s, block_f[:, :, None].to_broadcast(wide), ALU.subtract))
                            link(dve.tensor_scalar(missed[:, :, :], work, 0.0, None, ALU.is_ge))
                        if c in (1, 2, 3):
                            values, bound, op = ((work, float(2 * P), ALU.is_lt), (rel[:, :, :], 0.0, ALU.is_ge),
                                                 (rel[:, :, :], float(WINDOW), ALU.is_lt))[c - 1]
                            link(dve.scalar_tensor_tensor(out=missed[:, :, :], in0=values, scalar=bound, in1=missed[:, :, :],
                                                          op0=op, op1=ALU.mult))
                        if c == 3:
                            link(dve.tensor_scalar(missed[:, :, :], missed[:, :, :], -1.0, 1.0, ALU.mult, ALU.add))
                        if c == 4:
                            link(dve.scalar_tensor_tensor(out=missed[:, :, :], in0=dst_s, scalar=float(PAD_DST), in1=missed[:, :, :],
                                                          op0=ALU.is_lt, op1=ALU.mult))
                            link(dve.tensor_reduce(miss_sum[:, 0:1], missed[:, :, :].rearrange("p s t -> p (s t)"), AX.X, ALU.add))
                        if c == 5:
                            slope = float(P * CB // 2)
                            link(dve.tensor_scalar(block_f[:, :], iota[:, 0:NS], slope, slope * (1 - 2 * C_FIRST), ALU.mult, ALU.add))
                            link(dve.tensor_scalar(block_f[:, :], block_f[:, :], float(P * CB * (NI - 1 - C_FIRST)), None, ALU.min))
                            link(dve.tensor_tensor(work, dst_s, block_f[:, :, None].to_broadcast(wide), ALU.is_lt))
                            link(dve.tensor_reduce(miss_sum[:, 1:2], work.rearrange("p s t -> p (s t)"), AX.X, ALU.add))
                            link(dve.tensor_tensor(miss_sum[:, 0:1], miss_sum[:, 0:1], miss_sum[:, 1:2], ALU.add))

                    dve.wait_ge(src_landed, 16)
                    for c in range(NQ):
                        copy_index(0, c)
                    dve.wait_ge(consts_landed, 16 * N_CONSTS)
                    dve.tensor_copy(w_edge_split[:, 0, :], w_edge[:, :]).then_inc(w_split_made, 1)
                    dve.wait_ge(w_split_made, 1)
                    dve.tensor_tensor(w_edge_split[:, 1, :], w_edge[:, :], w_edge_split[:, 0, :], ALU.subtract).then_inc(w_split_made, 1)
                    dve.wait_ge(edges_landed, 16 * (2 + GROUPS))
                    split_low(0, 0)
                    link(dve.tensor_copy(base_f[:, :, :], base_i.rearrange("p (s g) -> p s g", g=GROUPS)))
                    link(dve.tensor_tensor(rel.rearrange("p s (k g) -> p s k g", g=GROUPS), dst_i.rearrange("p (s k g) -> p s k g", k=QUADS, g=GROUPS),
                                           base_f[:, :, None, :].to_broadcast([P, NS, QUADS, GROUPS]), ALU.subtract))
                    link(dve.tensor_scalar(block_i[:, :], base_i.rearrange("p (s g) -> p s g", g=GROUPS)[:, :, 0], 7, None,
                                           ALU.arith_shift_right))
                    link(dve.tensor_copy(block_f[:, :], block_i[:, :]))
                    link(dve.tensor_scalar(block_f[:, :], block_f[:, :], float(NT - 1), 0.0, ALU.min, ALU.max))
                    link(dve.tensor_copy(block_i[:, :], block_f[:, :]))
                    link(dve.tensor_scalar(block_f[:, :], block_f[:, :], float(P), None, ALU.mult))
                    link(dve.tensor_copy(row_node[:, :], base_row_i[:, :]))
                    for g in range(GROUPS):
                        lanes = slice(g * WINDOW, (g + 1) * WINDOW)
                        ins = dve.tensor_scalar(row_node[lanes, :], row_node[lanes, :], row[lanes, :], float(-g * WINDOW), ALU.add, ALU.add)
                    link(ins)
                    link(dve.tensor_tensor(place[:, :], row_node[:, :], block_f[:, :], ALU.subtract))
                    w_heads = wkv.rearrange("p k (h d) -> p (k h) d", d=DH)
                    link(dve.tensor_reduce(wkv_mean[:, :], w_heads, AX.X, ALU.add))
                    link(dve.tensor_scalar(wkv_mean[:, :], wkv_mean[:, :], 1.0 / DH, None, ALU.mult))
                    dve.tensor_tensor(w_heads, w_heads, wkv_mean[:, :, None].to_broadcast([P, KC * 2 * HEADS, DH]), ALU.subtract).then_inc(centred_weights, 1)

                    supertiles(0, first=True, before=False, kv_part=True)
                    supertiles(1, kv_part=True, kv_before=True, c_first=-1)
                    with dve.Fori(2, KV_ITERS) as i:
                        supertiles(i, kv_part=True, kv_before=True)
                    supertiles(KV_ITERS, kv_before=True)

                    supertiles(KV_ITERS + 1, mixing=True)
                    supertiles(KV_ITERS + 2, missing=True)
                    dve.wait_ge(w_mix_made, 1)
                    dve.tensor_copy(node_rows[:, :, NODE], node_i[:, :])
                    dve.memset(node_rows[:, :, NODE + 1:ROW], 0.0).then_inc(c_ready, 1)
                    dve.wait_ge(c_ready, 1)
                    supertiles(C_FIRST + 1, n=0, c_first=1)
                    supertiles(C_FIRST + 2, n=1, c_first=2)
                    with dve.Fori(C_FIRST + 3, NI - 1) as i:
                        supertiles(i, n=i - (C_FIRST + 1))
                    n = NI - 1 - (C_FIRST + 1)
                    supertiles(NI - 1, n=n, last=True)
                    add_blocks(NI - 1, 1)
                    dve.wait_ge(acc_added, NS)
                    dve.wait_ge(miss_found, 1)
                    dve.tensor_scalar(miss_i[:, :], banks[:, 5, 0:1], 1.0, None, ALU.min).then_inc(miss_known, 1)
                    c_moments(dve, S, n + 1, 0, C_LAST)
                    c_centre(dve, S, n + 1, C_LAST)
                    c_sum(dve, S, n + 1, 0, C_LAST, bank=0)
                    c_sum(dve, S, n + 1, 1, C_LAST, bank=1)
                    c_choose(dve, S, n)
                    c_moments(dve, S, n + 1, 1, C_LAST)
                    c_ranks(dve, S, n)
                    c_norm(dve, S, n + 1, C_LAST)
                    c_choose(dve, S, n + 1, C_LAST)
                    c_ranks(dve, S, n + 1, C_LAST)

                @block.scalar
                def _(act):
                    def silu(i, c):
                        act.wait_ge(msg_added, i * NQ + c + 1)
                        act.activation(msg[:, c, :, :], msg[:, c, :, :], ACT.Silu).then_inc(silu_done, 1)

                    def split_high(i, h, first=False):
                        act.wait_ge(attr_landed[h], i * 16 + 16)
                        if not first:
                            act.wait_ge(edge_summed, i * NQ + (h - 1) * QUADS)
                        act.copy(attr_split[0:D_EDGE, h, :], attr_sb[:, h, :]).then_inc(high_made, 1)

                    def copy_window(i, h, first=False):
                        act.wait_ge(segments_summed, i * NQ + (h + 1) * QUADS)
                        if not first:
                            act.wait_ge(placed, i * 2 + h - 1)
                        act.copy(window[:, h, :], banks[:, 4, 0:D]).then_inc(window_copied, 1)

                    def copy_kv(i, r, part, first=False):
                        act.wait_ge(kv_multiplied, (i * KV + r) * 2 + part + 1)
                        if not first:
                            act.wait_ge(*((v_scaled, i) if part == 0 else (dots_done, i * KV + r + 1 - KV)))
                        act.copy(kv[:, r, part * INNER:(part + 1) * INNER], banks[:, 6, :]).then_inc(kv_copied, 1)
                        if part == 1:
                            square(i, r, first)

                    def square(i, r, first=False):
                        act.wait_ge(kv_copied, (i * KV + r + 1) * 2)
                        if not (first and r == 0):
                            act.wait_ge(var_summed, i * KV + r)
                        act.activation(squares[:, :], kv[:, r, :], ACT.Square).then_inc(squared, 1)

                    def root(i):
                        act.wait_ge(var_summed, (i + 1) * KV)
                        act.activation(head_var[:, :, :], head_var[:, :, :], ACT.Sqrt, bias=eps[:, 0:1], scale=1.0 / DH).then_inc(heads_rooted, 1)

                    def supertiles(i, first=False, before=True, kv_part=False, kv_before=False, n=None, c_first=0, last=False,
                                   mixing=False):
                        for c in range(NQ):
                            h, k = divmod(c, QUADS)
                            if kv_before and c <= 1:
                                copy_kv(i - 1, KV - 1, c, first=(c_first == -1))
                            if kv_part and c >= 2:
                                copy_kv(i, *divmod(c - 2, 2), first)
                            if mixing and c in (3, 4):
                                act.wait_ge(dots_out_summed, c - 2)
                                part = slice((c - 3) * 2, (c - 2) * 2)
                                act.copy(dots_out[:, part, :], banks[:, 6, :].rearrange("p (q d) -> p q d", q=2)).then_inc(dots_out_copied, 1)
                            silu(i, c)
                            if kv_before and c == 1:
                                root(i - 1)
                            if c == 3 and not last:
                                split_high(i + 1, 0)
                            if c == 5 and not last:
                                split_high(i + 1, 1)
                            if k == 0:
                                if h == 1:
                                    copy_window(i, 0, first)
                                elif before:
                                    copy_window(i - 1, 1, first=(c_first == -1))
                            if n is not None:
                                if c <= 1 and c_first != 1:
                                    c_copy(act, S, n - 1, c, first=(c_first == 2))
                                if c == 1:
                                    c_root(act, S, n, 0)
                                if c == 4:
                                    c_root(act, S, n, 1)

                    for h in range(2):
                        split_high(0, h, first=True)
                    supertiles(0, first=True, before=False, kv_part=True)
                    supertiles(1, kv_part=True, kv_before=True, c_first=-1)
                    with act.Fori(2, KV_ITERS) as i:
                        supertiles(i, kv_part=True, kv_before=True)
                    supertiles(KV_ITERS, kv_before=True)
                    supertiles(KV_ITERS + 1, mixing=True)
                    act.wait_ge(w_mix_summed, 1)
                    act.mul(c_buf.w_mix[:, :, :], banks[:, 6, :].rearrange("p (k d) -> p k d", k=KC), 1.0 / N_NODES).then_inc(w_mix_made, 1)
                    supertiles(KV_ITERS + 2)
                    supertiles(C_FIRST + 1, n=0, c_first=1)
                    supertiles(C_FIRST + 2, n=1, c_first=2)
                    with act.Fori(C_FIRST + 3, NI - 1) as i:
                        supertiles(i, n=i - (C_FIRST + 1))
                    n = NI - 1 - (C_FIRST + 1)
                    supertiles(NI - 1, n=n, last=True)
                    copy_window(NI - 1, 1)
                    c_copy(act, S, n, 0)
                    c_copy(act, S, n, 1)
                    c_act(act, S, n + 1, C_LAST)

        with ExitStack() as ctx_g:
            def sb_g(name, shape, dt=F32):
                return ctx_g.enter_context(nc.sbuf_tensor(name, shape, dt))

            any_missed = nc.values_load(miss_i[0:1, 0:1], min_val=0, max_val=1)
            index_g = sb_g("index_g", [P, 1], I32)
            attr_g = sb_g("attr_g", [D_EDGE, P])
            msg_g = sb_g("msg_g", [P, D])
            wanted = sb_g("wanted", [P, 1])
            mask_g = sb_g("mask_g", [P, P])
            w_edge_g = sb_g("w_edge_g", [D_EDGE, D])
            w_landed_g = sem("w_landed_g")
            edges_loaded_g = sem("edges_loaded_g")
            gathered_g = sem("gathered_g")
            product_g = sem("product_g")
            added_g = sem("added_g")
            silu_g = sem("silu_g")
            wanted_g = sem("wanted_g")
            mask_made_g = sem("mask_made_g")
            summed_g = sem("summed_g")
            acc_g = sem("acc_g")
            tile_done_g = sem("tile_done_g")
            sp_tick = sem("sp_tick")

            with nc.If(any_missed):
                with nc.Block() as block:
                    def each_tile(engine, body):
                        with engine.Fori(0, NS) as s:
                            with engine.Fori(0, TILES // 2) as pair:
                                for half in range(2):
                                    body(s, pair, half, (s * (TILES // 2) + pair) * 2 + half)

                    @block.sync
                    def _(sp):
                        def load(s, pair, half, u):
                            sp.wait_ge(tile_done_g, u + 1)
                            sp.sem_inc(sp_tick, 1)
                            with nc.allow_non_contiguous_dma(reason="one column of indices"):
                                sp.dma_start(index_g[:, :], src[:, bass.ds(u, 1)]).then_inc(edges_loaded_g, 16)
                            sp.dma_start(attr_g[:, :], attr[:, bass.ds(s, 1), bass.ds((pair * 2 + half) * P, P)].rearrange("p s e -> p (s e)")).then_inc(edges_loaded_g, 16)
                        sp.dma_start(w_edge_g[:, :], w_gnn[D:D + D_EDGE, :]).then_inc(w_landed_g, 16)
                        sp.sem_inc(tile_done_g, 1)
                        each_tile(sp, load)

                    @block.gpsimd
                    def _(pool):
                        def gather(s, pair, half, u):
                            pool.wait_ge(edges_loaded_g, (u + 1) * 32)
                            pool.sem_inc(pool_tick, 1)
                            pool.indirect_dma_start(msg_g[:, :], None, y_dram, bass.IndirectOffsetOnAxis(ap=index_g[:, 0:1], axis=0),
                                                    bounds_check=N_NODES - 1, oob_is_err=False).then_inc(gathered_g, 16)
                        each_tile(pool, gather)

                    @block.tensor
                    def _(pe):
                        def products(s, pair, half, u):
                            pe.wait_ge(edges_loaded_g, (u + 1) * 32)
                            pe.matmul(banks[:, 0, 0:D], attr_g[:, :], w_edge_g[:, :], start=True, stop=True).then_inc(product_g, 1)
                            pe.wait_ge(silu_g, u + 1)
                            pe.sem_inc(pe_tick, 1)
                            with pe.Fori(0, NT) as b:
                                v = u * NT + b
                                pe.wait_ge(mask_made_g, v + 1)
                                pe.matmul(banks[:, 1, 0:D], mask_g[:, :], msg_g[:, :], start=True, stop=True).then_inc(summed_g, 1)
                        pe.wait_ge(w_landed_g, 16)
                        each_tile(pe, products)

                    @block.scalar
                    def _(act):
                        def silu(s, pair, half, u):
                            act.wait_ge(added_g, u + 1)
                            act.activation(msg_g[:, :], msg_g[:, :], ACT.Silu).then_inc(silu_g, 1)
                        each_tile(act, silu)

                    @block.vector
                    def _(dve):
                        def add(s, pair, half, u):
                            dve.wait_ge(product_g, u + 1)
                            dve.wait_ge(gathered_g, (u + 1) * 16)
                            dve.tensor_tensor(msg_g[:, :], msg_g[:, :], banks[:, 0, 0:D], ALU.add).then_inc(added_g, 1)
                            dst_tile = dst_i.rearrange("p (s t) -> p s t", t=TILES)[:, bass.ds(s, 1), bass.ds(pair * 2 + half, 1)].rearrange("p s t -> p (s t)")
                            missed_tile = missed[:, bass.ds(s, 1), bass.ds(pair * 2 + half, 1)].rearrange("p s t -> p (s t)")
                            dve.scalar_tensor_tensor(out=wanted[:, :], in0=dst_tile, scalar=1.0, in1=missed_tile,
                                                     op0=ALU.add, op1=ALU.mult).then_inc(wanted_g, 1)
                            dve.wait_ge(wanted_g, u * (NT + 2) + 1)
                            dve.tensor_scalar(wanted[:, :], wanted[:, :], 1.0, None, ALU.subtract).then_inc(wanted_g, 1)
                            with dve.Fori(0, NT) as b:
                                v = u * NT + b
                                dve.wait_ge(wanted_g, u * (NT + 2) + b + 2)
                                dve.tensor_scalar(mask_g[:, :], iota[:, 0:P], wanted[:, :], None, ALU.is_equal).then_inc(mask_made_g, 1)
                                dve.wait_ge(mask_made_g, v + 1)
                                dve.tensor_scalar(wanted[:, :], wanted[:, :], float(P), None, ALU.subtract).then_inc(wanted_g, 1)
                                dve.wait_ge(summed_g, v + 1)
                                block_b = acc[:, bass.ds(b, 1), :]
                                dve.tensor_tensor(block_b, block_b, banks[:, 1:2, 0:D], ALU.add).then_inc(acc_g, 1)
                            dve.wait_ge(acc_g, (u + 1) * NT)
                            dve.sem_inc(tile_done_g, 1)
                        each_tile(dve, add)

                R = Semaphores("again")
                with nc.Block() as block:
                    @block.sync
                    def _(sp):
                        c_load(sp, R, 0, first=True)
                        with sp.Fori(1, CN - 1) as n:
                            c_load(sp, R, n)
                        c_load(sp, R, CN - 1, C_LAST)

                    @block.tensor
                    def _(pe):
                        c_pe(pe, R, 0, first=True)
                        with pe.Fori(1, CN - 1) as n:
                            c_pe(pe, R, n)
                        c_pe(pe, R, CN - 1, C_LAST)

                    @block.scalar
                    def _(act):
                        c_act(act, R, 0, first=True)
                        with act.Fori(1, CN - 1) as n:
                            c_act(act, R, n)
                        c_act(act, R, CN - 1, C_LAST)

                    @block.vector
                    def _(dve):
                        c_dve(dve, R, 0, first=True)
                        with dve.Fori(1, CN - 1) as n:
                            c_dve(dve, R, n)
                        c_dve(dve, R, CN - 1, C_LAST)

        slot_i = sb("slot_i", [P, NT], I32)
        expert_end = sb("expert_end", [P, EXPERTS])
        tile_expert = sb("tile_expert", [P, SLOT_TILES], I32)
        with ExitStack() as ctx_s:
            def sb_s(name, shape, dt=F32):
                return ctx_s.enter_context(nc.sbuf_tensor(name, shape, dt))

            counts = sb_s("counts", [P, EXPERTS])
            counts_i = sb_s("counts_i", [P, EXPERTS], I32)
            ends = sb_s("ends", [P, 2, 2 * EXPERTS])
            begun = sb_s("begun", [P, NT, EXPERTS])
            slot_f = sb_s("slot_f", [P, NT])
            s_steps = sem("s_steps")
            packs = acc.rearrange("p t d -> p (t d)")[:, 0:EXPERTS * PACK].rearrange("p (e n) -> p e n", n=PACK)
            packs_landed = sem("packs_landed")
            AT_ONCE = 8
            counted = sem("counted")

            with nc.Block() as block:
                @block.sync
                def _(sp):
                    for e in range(0, EXPERTS, AT_ONCE):
                        sp.dma_start(packs[:, e:e + AT_ONCE, :], experts[e:e + AT_ONCE].rearrange("e p n -> p e n")).then_inc(packs_landed, 16)

                @block.tensor
                def _(pe):
                    pe.matmul(banks[:, 0, 0:EXPERTS], c_buf.ones[:, :], c_buf.counted[:, :], start=True, stop=True).then_inc(counted, 1)

                @block.vector
                def _(dve):
                    steps = 0

                    def link(ins):
                        nonlocal steps
                        steps += 1
                        ins.then_inc(s_steps, 1)
                        dve.wait_ge(s_steps, steps)

                    link(dve.memset(ends[:, :, 0:EXPERTS], 0.0))
                    dve.wait_ge(counted, 1)
                    link(dve.tensor_scalar(counts[:, :], banks[:, 0, 0:EXPERTS], float(P - 1), None, ALU.add))
                    link(dve.tensor_copy(counts_i[:, :], counts[:, :]))
                    link(dve.tensor_scalar(counts_i[:, :], counts_i[:, :], 7, None, ALU.arith_shift_right))
                    link(dve.tensor_copy(counts[:, :], counts_i[:, :]))
                    link(dve.tensor_copy(ends[:, 0, EXPERTS:], counts[:, :]))
                    a, shift = 0, 1
                    while shift < EXPERTS:
                        link(dve.tensor_tensor(ends[:, 1 - a, EXPERTS:], ends[:, a, EXPERTS:], ends[:, a, EXPERTS - shift:2 * EXPERTS - shift], ALU.add))
                        a, shift = 1 - a, 2 * shift
                    dve.tensor_copy(expert_end[:, :], ends[:, a, EXPERTS:])
                    link(dve.tensor_tensor(ends[:, 1 - a, EXPERTS:], ends[:, a, EXPERTS:], counts[:, :], ALU.subtract))
                    link(dve.tensor_tensor(begun[:, :, :], onehot[:, :, :], ends[:, 1 - a:2 - a, EXPERTS:].to_broadcast([P, NT, EXPERTS]), ALU.mult))
                    link(dve.tensor_reduce(slot_f[:, :], begun[:, :, :], AX.X, ALU.add))
                    link(dve.scalar_tensor_tensor(out=slot_f[:, :], in0=slot_f[:, :], scalar=float(P), in1=rank[:, :], op0=ALU.mult, op1=ALU.add))
                    link(dve.tensor_copy(slot_i[:, :], slot_f[:, :]))

        RING = 16
        HALF = RING // 2
        DEEP = 4
        LOAD = 4
        ITERS = SLOT_TILES // RING
        assert SLOT_TILES == ITERS * RING
        MAIN = ITERS - 1
        with ExitStack() as ctx_d:
            def sb_d(name, shape, dt=F32):
                return ctx_d.enter_context(nc.sbuf_tensor(name, shape, dt))

            slot_rows = sb_d("slot_rows", [P, RING, ROW])
            weights = sb_d("weights", [P, HALF, PACK])
            node = sb_d("node", [P, HALF], I32)
            slot_xf = sb_d("slot_xf", [P, DEEP, D])
            slot_xt = sb_d("slot_xt", [P, DEEP, D])
            hidden_t = sb_d("hidden_t", [HID + 1, DEEP, P])
            result = sb_d("result", [P, HALF, D])

            tile_iota = sb_d("tile_iota", [P, SLOT_TILES])
            ended = sb_d("ended", [P, SLOT_TILES, EXPERTS])
            expert_f = sb_d("expert_f", [P, SLOT_TILES])
            more_i = sb_d("more_i", [P, 1], I32)

            d_steps = sem("d_steps")
            experts_known = sem("experts_known")
            scattered = sem("scattered")
            rows_landed = [sem(f"rows_landed{part}") for part in range(RING // LOAD)]
            result_stored = [sem(f"result_stored{c}") for c in range(HALF)]
            ones_row_made = sem("ones_row_made")
            weights_picked = sem("weights_picked")
            slots_normed = sem("slots_normed")
            slots_turned = sem("slots_turned")
            slots_t_made = sem("slots_t_made")
            hidden_summed = sem("hidden_summed")
            hidden_t_made = sem("hidden_t_made")
            result_summed = sem("result_summed")
            result_made = sem("result_made")

            def run_sync(sp, begin, end):
                def load(i, part, first=False):
                    if not first:
                        sp.wait_ge(result_made, i * RING + (part + 1) * LOAD - RING)
                    sp.dma_start(slot_rows[:, part * LOAD:(part + 1) * LOAD, :],
                                 slot_tiles[:, bass.ds(i * RING + part * LOAD, LOAD), :]).then_inc(rows_landed[part], 16)

                for part in range(RING // LOAD):
                    load(begin, part, first=(begin == 0))
                if begin + 1 < end:
                    with sp.Fori(begin + 1, end) as i:
                        for part in range(RING // LOAD):
                            load(i, part)

            def run_pool(pool, begin, end):
                with pool.Fori(begin, end) as i:
                    for c in range(RING):
                        pool.wait_ge(result_made, i * RING + c + 1)
                        pool.sem_inc(pool_tick, 1)
                        pool.indirect_dma_start(out, bass.IndirectOffsetOnAxis(ap=node[:, c % HALF:c % HALF + 1], axis=0), result[:, c % HALF, :], None,
                                                bounds_check=NT * P - 1, oob_is_err=False).then_inc(result_stored[c % HALF], 16)
                for c in range(HALF):
                    pool.wait_ge(result_stored[c], 16 * 2 * end)

            def run_tensor(pe, begin, end):
                def turn(i, c, first=False):
                    pe.wait_ge(slots_normed, i * RING + c + 1)
                    if not (first and c < 2):
                        pe.wait_ge(slots_t_made, i * RING + c - 1)
                    for k in range(KC):
                        ins = pe.transpose(banks[:, c % 2, k * P:(k + 1) * P], slot_xf[:, c % DEEP, k * P:(k + 1) * P], ident[:, :])
                    ins.then_inc(slots_turned, 1)

                def first_layer(i, c, first=False):
                    pe.wait_ge(slots_t_made, i * RING + c + 1)
                    pe.wait_ge(weights_picked, i * RING + c + 1)
                    if not (first and c < 2):
                        pe.wait_ge(hidden_t_made, i * RING + c - 1)
                    for k in range(KC):
                        ins = pe.matmul(banks[0:HID, 2 + c % 2, 0:P], weights[:, c % HALF, k * HID:(k + 1) * HID],
                                        slot_xt[:, c % DEEP, k * P:(k + 1) * P], start=(k == 0), stop=(k == KC - 1))
                    ins.then_inc(hidden_summed, 1)

                def second_layer(i, c, first=False):
                    pe.wait_ge(hidden_t_made, i * RING + c + 1)
                    if not (first and c < 2):
                        pe.wait_ge(result_made, i * RING + c - 1)
                    pe.matmul(banks[:, 6 + c % 2, 0:D], hidden_t[:, c % DEEP, :], weights[0:HID + 1, c % HALF, KC * HID:KC * HID + D],
                              start=True, stop=True).then_inc(result_summed, 1)

                stages = ((0, turn), (2, first_layer), (4, second_layer))

                def tiles(i, begins=False, first=False):
                    for c in range(RING):
                        for lag, stage in stages:
                            if c >= lag:
                                stage(i, c - lag, first)
                            elif not begins:
                                stage(i - 1, c - lag + RING)

                tiles(begin, begins=True, first=(begin == 0))
                if begin + 1 < end:
                    with pe.Fori(begin + 1, end) as i:
                        tiles(i)
                for c in range(RING, RING + 4):
                    for lag, stage in stages:
                        if c - lag < RING:
                            stage(end - 1, c - lag)

            def run_scalar(act, begin, end):
                def pick(i, c, first=False):
                    expert = act.value_load(tile_expert[0:1, bass.ds(i * RING + c, 1)], min_val=0, max_val=EXPERTS - 1)
                    if not (first and c < HALF):
                        act.wait_ge(result_summed, i * RING + c + 1 - HALF)
                    act.copy(weights[:, c % HALF, :], packs[:, bass.ds(expert, 1), :]).then_inc(weights_picked, 1)

                def copy_turned(i, c, first=False):
                    act.wait_ge(slots_turned, i * RING + c + 1)
                    if not (first and c < DEEP):
                        act.wait_ge(hidden_summed, i * RING + c + 1 - DEEP)
                    act.copy(slot_xt[:, c % DEEP, :], banks[:, c % 2, 0:D]).then_inc(slots_t_made, 1)

                def relu_hidden(i, c, first=False):
                    act.wait_ge(hidden_summed, i * RING + c + 1)
                    if not (first and c < DEEP):
                        act.wait_ge(result_summed, i * RING + c + 1 - DEEP)
                    act.activation(hidden_t[0:HID, c % DEEP, :], banks[0:HID, 2 + c % 2, 0:P], ACT.Relu,
                                   bias=weights[0:HID, c % HALF, PACK - 1:PACK]).then_inc(hidden_t_made, 1)

                def tiles(i, begins=False, first=False):
                    for c in range(RING):
                        copy_turned(i, c, first)
                        if c >= 3:
                            relu_hidden(i, c - 3, first)
                        elif not begins:
                            relu_hidden(i - 1, c - 3 + RING)
                        pick(i, c, first)

                tiles(begin, begins=True, first=(begin == 0))
                if begin + 1 < end:
                    with act.Fori(begin + 1, end) as i:
                        tiles(i)
                for c in range(RING - 3, RING):
                    relu_hidden(end - 1, c)

            def run_vector(dve, begin, end):
                def norm_slots(i, c, first=False):
                    dve.wait_ge(rows_landed[c // LOAD], (i + 1) * 16)
                    if not (first and c < DEEP):
                        dve.wait_ge(slots_turned, i * RING + c + 1 - DEEP)
                    dve.tensor_scalar(slot_xf[:, c % DEEP, :], slot_rows[:, c, 0:D], slot_rows[:, c, MEAN:MEAN + 1],
                                      slot_rows[:, c, RSTD:RSTD + 1], ALU.subtract, ALU.mult).then_inc(slots_normed, 1)

                def add_result(i, c, first=False):
                    dve.wait_ge(result_summed, i * RING + c + 1)
                    if not (first and c < HALF):
                        dve.wait_ge(result_stored[c % HALF], (i * 2 + c // HALF) * 16)
                    dve.tensor_copy(node[:, c % HALF:c % HALF + 1], slot_rows[:, c, NODE:NODE + 1])
                    dve.scalar_tensor_tensor(out=result[:, c % HALF, :], in0=banks[:, 6 + c % 2, 0:D], scalar=0.0, in1=slot_rows[:, c, 0:D],
                                             op0=ALU.max, op1=ALU.add).then_inc(result_made, 1)

                LAG = 6

                def tiles(i, begins=False, first=False):
                    for c in range(RING):
                        norm_slots(i, c, first)
                        if c >= LAG:
                            add_result(i, c - LAG, first)
                        elif not begins:
                            add_result(i - 1, c - LAG + RING)

                tiles(begin, begins=True, first=(begin == 0))
                if begin + 1 < end:
                    with dve.Fori(begin + 1, end) as i:
                        tiles(i)
                for c in range(RING - LAG, RING):
                    add_result(end - 1, c)

            with nc.Block() as block:
                @block.sync
                def _(sp):
                    sp.wait_ge(scattered, 16 * NT)
                    run_sync(sp, 0, MAIN)

                @block.gpsimd
                def _(pool):
                    for t in range(NT):
                        pool.indirect_dma_start(sorted_in, bass.IndirectOffsetOnAxis(ap=slot_i[:, t:t + 1], axis=0), node_rows[:, t, :], None,
                                                bounds_check=SLOT_TILES * P - 1, oob_is_err=False).then_inc(scattered, 16)
                    run_pool(pool, 0, MAIN)

                @block.tensor
                def _(pe):
                    pe.wait_ge(ones_row_made, 1)
                    run_tensor(pe, 0, MAIN)

                @block.scalar
                def _(act):
                    act.wait_ge(packs_landed, 16 * (EXPERTS // AT_ONCE))
                    act.wait_ge(experts_known, 1)
                    run_scalar(act, 0, MAIN)

                @block.vector
                def _(dve):
                    wide = [P, SLOT_TILES, EXPERTS]
                    dve.tensor_copy(tile_iota[:, :], tile_iota_i[:, :]).then_inc(d_steps, 1)
                    dve.wait_ge(d_steps, 1)
                    dve.tensor_tensor(ended[:, :, :], tile_iota[:, :, None].to_broadcast(wide), expert_end[:, None, :].to_broadcast(wide),
                                      ALU.is_ge).then_inc(d_steps, 1)
                    dve.wait_ge(d_steps, 2)
                    dve.tensor_reduce(expert_f[:, :], ended[:, :, :], AX.X, ALU.add).then_inc(d_steps, 1)
                    dve.wait_ge(d_steps, 3)
                    dve.tensor_scalar(tile_expert[:, :], expert_f[:, :], float(EXPERTS - 1), None, ALU.min).then_inc(experts_known, 1)
                    dve.tensor_scalar(more_i[:, :], expert_end[:, EXPERTS - 1:EXPERTS], float(MAIN * RING), None, ALU.is_gt).then_inc(d_steps, 1)
                    dve.wait_ge(d_steps, 4)
                    dve.memset(hidden_t[HID:HID + 1, :, :], 1.0).then_inc(ones_row_made, 1)
                    run_vector(dve, 0, MAIN)

            more = nc.values_load(more_i[0:1, 0:1], min_val=0, max_val=1)
            with nc.If(more):
                with nc.Block() as block:
                    @block.sync
                    def _(sp):
                        run_sync(sp, MAIN, ITERS)

                    @block.gpsimd
                    def _(pool):
                        run_pool(pool, MAIN, ITERS)

                    @block.tensor
                    def _(pe):
                        run_tensor(pe, MAIN, ITERS)

                    @block.scalar
                    def _(act):
                        run_scalar(act, MAIN, ITERS)

                    @block.vector
                    def _(dve):
                        run_vector(dve, MAIN, ITERS)


def _layout(inputs):
    import numpy as np
    x = np.asarray(inputs["x"])
    a = {}
    a["x"] = np.concatenate([x, np.zeros((NT * P - N_NODES, D), x.dtype)])
    E = NS * SUPER_EDGES

    def edges(v, fill):
        v = np.asarray(v)
        pad = np.full((E - N_EDGES,) + v.shape[1:], fill, v.dtype)
        return np.concatenate([v, pad]).reshape((NS, GROUPS, QUADS, P) + v.shape[1:])

    src = edges(inputs["src"], 0)
    dst = edges(inputs["dst"], PAD_DST)
    attr = edges(inputs["edge_attr_64"], 0)
    a["src"] = np.ascontiguousarray(src.transpose(3, 0, 2, 1)).reshape(P, NS * TILES)
    a["dst"] = np.ascontiguousarray(dst.transpose(3, 0, 2, 1)).reshape(P, NS * TILES)
    a["attr"] = np.ascontiguousarray(attr.transpose(4, 0, 2, 1, 3)).reshape(D_EDGE, NS, TILES * P)
    a["base_group"] = np.ascontiguousarray(dst[:, :, 0, 0]).reshape(1, NS * GROUPS)
    a["base_row"] = np.ascontiguousarray(dst[:, :, 0, 0].T)
    a["w_gnn"] = inputs["L0_gnn_W"]
    a["b_gnn"] = np.asarray(inputs["L0_gnn_b"]).reshape(1, D)
    a["gamma"] = np.asarray(inputs["L0_gnn_gamma"]).reshape(1, D)
    a["beta"] = np.asarray(inputs["L0_gnn_beta"]).reshape(1, D)
    wqkv = np.asarray(inputs["L0_mix_Wqkv"])
    a["wq"] = wqkv[:INNER]
    a["wk_t"] = wqkv[INNER:2 * INNER].T
    a["wv_t"] = wqkv[2 * INNER:].T
    a["wout_t"] = np.asarray(inputs["L0_mix_Wout"]).T
    a["bout"] = np.asarray(inputs["L0_mix_bout"]).reshape(1, D)
    a["router_t"] = np.asarray(inputs["L0_ffn_router_w"]).T
    a["router_b"] = np.asarray(inputs["L0_ffn_router_b"]).reshape(1, EXPERTS)
    pack = np.zeros((EXPERTS, P, PACK), np.float32)
    pack[:, :, :KC * HID] = np.asarray(inputs["L0_ffn_W1"]).reshape(EXPERTS, KC, P, HID).transpose(0, 2, 1, 3).reshape(EXPERTS, P, KC * HID)
    pack[:, :HID, KC * HID:KC * HID + D] = np.asarray(inputs["L0_ffn_W2"])
    pack[:, HID, KC * HID:KC * HID + D] = np.asarray(inputs["L0_ffn_b2"])
    pack[:, :HID, PACK - 1] = np.asarray(inputs["L0_ffn_b1"])
    a["experts"] = pack
    return {k: np.ascontiguousarray(v) for k, v in a.items()}


def kernel(**inputs):
    import concourse.bacc as bacc
    from concourse.bass_utils import run_bass_kernel_spmd

    nc = bacc.Bacc("TRN2", target_bir_lowering=False, num_devices=1)
    arrays, args = {}, {}
    for name, a in _layout(inputs).items():
        arrays[f"in_{name}"] = a
        args[name] = nc.dram_tensor(f"in_{name}", a.shape, mybir.dt.from_np(a.dtype), kind="ExternalInput").ap()
    args["out"] = nc.dram_tensor("out_0", (NT * P, D), F32, kind="ExternalOutput").ap()
    program(nc, **args)
    r = run_bass_kernel_spmd(nc, [arrays], core_ids=[0])
    return r.results[0]["out_0"][:N_NODES]
```
